# Optimizing a Trainium2 kernel written in Bass

```python
import numpy as np
import jax
import jax.numpy as jnp

def _softmax(x, axis=-1):
    return jax.nn.softmax(x, axis=axis)

def _gelu(x):
    return jax.nn.gelu(x, approximate=True)

def _silu(x):
    return jax.nn.silu(x)

def _sigmoid(x):
    return jax.nn.sigmoid(x)

def _layernorm(x, axis=-1, eps=1e-05):
    m = jnp.mean(x, axis=axis, keepdims=True)
    v = jnp.var(x, axis=axis, keepdims=True)
    return (x - m) / jnp.sqrt(v + eps)

def _scatter_add(tgt, idx, src, axis=0):
    return tgt.at[idx].add(src)

def _segment_sum(src, seg, n):
    return jax.ops.segment_sum(src, seg, n)
kernel_name = 'mk_lm_tower_d1_tok_ids768_r4_5d402c'

def setup_inputs(seed: int=0):
    np.random.seed(seed)
    _w = jnp.asarray

    def _rec_inputs():
        import jax
        import jax.numpy as jnp
        _rk = jax.random.key(seed)
        x = jax.random.randint(jax.random.fold_in(_rk, 1), (2, 1024), 0, 6, jnp.int32)
        mask_BS_f1_0 = jnp.where(jnp.ones((2, 1024), dtype=bool), 1.0, 0.0).astype(jnp.float32)
        return (x, mask_BS_f1_0)
    x, mask_BS_f1_0 = _rec_inputs()

    def _L0_tok_setup():
        import jax, jax.numpy as jnp
        import numpy as np
        VOCAB = 6
        EPS = 1e-12

        def _conv1d_same(x, w):
            k = w.shape[-1]
            return jax.lax.conv_general_dilated(x, w, window_strides=(1,), padding=[(k // 2, k // 2)], dimension_numbers=('NCH', 'OIH', 'NCH'))
        key = jax.random.key(seed)
        k1, k2, k3, k4 = jax.random.split(key, 4)
        B, L = (32, 512)
        Cin, Cout = (VOCAB - 1, 64)
        return {'input_ids': jax.random.randint(k1, (B, L), 0, VOCAB, dtype=jnp.int64), 'attention_mask': jnp.ones((B, L), dtype=jnp.float32), 'W3': jax.random.normal(k2, (Cout, Cin, 3), dtype=jnp.float32) * 0.1, 'W5': jax.random.normal(k3, (Cout, Cin, 5), dtype=jnp.float32) * 0.1, 'W7': jax.random.normal(k4, (Cout, Cin, 7), dtype=jnp.float32) * 0.1, 'ln_gamma': jnp.ones((192,), dtype=jnp.float32), 'ln_beta': jnp.zeros((192,), dtype=jnp.float32)}
    _L0_tok_all = _L0_tok_setup()
    _L0_tok_in = {k: v for k, v in _L0_tok_all.items() if k in ('W3', 'W5', 'W7', 'ln_gamma', 'ln_beta')}
    del _L0_tok_all

    def _L0_attn_setup():
        import jax, jax.numpy as jnp
        import numpy as np
        HIDDEN = 192
        NUM_HEADS = 12
        HEAD_DIM = 64

        def _xavier(key, shape):
            fan_in, fan_out = (shape[1], shape[0])
            limit = float(np.sqrt(6.0 / (fan_in + fan_out)))
            return jax.random.uniform(key, shape, jnp.float32, -limit, limit)
        key = jax.random.key(seed)
        k1, k2, k3 = jax.random.split(key, 3)
        B, N = (4, 512)
        x = jax.random.normal(k1, (B, N, HIDDEN), dtype=jnp.float32)
        qkv_w = _xavier(k2, (3 * NUM_HEADS * HEAD_DIM, HIDDEN))
        qkv_b = jnp.zeros((3 * NUM_HEADS * HEAD_DIM,), jnp.float32)
        proj_w = _xavier(k3, (HIDDEN, NUM_HEADS * HEAD_DIM))
        proj_b = jnp.zeros((HIDDEN,), jnp.float32)
        return {'x': x, 'qkv_w': qkv_w, 'qkv_b': qkv_b, 'proj_w': proj_w, 'proj_b': proj_b}
    _L0_attn_all = _L0_attn_setup()
    _L0_attn_in = {k: v for k, v in _L0_attn_all.items() if k in ('qkv_w', 'qkv_b', 'proj_w', 'proj_b')}
    del _L0_attn_all

    def _L0_ffn_setup():
        import jax, jax.numpy as jnp
        import numpy as np
        H = 12
        ALPHA = (1, 2, 3)
        DEPTH = 5
        BLOCK_DEPTH = 3
        TOTAL_DEPTH_M1 = 14 - 1
        SMALL_ACTIVE = BLOCK_DEPTH <= DEPTH <= TOTAL_DEPTH_M1 - BLOCK_DEPTH

        def _ln(x, g, b, eps=1e-05):
            m = jnp.mean(x, axis=-1, keepdims=True)
            v = jnp.mean((x - m) ** 2, axis=-1, keepdims=True)
            return (x - m) * jax.lax.rsqrt(v + eps) * g + b

        def _attn_branch(xp, w_qkv, w_proj, b_proj, keep_heads, keep_ch):
            B2, N, C = xp.shape
            hd = C // H
            scale = hd ** (-0.5)
            qkv = (xp @ w_qkv).reshape(B2, N, 3, H, hd).transpose(2, 0, 3, 1, 4)
            hmask = (jnp.arange(H) < keep_heads).astype(xp.dtype)[None, :, None, None]
            q, k, v = (qkv[0] * hmask, qkv[1] * hmask, qkv[2] * hmask)
            a = jax.nn.softmax(jnp.einsum('bhnd,bhmd->bhnm', q, k) * scale, axis=-1)
            o = jnp.einsum('bhnm,bhmd->bhnd', a, v).transpose(0, 2, 1, 3).reshape(B2, N, C)
            o = o @ w_proj + b_proj
            cmask = (jnp.arange(C) < keep_ch).astype(xp.dtype)
            return o * cmask

        def _mlp_branch(xp, w1, b1, w2, b2, keep_ch):
            C = xp.shape[-1]
            cmask = (jnp.arange(C) < keep_ch).astype(xp.dtype)
            h = jax.nn.gelu(xp * cmask @ w1 + b1, approximate=False)
            return (h @ w2 + b2) * cmask
        key = jax.random.key(seed)
        ks = jax.random.split(key, 8)
        B, N, C = (64, 257, 192)
        HID = 4 * C

        def w(k, shape):
            return jax.random.normal(k, shape, jnp.float32) * 0.02
        return {'x': jax.random.normal(ks[0], (B, N, C), jnp.float32), 'gumbel_weights': jax.random.uniform(ks[1], (3,), jnp.float32), 'n1l_g': jnp.ones((C,), jnp.float32), 'n1l_b': jnp.zeros((C,), jnp.float32), 'n1s_g': jnp.ones((C,), jnp.float32), 'n1s_b': jnp.zeros((C,), jnp.float32), 'w_qkv': w(ks[2], (C, 3 * C)), 'w_proj': w(ks[3], (C, C)), 'b_proj': jnp.zeros((C,), jnp.float32), 'n2l_g': jnp.ones((C,), jnp.float32), 'n2l_b': jnp.zeros((C,), jnp.float32), 'n2s_g': jnp.ones((C,), jnp.float32), 'n2s_b': jnp.zeros((C,), jnp.float32), 'w_fc1': w(ks[4], (C, HID)), 'b_fc1': jnp.zeros((HID,), jnp.float32), 'w_fc2': w(ks[5], (HID, C)), 'b_fc2': jnp.zeros((C,), jnp.float32)}
    _L0_ffn_all = _L0_ffn_setup()
    _L0_ffn_in = {k: v for k, v in _L0_ffn_all.items() if k in ('gumbel_weights', 'n1l_g', 'n1l_b', 'n1s_g', 'n1s_b', 'w_qkv', 'w_proj', 'b_proj', 'n2l_g', 'n2l_b', 'n2s_g', 'n2s_b', 'w_fc1', 'b_fc1', 'w_fc2', 'b_fc2')}
    del _L0_ffn_all
    return {'x': x, 'mask_BS_f1_0': mask_BS_f1_0, 'L0_tok_W3': _L0_tok_in['W3'], 'L0_tok_W5': _L0_tok_in['W5'], 'L0_tok_W7': _L0_tok_in['W7'], 'L0_tok_ln_gamma': _L0_tok_in['ln_gamma'], 'L0_tok_ln_beta': _L0_tok_in['ln_beta'], 'L0_attn_qkv_w': _L0_attn_in['qkv_w'], 'L0_attn_qkv_b': _L0_attn_in['qkv_b'], 'L0_attn_proj_w': _L0_attn_in['proj_w'], 'L0_attn_proj_b': _L0_attn_in['proj_b'], 'L0_ffn_gumbel_weights': _L0_ffn_in['gumbel_weights'], 'L0_ffn_n1l_g': _L0_ffn_in['n1l_g'], 'L0_ffn_n1l_b': _L0_ffn_in['n1l_b'], 'L0_ffn_n1s_g': _L0_ffn_in['n1s_g'], 'L0_ffn_n1s_b': _L0_ffn_in['n1s_b'], 'L0_ffn_w_qkv': _L0_ffn_in['w_qkv'], 'L0_ffn_w_proj': _L0_ffn_in['w_proj'], 'L0_ffn_b_proj': _L0_ffn_in['b_proj'], 'L0_ffn_n2l_g': _L0_ffn_in['n2l_g'], 'L0_ffn_n2l_b': _L0_ffn_in['n2l_b'], 'L0_ffn_n2s_g': _L0_ffn_in['n2s_g'], 'L0_ffn_n2s_b': _L0_ffn_in['n2s_b'], 'L0_ffn_w_fc1': _L0_ffn_in['w_fc1'], 'L0_ffn_b_fc1': _L0_ffn_in['b_fc1'], 'L0_ffn_w_fc2': _L0_ffn_in['w_fc2'], 'L0_ffn_b_fc2': _L0_ffn_in['b_fc2']}

def reference(x, mask_BS_f1_0, L0_tok_W3, L0_tok_W5, L0_tok_W7, L0_tok_ln_gamma, L0_tok_ln_beta, L0_attn_qkv_w, L0_attn_qkv_b, L0_attn_proj_w, L0_attn_proj_b, L0_ffn_gumbel_weights, L0_ffn_n1l_g, L0_ffn_n1l_b, L0_ffn_n1s_g, L0_ffn_n1s_b, L0_ffn_w_qkv, L0_ffn_w_proj, L0_ffn_b_proj, L0_ffn_n2l_g, L0_ffn_n2l_b, L0_ffn_n2s_g, L0_ffn_n2s_b, L0_ffn_w_fc1, L0_ffn_b_fc1, L0_ffn_w_fc2, L0_ffn_b_fc2):
    import jax
    import jax.numpy as jnp

    def _L0_tok_ref(input_ids, attention_mask, W3, W5, W7, ln_gamma, ln_beta):
        import jax, jax.numpy as jnp
        import numpy as np
        VOCAB = 6
        EPS = 1e-12

        def _conv1d_same(x, w):
            k = w.shape[-1]
            return jax.lax.conv_general_dilated(x, w, window_strides=(1,), padding=[(k // 2, k // 2)], dimension_numbers=('NCH', 'OIH', 'NCH'))
        oh = jax.nn.one_hot(input_ids, VOCAB, dtype=jnp.float32)[:, :, :VOCAB - 1]
        x = jnp.transpose(oh, (0, 2, 1))
        h = jnp.concatenate([_conv1d_same(x, W3), _conv1d_same(x, W5), _conv1d_same(x, W7)], axis=1)
        h = h * attention_mask[:, None, :]
        h = jnp.transpose(h, (0, 2, 1))
        mu = jnp.mean(h, axis=-1, keepdims=True)
        var = jnp.mean(jnp.square(h - mu), axis=-1, keepdims=True)
        out = (h - mu) * jax.lax.rsqrt(var + EPS) * ln_gamma + ln_beta
        return out

    def _L0_attn_ref(x, qkv_w, qkv_b, proj_w, proj_b):
        import jax, jax.numpy as jnp
        import numpy as np
        HIDDEN = 192
        NUM_HEADS = 12
        HEAD_DIM = 64

        def _xavier(key, shape):
            fan_in, fan_out = (shape[1], shape[0])
            limit = float(np.sqrt(6.0 / (fan_in + fan_out)))
            return jax.random.uniform(key, shape, jnp.float32, -limit, limit)
        B, N, _ = x.shape
        nh, H = (NUM_HEADS, HEAD_DIM)
        qkv = jnp.einsum('bnd,od->bno', x, qkv_w) + qkv_b
        q, k, v = jnp.split(qkv, 3, axis=-1)

        def heads(t):
            return t.reshape(B, N, nh, H).transpose(0, 2, 1, 3)
        q, k, v = (heads(q), heads(k), heads(v))
        scores = jnp.einsum('bhnd,bhmd->bhnm', q, k) / jnp.sqrt(jnp.float32(H))
        attn = jax.nn.softmax(scores, axis=-1)
        out = jnp.einsum('bhnm,bhmd->bhnd', attn, v)
        out = out.transpose(0, 2, 1, 3).reshape(B, N, nh * H)
        out = jnp.einsum('bnk,ok->bno', out, proj_w) + proj_b
        return out

    def _L0_ffn_ref(x, gumbel_weights, n1l_g, n1l_b, n1s_g, n1s_b, w_qkv, w_proj, b_proj, n2l_g, n2l_b, n2s_g, n2s_b, w_fc1, b_fc1, w_fc2, b_fc2):
        import jax, jax.numpy as jnp
        import numpy as np
        H = 12
        ALPHA = (1, 2, 3)
        DEPTH = 5
        BLOCK_DEPTH = 3
        TOTAL_DEPTH_M1 = 14 - 1
        SMALL_ACTIVE = BLOCK_DEPTH <= DEPTH <= TOTAL_DEPTH_M1 - BLOCK_DEPTH

        def _ln(x, g, b, eps=1e-05):
            m = jnp.mean(x, axis=-1, keepdims=True)
            v = jnp.mean((x - m) ** 2, axis=-1, keepdims=True)
            return (x - m) * jax.lax.rsqrt(v + eps) * g + b

        def _attn_branch(xp, w_qkv, w_proj, b_proj, keep_heads, keep_ch):
            B2, N, C = xp.shape
            hd = C // H
            scale = hd ** (-0.5)
            qkv = (xp @ w_qkv).reshape(B2, N, 3, H, hd).transpose(2, 0, 3, 1, 4)
            hmask = (jnp.arange(H) < keep_heads).astype(xp.dtype)[None, :, None, None]
            q, k, v = (qkv[0] * hmask, qkv[1] * hmask, qkv[2] * hmask)
            a = jax.nn.softmax(jnp.einsum('bhnd,bhmd->bhnm', q, k) * scale, axis=-1)
            o = jnp.einsum('bhnm,bhmd->bhnd', a, v).transpose(0, 2, 1, 3).reshape(B2, N, C)
            o = o @ w_proj + b_proj
            cmask = (jnp.arange(C) < keep_ch).astype(xp.dtype)
            return o * cmask

        def _mlp_branch(xp, w1, b1, w2, b2, keep_ch):
            C = xp.shape[-1]
            cmask = (jnp.arange(C) < keep_ch).astype(xp.dtype)
            h = jax.nn.gelu(xp * cmask @ w1 + b1, approximate=False)
            return (h @ w2 + b2) * cmask
        B, N, C = x.shape
        B2 = B // 2
        nl = _ln(x[:B2], n1l_g, n1l_b)
        ns = _ln(x[B2:], n1s_g, n1s_b)
        a_large = _attn_branch(nl, w_qkv, w_proj, b_proj, H, C)
        if SMALL_ACTIVE:
            a_small = sum((gumbel_weights[i] * _attn_branch(ns, w_qkv, w_proj, b_proj, H // ALPHA[i], C // ALPHA[i]) for i in range(3)))
            attn_out = jnp.concatenate([a_large, a_small], axis=0)
        else:
            attn_out = jnp.concatenate([a_large, a_large], axis=0)
        x = x + attn_out
        nl2 = _ln(x[:B2], n2l_g, n2l_b)
        ns2 = _ln(x[B2:], n2s_g, n2s_b)
        m_large = _mlp_branch(nl2, w_fc1, b_fc1, w_fc2, b_fc2, C)
        if SMALL_ACTIVE:
            m_small = sum((gumbel_weights[i] * _mlp_branch(ns2, w_fc1, b_fc1, w_fc2, b_fc2, C // ALPHA[i]) for i in range(3)))
            mlp_out = jnp.concatenate([m_large, m_small], axis=0)
        else:
            mlp_out = jnp.concatenate([m_large, m_large], axis=0)
        return x + mlp_out
    h = _L0_tok_ref(x, mask_BS_f1_0, L0_tok_W3, L0_tok_W5, L0_tok_W7, L0_tok_ln_gamma, L0_tok_ln_beta)
    h = h + _L0_attn_ref(_layernorm(h, axis=-1), L0_attn_qkv_w, L0_attn_qkv_b, L0_attn_proj_w, L0_attn_proj_b)
    h = h + _L0_ffn_ref(_layernorm(h, axis=-1), L0_ffn_gumbel_weights, L0_ffn_n1l_g, L0_ffn_n1l_b, L0_ffn_n1s_g, L0_ffn_n1s_b, L0_ffn_w_qkv, L0_ffn_w_proj, L0_ffn_b_proj, L0_ffn_n2l_g, L0_ffn_n2l_b, L0_ffn_n2s_g, L0_ffn_n2s_b, L0_ffn_w_fc1, L0_ffn_b_fc1, L0_ffn_w_fc2, L0_ffn_b_fc2)
    return h

_drawn_inputs = setup_inputs


def setup_inputs(seed=0):
    import zlib

    import numpy as np

    out = dict(_drawn_inputs(seed))
    spreads = {'L0_tok_ln_gamma': (1.0, 0.2),
     'L0_tok_ln_beta': (0.0, 0.1),
     'L0_attn_qkv_b': (0.0, 0.1),
     'L0_attn_proj_b': (0.0, 0.1),
     'L0_ffn_n1l_g': (1.0, 0.6),
     'L0_ffn_n1l_b': (0.0, 0.8),
     'L0_ffn_n1s_g': (1.0, 0.6),
     'L0_ffn_n1s_b': (0.0, 0.8),
     'L0_ffn_b_proj': (0.0, 0.1),
     'L0_ffn_n2l_g': (1.0, 0.6),
     'L0_ffn_n2l_b': (0.0, 2.0),
     'L0_ffn_n2s_g': (1.0, 0.6),
     'L0_ffn_n2s_b': (0.0, 2.0),
     'L0_ffn_b_fc1': (0.0, 0.777),
     'L0_ffn_b_fc2': (0.0, 0.1)}
    factors = {'L0_ffn_gumbel_weights': 6.596, 'L0_ffn_w_qkv': 4.183, 'L0_ffn_w_proj': 4.401}
    for name, (base, spread) in spreads.items():
        noise = np.random.default_rng([zlib.crc32(name.encode()), seed]).standard_normal(out[name].shape)
        drawn = base * np.exp(spread * noise) if base else spread * noise
        out[name] = jnp.asarray(drawn.astype(out[name].dtype))
    for name, factor in factors.items():
        out[name] = (out[name] * factor).astype(out[name].dtype)
    return out
```

```python
from contextlib import ExitStack

import concourse.bass as bass
from concourse import mybir

F32 = mybir.dt.float32
F32R = mybir.dt.float32r
BF16 = mybir.dt.bfloat16
I32 = mybir.dt.int32
ALU = mybir.AluOpType
ACT = mybir.ActivationFunctionType
AX = mybir.AxisListType

P = 128
B = 2
S = 1024
N = B * S
C = 192
CH = C - P
TB = N // P
KB = S // P
HALF = S // 2
H = 12
D1 = 64
D2 = 16
PAIRS = H // 2
MROW = 96
KC = MROW + 2
CONV_ROWS = 99
KEEP = [C, C // 2, C // 3]
HKEEP = [H, H // 2, H // 3]
F = 4 * C
FB = F // P
NROT = 3
NP = 4


def tower(nc, a, out):
    with ExitStack() as ctx:
        def sb(name, shape, dt=F32):
            return ctx.enter_context(nc.sbuf_tensor(name, shape, dt))

        def sem(name):
            return ctx.enter_context(nc.semaphore(name))

        PS = ctx.enter_context(nc.psum_tensor("PS", [P, 8, HALF], F32))
        scoreB = [PS[:, 2 * i:2 * i + 2, :] for i in range(2)]
        rotT = [PS[:, 4 + i, :] for i in range(NROT)]
        psO = PS[:, 7, :]

        HT = sb("HT", [P, TB, C])
        XAh = sb("XAh", [P, N], F32R)
        XAl = sb("XAl", [P, N], F32R)
        XC = sb("XC", [P, N], F32R)
        BIG = sb("BIG", [P, 12288])
        QK = sb("QK", [P, 8 * S], F32R)
        PA = sb("PA", [P, 6 * S])
        TQ = sb("TQ", [P, S])
        HH = sb("HH", [P, S], F32R)
        LL = sb("LL", [P, S], F32R)
        V1 = sb("V1", [P, B, KB, P])
        WRAW = sb("WRAW", [P, 2, 3, P])
        WH = sb("WH", [P, 2, 3, P], F32R)
        WL = sb("WL", [P, 2, 3, P], F32R)
        WP1 = sb("WP1", [P, 2, PAIRS, C])
        WP2 = sb("WP2", [MROW, B, 2, C])
        MZ = sb("MZ", [P, 2, KB, P], BF16)
        MC = sb("MC", [P, 2, KB])
        DEN = sb("DEN", [P, HALF])
        REC = sb("REC", [P, HALF])
        ORAW = sb("ORAW", [P, HALF])
        identF = sb("identF", [P, P])
        identB = sb("identB", [P, P], BF16)
        ones = sb("ones", [P, D1])
        STAT = sb("STAT", [P, TB, 6])
        MV = sb("MV", [P, TB, 2])
        SD = sb("SD", [P, TB])
        RS = sb("RS", [P, TB])
        gcols = sb("gcols", [P, 3, B, 2, 2])
        qkb = sb("qkb", [P, 2])
        qkbs = sb("qkbs", [P, 2])
        qks = sb("qks", [P, 1])
        bvc = sb("bvc", [P, PAIRS])
        maskc = sb("maskc", [P, TB])
        vocab = sb("vocab", [P, 1])
        gw = sb("gw", [P, 3])
        b1c = sb("b1c", [P, FB])
        rows = sb("rows", [P, 5, C])
        bias1 = sb("bias1", [P, C])
        bias2 = sb("bias2", [P, B, C])
        biasM = sb("biasM", [P, B, C])

        def q_of(u):
            return QK[:, (u % 2) * S:(u % 2 + 1) * S]

        def k_of(u):
            return QK[:, (2 + u % 2) * S:(3 + u % 2) * S]

        def q2_of(u):
            return QK[:, (4 + u % 2) * S:(5 + u % 2) * S]

        def k2_of(u):
            return QK[:, (6 + u % 2) * S:(7 + u % 2) * S]

        def q3_of(u):
            return QK[:, (u % 3) * S:(u % 3 + 1) * S]

        def k3_of(u):
            return QK[:, (3 + u % 3) * S:(4 + u % 3) * S]

        def prob(i):
            return PA[:, (i % NP) * S:(i % NP + 1) * S]

        def psum_of(u):
            return PA[:, (NP + u % 2) * S:(NP + 1 + u % 2) * S]

        OT = BIG[:, :].rearrange("p (b h x n) -> p b h x n", b=B, h=PAIRS, x=2)
        Y = BIG[:, 0:TB * C].rearrange("p (t c) -> p t c", t=TB)
        NT = BIG[:, TB * C:TB * C + TB * 2 * P].rearrange("p (t c) -> p t c", t=TB)
        V2W = D2 + 1
        V2 = BIG[:, 6144:6144 + B * KB * H * V2W].rearrange("p (b t h d) -> p b t h d", b=B, t=KB, h=H)
        O2S = [BIG[:, 9600 + 256 * i:9856 + 256 * i] for i in range(2)]
        HB = BIG[:, 3072:3072 + 3 * FB * HALF].rearrange("p (e m n) -> p e m n", e=3, m=FB)
        V2S = V1[:, 0, :, :].rearrange("p a b -> p (a b)")[:, 0:3 * KB * V2W].rearrange("p (u t d) -> p u t d", u=3, t=KB)
        O2 = PA[0:MROW, 0:4 * S].rearrange("p (b g n) -> p b g n", b=B, g=2)
        R2 = BIG[0:MROW, 6144:6144 + 4 * S].rearrange("p (b g n) -> p b g n", b=B, g=2)
        D2T = BIG[0:MROW, 10496:10752]
        R2T = BIG[0:MROW, 10752:11008]

        QD = nc.dram_tensor("QD", [B, H, 4 * D2, S], F32, kind="Internal").ap()
        KD = nc.dram_tensor("KD", [B, H, 4 * D2, S], F32, kind="Internal").ap()
        OD = nc.dram_tensor("OD", [B, H, V2W, S], F32, kind="Internal").ap()
        RD = nc.dram_tensor("RD", [4, B, H, S // 4], F32, kind="Internal").ap()

        phase_done = sem("phase_done")
        loads = sem("loads")
        dve_step = sem("dve_step")
        act_step = sem("act_step")
        pool_step = sem("pool_step")
        consts = sem("consts")
        conv_in = sem("conv_in")
        conv_out = sem("conv_out")
        h0_ready = sem("h0_ready")
        var_ready = sem("var_ready")
        std_ready = sem("std_ready")
        tr_done = sem("tr_done")
        xt_high = sem("xt_high")
        xt_t = sem("xt_t")
        xt_low = sem("xt_low")
        raw1 = sem("raw1")
        wh_done = sem("wh_done")
        wl_done = sem("wl_done")
        w_used = sem("w_used")
        b_ready = sem("b_ready")
        rowmax = sem("rowmax")
        mz_hi = sem("mz_hi")
        mz_ready = sem("mz_ready")
        rot_ready = sem("rot_ready")
        rot_done = sem("rot_done")
        pv_done = sem("pv_done")
        psum_step = sem("psum_step")
        o_copied = sem("o_copied")
        rec_done = sem("rec_done")
        ot_done = sem("ot_done")
        hh_done = sem("hh_done")
        ll_done = sem("ll_done")
        moved = [sem(f"moved{i}") for i in range(2)]
        proj_ready = sem("proj_ready")
        proj_used = sem("proj_used")
        w_loaded = sem("w_loaded")
        q2_ready = sem("q2_ready")
        q2_high = sem("q2_high")
        q2_low = sem("q2_low")
        q2_stored = sem("q2_stored")
        loaded3 = [sem(f"loaded{i}") for i in range(3)]
        v2s_ready = sem("v2s_ready")
        sums_in = sem("sums_in")
        sums_out = sem("sums_out")
        o2_copied = sem("o2_copied")
        o2_stored = [sem(f"o2_stored{i}") for i in range(2)]
        tail_dma = sem("tail_dma")
        fc1_ready = sem("fc1_ready")
        fc1_used = sem("fc1_used")
        fc2_ready = sem("fc2_ready")
        fc2_used = sem("fc2_used")
        stored = sem("stored")

        nphase = {}

        def barrier(eng, name):
            nphase[name] = nphase.get(name, 0) + 1
            eng.drain().then_inc(phase_done, 1)
            eng.wait_ge(phase_done, 5 * nphase[name])

        block = ctx.enter_context(nc.Block())

        BSLOT = [0, 1, 2, 2, 2, 1, 0, 0]
        PRO = 9

        def unit_tiles(j, last):
            t = []
            for i in range(KB):
                if i == 7 and not (last and j == 3):
                    t += [(i, "M", x, j) for x in range(2)]
                t += [(i, "C", x, j) for x in range(2)]
                if i == 1 and j > 0:
                    t += [(i, "D", 0, j - 1)]
                if j % 2 == 0 and i in (2, 3, 6) and not (last and j == 2):
                    t += [(i, "V", {2: 0, 3: 1, 6: 2}[i], j)]
                if i in (4, 5) and not (last and j >= 2):
                    t += [(i, "A", i - 4, j)]
            if j == 3:
                t += [(KB, "D", 0, j)]
            return t

        def key_of(tile):
            slot, kind, x, owner = tile
            return owner, kind, x, slot if kind == "C" else 0

        tile_no = [{key_of(t): PRO + n for n, t in enumerate(t for j in range(4) for t in unit_tiles(j, last))}
                   for last in (False, True)]
        BODY = len(tile_no[0])
        R1 = PRO + (PAIRS - 1) * BODY + len(tile_no[1])
        PV1 = NP + KB * 2 * H
        assert BODY % NROT == 0 and PRO % NROT == 0
        VBLK = [range(0, 3), range(3, 6), range(6, 8)]

        PRO2, ROT2 = 2, 2 * KB + 2
        AHEAD = 10

        @block.sync
        def _(sp):
            for dst, src in [(PA[0:CONV_ROWS, 0:N].bitcast(I32), a["windows"]), (PA[0:CONV_ROWS, N:N + C], a["convw"]),
                             (vocab[:, :], a["vocab"]), (maskc[:, :], a["mask"]), (identF[:, :], a["ident"]),
                             (gcols[:, :, :, :, :].rearrange("p a b c d -> p (a b c d)"), a["gcols"]),
                             (qks[:, :], a["qks"]), (bvc[:, :], a["bvc"]), (b1c[:, :], a["b1c"]),
                             (WP1[:, :, :, :].rearrange("p a b c -> p (a b c)"), a["wp1"]),
                             (WP2[:, 0, :, :].rearrange("p b c -> p (b c)"), a["wp2"]),
                             (gw[:, :], a["gw"].partition_broadcast(P)),
                             (rows[:, :, :], a["rows"].partition_broadcast(P))]:
                sp.dma_start(dst, src).then_inc(loads, 16)
            barrier(sp, "sp")
            barrier(sp, "sp")
            sp.dma_start(WRAW[:, :, :, :].rearrange("p a b c -> p (a b c)"), a["w1"][0]).then_inc(raw1, 16)
            sp.dma_start(qkb[:, :], a["qkb"][0]).then_inc(raw1, 16)

            def move(k, nth):
                sp.wait_ge(ll_done, nth)
                for dst, src in [(q_of(k)[0:D1], HH[0:D1]), (q_of(k)[D1:P], LL[0:D1]), (k_of(k)[0:D1], HH[D1:P]),
                                 (k_of(k)[D1:P], HH[D1:P]), (q2_of(k)[0:D1], HH[0:D1]), (k2_of(k)[0:D1], LL[D1:P])]:
                    sp.dma_start(dst.bitcast(F32), src.bitcast(F32)).then_inc(moved[k % 2], 16)

            move(0, 1)
            move(1, 2)

            def body1(p, last):
                if not last:
                    nth = sp.snap(p + 1)
                    sp.wait_ge(wl_done, nth)
                    sp.dma_start(WRAW[:, :, :, :].rearrange("p a b c -> p (a b c)"), a["w1"][nth]).then_inc(raw1, 16)
                    sp.dma_start(qkb[:, :], a["qkb"][nth]).then_inc(raw1, 16)
                for j in range(4):
                    if last and j >= 2:
                        break
                    keys_used, nth = p * BODY + tile_no[last][(j, "C", 1, 7)] + 1, 4 * p + j + 3
                    if not last:
                        keys_used, nth = sp.to_reg(keys_used), sp.to_reg(nth)
                    sp.wait_ge(rot_ready, keys_used)
                    move(j, nth)
            with sp.Fori(0, PAIRS - 1) as p:
                body1(p, False)
            body1(PAIRS - 1, True)
            barrier(sp, "sp")
            barrier(sp, "sp")
            barrier(sp, "sp")
            sp.dma_start(PA[:, 0:2 * 3 * C], a["w2qkv"]).then_inc(w_loaded, 16)
            for m in range(4):
                for b in range(B):
                    n = B * m + b
                    sp.wait_ge(q2_high, 2 * n + 2)
                    sp.wait_ge(q2_low, 2 * n + 2)
                    g = m % 2
                    for part, src in ((0, HH), (1, LL)):
                        for s in ((0, 2), (1, 3))[part] if m < 2 else ((0, 1), (2, 3))[part]:
                            dst = (QD if m < 2 else KD)[b, 6 * g:6 * g + 6, D2 * s:D2 * s + D2, :]
                            for h in range(6):
                                sp.dma_start(dst[h], src[D2 * h:D2 * h + D2, :].bitcast(F32)).then_inc(q2_stored, 16)
                    sp.wait_ge(q2_stored, 16 * 24 * (n + 1))
            barrier(sp, "sp")

            def load3(b, h, k):
                sp.dma_start(q3_of(k)[0:4 * D2].bitcast(F32), QD[b, h]).then_inc(loaded3[k % 3], 16)
                sp.dma_start(k3_of(k)[0:4 * D2].bitcast(F32), KD[b, h]).then_inc(loaded3[k % 3], 16)

            for u in range(3):
                load3(u % 2, u // 2, u)

            def store2(nth, j, b, h):
                sp.wait_ge(o2_copied, nth)
                for g in range(4):
                    sp.dma_start(OD[b, h, :, 256 * g:256 * g + 256], O2S[j % 2][32 * g:32 * g + V2W, :])\
                        .then_inc(o2_stored[j % 2], 16)

            def body2(it, last):
                def reg(value):
                    return value if last else sp.snap(value)

                for j in range(7):
                    if j > 0:
                        store2(reg(6 * it + j), j - 1, (j - 1) % 2, reg(3 * it + (j - 1) // 2))
                    if j < 6 and not (last and j >= 3):
                        keys_used = reg(R1 + it * 6 * ROT2 + PRO2 + ROT2 * (j + 1))
                        h = reg(3 * it + (j + 3) // 2)
                        sp.wait_ge(rot_ready, keys_used)
                        load3((j + 3) % 2, h, j)
            with sp.Fori(0, H // 3 - 1) as it:
                body2(it, False)
            body2(H // 3 - 1, True)
            for i in range(2):
                sp.wait_ge(o2_stored[i], 64 * H)
            for b in range(B):
                for g in range(2):
                    for h in range(6):
                        sp.dma_start(O2[D2 * h:D2 * h + D2, b, g, :], OD[b, 6 * g + h, 0:D2, :]).then_inc(tail_dma, 16)
            for q in range(4):
                sp.dma_start(D2T[2 * H * q:2 * H * q + 2 * H, :],
                             OD[:, :, D2, 256 * q:256 * q + 256].rearrange("b h n -> (b h) n")).then_inc(sums_in, 16)
            sp.wait_ge(rec_done, 8 + 4 * 2 * H + 1)
            sp.dma_start(RD.rearrange("q b h n -> (q b h) n"), R2T).then_inc(sums_out, 16)
            sp.wait_ge(sums_out, 16)
            for b in range(B):
                for g in range(2):
                    for h in range(6):
                        sp.dma_start(R2[D2 * h:D2 * h + D2, b, g, :].rearrange("p (q n) -> p q n", q=4),
                                     RD[:, b, 6 * g + h, :].partition_broadcast(D2))\
                            .then_inc(tail_dma, 16)
            sp.wait_ge(tail_dma, 16 * 48)
            barrier(sp, "sp")
            barrier(sp, "sp")
            barrier(sp, "sp")
            sp.dma_start(PA[:, 0:FB * C], a["wfc2"]).then_inc(w_loaded, 16)
            sp.dma_start(PA[:, 4 * FB * C:4 * FB * C + 2 * F], a["wfc1"]).then_inc(w_loaded, 16)
            for t in range(TB):
                sp.wait_ge(fc2_used, t + 1)
                sp.dma_start(out[P * t:P * t + P, :], HT[:, t, :]).then_inc(stored, 16)
            sp.wait_ge(stored, 16 * TB)
            barrier(sp, "sp")

        @block.gpsimd
        def _(pool):
            nc.gpsimd.memset(ones[:, :], 1.0).then_inc(consts, 1)
            nc.gpsimd.memset(MZ[:, :, :, :], 0.0).then_inc(consts, 1)
            pool.wait_ge(loads, 16 * 13)
            nc.gpsimd.tensor_scalar(WP2[:, 1, :, :], WP2[:, 0, :, :], gw[0:MROW, 0:1], None, ALU.mult).then_inc(pool_step, 1)
            nc.gpsimd.tensor_scalar(bias2[:, 1, :], rows[:, 3, :], gw[:, 0:1], None, ALU.mult).then_inc(pool_step, 1)
            nc.gpsimd.tensor_scalar(biasM[:, 1, :], rows[:, 4, :], gw[:, 0:1], None, ALU.mult).then_inc(pool_step, 1)
            nc.gpsimd.tensor_copy(bias2[:, 0, :], rows[:, 3, :]).then_inc(pool_step, 1)
            nc.gpsimd.tensor_copy(biasM[:, 0, :], rows[:, 4, :]).then_inc(pool_step, 1)
            barrier(pool, "pool")
            barrier(pool, "pool")
            pool.sem_inc(psum_step, NP)

            def low(u):
                pool.wait_ge(hh_done, u + 1)
                nc.gpsimd.tensor_tensor(LL[:, :], TQ[:, :], HH[:, :].bitcast(F32), ALU.subtract).then_inc(ll_done, 1)

            low(0)
            pool.wait_ge(moved[0], 96)
            low(1)

            def body1(p, last):
                for j in range(4):
                    u = 4 * p + j
                    for i in range(1, KB):
                        pool.wait_ge(rot_done, p * BODY + tile_no[last][(j, "C", 1, i)] + 1)
                        if i == 1:
                            pool.wait_ge(rec_done, 4 * u + 4)
                            nc.gpsimd.tensor_tensor(psum_of(j), prob(0), prob(1), ALU.add).then_inc(psum_step, 1)
                        else:
                            pool.wait_ge(psum_step, NP + 7 * u + i - 1)
                            nc.gpsimd.tensor_tensor(psum_of(j), prob(i), psum_of(j), ALU.add).then_inc(psum_step, 1)
                        if i == 6 and not (last and j >= 2):
                            pool.wait_ge(moved[(j + 1) % 2], 96 * (2 * p + (j + 1) // 2 + 1))
                            low(u + 2)
            with pool.Fori(0, PAIRS - 1) as p:
                body1(p, False)
            body1(PAIRS - 1, True)
            barrier(pool, "pool")
            barrier(pool, "pool")
            barrier(pool, "pool")
            nc.gpsimd.memset(V2[:, :, :, :, D2:V2W], 1.0).then_inc(consts, 1)
            barrier(pool, "pool")

            def stage_v(b, h, k):
                nc.gpsimd.tensor_copy(V2S[:, k % 3, :, :], V2[:, b, :, h, :]).then_inc(v2s_ready, 1)

            for u in range(3):
                stage_v(u % 2, u // 2, u)

            def body2(it, last):
                for j in range(6):
                    if not (last and j >= 3):
                        pool.wait_ge(pv_done, PV1 + KB * (6 * it + j + 1))
                        stage_v((j + 3) % 2, 3 * it + (j + 3) // 2, j)
            with pool.Fori(0, H // 3 - 1) as it:
                body2(it, False)
            body2(H // 3 - 1, True)
            barrier(pool, "pool")
            barrier(pool, "pool")
            barrier(pool, "pool")
            pool.wait_ge(w_loaded, 48)
            w = PA[:, 0:FB * C]
            for i in range(3):
                nc.gpsimd.tensor_scalar(PA[:, (i + 1) * FB * C:(i + 2) * FB * C], w, gw[:, i:i + 1], None, ALU.mult)\
                    .then_inc(pool_step, 1)
            barrier(pool, "pool")

        @block.scalar
        def _(act):
            act.wait_ge(loads, 16 * 13)
            for t in range(TB):
                act.wait_ge(conv_out, t // 2 * 2 + 2)
                nc.scalar.activation(HT[:, t, :], PS[:, t // 2, 256 * (t % 2):256 * (t % 2) + C], ACT.Identity,
                                     scale=maskc[:, t:t + 1]).then_inc(h0_ready, 1)
            nstd = [0]

            def std():
                nstd[0] += 1
                act.wait_ge(var_ready, nstd[0])
                nc.scalar.activation(SD[:, :], SD[:, :], ACT.Sqrt).then_inc(std_ready, 1)
            std()
            std()
            barrier(act, "act")

            nx = [0]

            def transposed(stage):
                for g in range(4):
                    nx[0] += 1
                    act.wait_ge(tr_done, nx[0])
                    cols = slice(HALF * g, HALF * g + HALF)
                    for c, dst in ((0, XAh), (1, XC)):
                        nc.scalar.activation(dst[:, cols], PS[:, 2 * (g % 2) + c, :], ACT.Identity,
                                             scale=gcols[:, stage, g // 2, c, 0:1], bias=gcols[:, stage, g // 2, c, 1:2])\
                            .then_inc(xt_high, 1)
            transposed(0)
            barrier(act, "act")

            def take(n):
                act.wait_ge(rot_ready, n + 1)

            def t_half(k, hh, hcol, n):
                take(n)
                nc.scalar.activation(TQ[:, HALF * hh:HALF * hh + HALF], rotT[k % NROT], ACT.Identity,
                                     scale=qks[:, 0:1], bias=qkbs[:, hcol:hcol + 1]).then_inc(rot_done, 1)

            def v_tile(k, b, part, n):
                take(n)
                blk = VBLK[part]
                nc.scalar.activation(V1[:, b, blk[0]:blk[-1] + 1, :].rearrange("p t d -> p (t d)"),
                                     rotT[k % NROT][:, 0:P * len(blk)], ACT.Copy).then_inc(rot_done, 1)

            def m_tile(k, dst, hh, n):
                take(n)
                nc.scalar.activation(dst[MROW:MROW + 2, HALF * hh:HALF * hh + HALF], rotT[k % NROT][MROW:MROW + 2, :],
                                     ACT.Copy).then_inc(rot_done, 1)

            for k in range(2):
                if k == 1:
                    act.wait_ge(ll_done, 1)
                for hh in range(2):
                    t_half(2 * k + hh, hh, k, 2 * k + hh)
            for part in range(3):
                v_tile(4 + part, 0, part, 4 + part)
            for hh in range(2):
                m_tile(7 + hh, q2_of(0), hh, 7 + hh)

            def body1(p, last):
                for j in range(4):
                    u = 4 * p + j
                    for tile in unit_tiles(j, last):
                        i, kind, x, owner = tile
                        k = tile_no[last][key_of(tile)]
                        n = p * BODY + k
                        if kind == "C":
                            take(n)
                            if x == 0:
                                act.wait_ge(pv_done, KB * u + i + 1)
                                act.wait_ge(psum_step, 7 * u + i + 1 if i < 4 else 7 * u + max(i - 4, 1) + 4)
                            nc.scalar.activation(prob(i)[:, HALF * x:HALF * x + HALF], rotT[k % NROT], ACT.Exp)\
                                .then_inc(rot_done, 1)
                            if i == 0 and x == 1 and j > 0:
                                copy_o(u - 1)
                        elif kind == "D":
                            take(n)
                            act.wait_ge(rec_done, 4 * (4 * p + owner) + 8)
                            nc.scalar.activation(DEN[:, :], rotT[k % NROT], ACT.Copy).then_inc(rot_done, 1)
                        elif kind == "A":
                            if x == 0:
                                act.wait_ge(ll_done, u + 2)
                            t_half(k, x, j % 2, n)
                        elif kind == "V":
                            v_tile(k, 1 if j == 0 else 0, x, n)
                        elif kind == "M":
                            m_tile(k, q2_of(j + 1), x, n)

            def copy_o(u):
                act.wait_ge(pv_done, NP + KB * (u + 1))
                act.wait_ge(ot_done, 2 * u)
                nc.scalar.activation(ORAW[:, :], psO, ACT.Copy).then_inc(o_copied, 1)
            with act.Fori(0, PAIRS - 1) as p:
                body1(p, False)
                copy_o(4 * p + 3)
            body1(PAIRS - 1, True)
            copy_o(4 * PAIRS - 1)
            barrier(act, "act")
            std()
            std()
            barrier(act, "act")
            transposed(1)
            barrier(act, "act")

            for m in range(4):
                for b in range(B):
                    for hh in range(2):
                        n = 2 * (B * m + b) + hh
                        act.wait_ge(q2_ready, n + 1)
                        if hh == 0 and n:
                            act.wait_ge(q2_stored, 16 * 24 * (B * m + b))
                        nc.scalar.activation(HH[0:MROW, HALF * hh:HALF * hh + HALF], PS[0:MROW, n % 4, :], ACT.Identity,
                                             scale=0.25 if m < 2 else 1.0).then_inc(q2_high, 1)
            for t in range(TB):
                act.wait_ge(q2_ready, 16 + t + 1)
                nc.scalar.activation(V2[:, t // KB, t % KB, :, 0:D2],
                                     PS[:, 4 + t % 4, 0:C].rearrange("p (h d) -> p h d", h=H), ACT.Copy)\
                    .then_inc(q2_high, 1)
            barrier(act, "act")

            base = R1
            for hh in range(2):
                act.wait_ge(rot_ready, base + hh + 1)
                nc.scalar.activation(q3_of(0)[MROW:MROW + 2, HALF * hh:HALF * hh + HALF], rotT[hh][MROW:MROW + 2, :],
                                     ACT.Copy).then_inc(rot_done, 1)

            def body2(it, last):
                for j in range(6):
                    u = 6 * it + j
                    k = ROT2 * j + PRO2
                    for i in range(KB):
                        if i == 7:
                            if not (last and j == 5):
                                for hh in range(2):
                                    act.wait_ge(rot_ready, base + it * 6 * ROT2 + k + 1)
                                    nc.scalar.activation(q3_of(j + 1)[MROW:MROW + 2, HALF * hh:HALF * hh + HALF],
                                                         rotT[k % NROT][MROW:MROW + 2, :], ACT.Copy).then_inc(rot_done, 1)
                                    k += 1
                        for hh in range(2):
                            act.wait_ge(rot_ready, base + it * 6 * ROT2 + k + 1)
                            if hh == 0:
                                act.wait_ge(pv_done, PV1 - NP + KB * u + i + 1)
                            nc.scalar.activation(prob(i)[:, HALF * hh:HALF * hh + HALF], rotT[k % NROT], ACT.Exp)\
                                .then_inc(rot_done, 1)
                            k += 1
            with act.Fori(0, H // 3 - 1) as it:
                body2(it, False)
            body2(H // 3 - 1, True)
            barrier(act, "act")
            std()
            barrier(act, "act")
            transposed(2)
            barrier(act, "act")
            nh = 0
            for g in range(4):
                for e in range(1 if g < 2 else 3):
                    for m in range(FB):
                        act.wait_ge(fc1_ready, nh + 1)
                        if m == 0 and g > 0:
                            act.wait_ge(fc2_ready, 4 * g)
                        nc.scalar.activation(HB[:, e, m, :], PS[:, nh % 4, :], ACT.Gelu, bias=b1c[:, m:m + 1])\
                            .then_inc(fc1_used, 1)
                        nh += 1
            barrier(act, "act")

        @block.vector
        def _(dve):
            cnt = [0]

            def link(ins):
                cnt[0] += 1
                ins.then_inc(dve_step, 1)
                dve.wait_ge(dve_step, cnt[0])

            def note(ins):
                cnt[0] += 1
                ins.then_inc(dve_step, 1)

            nln = [0]

            def stats(src, eps):
                for t in range(TB):
                    note(nc.vector.bn_stats(STAT[:, t, :], src[:, t, :]))
                dve.wait_ge(dve_step, cnt[0])
                for t in range(TB):
                    note(nc.vector.bn_aggr(MV[:, t, :], STAT[:, t, :]))
                dve.wait_ge(dve_step, cnt[0])
                nln[0] += 1
                nc.vector.tensor_scalar(SD[:, :], MV[:, :, 1], eps, None, ALU.add).then_inc(var_ready, 1)
                dve.wait_ge(std_ready, nln[0])
                link(nc.vector.reciprocal(RS[:, :], SD[:, :]))

            def twice():
                link(nc.vector.tensor_copy(NT[:, :, C:2 * P], NT[:, :, P:C]))

            def normalise(dst, src):
                for t in range(TB):
                    note(nc.vector.tensor_scalar(dst[:, t, 0:C], src[:, t, :], MV[:, t, 0:1], RS[:, t:t + 1],
                                                 ALU.subtract, ALU.mult))
                dve.wait_ge(dve_step, cnt[0])

            dve.wait_ge(loads, 16 * 13)
            E = QK[0:CONV_ROWS, 0:N]
            WS = WH[:, :, :, :].rearrange("p a b c -> p (a b c)")[0:CONV_ROWS, 0:C]
            link(nc.vector.tensor_copy(WS, PA[0:CONV_ROWS, N:N + C]))
            link(nc.vector.tensor_tensor(WS[64:CONV_ROWS], PA[64:CONV_ROWS, N:N + C], WS[64:CONV_ROWS].bitcast(F32),
                                         ALU.subtract))
            nc.vector.tensor_scalar(E, PA[0:CONV_ROWS, 0:N].bitcast(I32), vocab[0:CONV_ROWS, 0:1], None, ALU.is_equal)\
                .then_inc(conv_in, 1)
            link(nc.vector.tensor_copy(identB[:, :], identF[:, :]))
            dve.wait_ge(pool_step, 5)
            for i, heads, ch in ((1, HKEEP[1] * D2, KEEP[1]), (2, HKEEP[2] * D2, KEEP[2])):
                w = WP2[0:heads, 1, 0, 0:ch]
                note(nc.vector.scalar_tensor_tensor(out=w, in0=WP2[0:heads, 0, 0, 0:ch], scalar=gw[0:heads, i:i + 1], in1=w,
                                                    op0=ALU.mult, op1=ALU.add))
                for bias, r in ((bias2, 3), (biasM, 4)):
                    note(nc.vector.scalar_tensor_tensor(out=bias[:, 1, 0:ch], in0=rows[:, r, 0:ch], scalar=gw[:, i:i + 1],
                                                        in1=bias[:, 1, 0:ch], op0=ALU.mult, op1=ALU.add))
                dve.wait_ge(dve_step, cnt[0])
            dve.wait_ge(h0_ready, TB)
            stats(HT, 1e-12)
            normalise(HT, HT)
            g3 = rows[:, 0, :].unsqueeze(1).broadcast_to([P, TB, C])
            b3 = rows[:, 1, :].unsqueeze(1).broadcast_to([P, TB, C])
            link(nc.vector.tensor_tensor(HT[:, :, :], HT[:, :, :], g3, ALU.mult))
            link(nc.vector.tensor_tensor(HT[:, :, :], HT[:, :, :], b3, ALU.add))
            stats(HT, 1e-5)
            normalise(NT, HT)
            twice()
            barrier(dve, "dve")

            nx = [0]

            def transposed(stage):
                for g in range(4):
                    nx[0] += 1
                    n = nx[0]
                    cols = slice(HALF * g, HALF * g + HALF)
                    t = [PA[:, (2 * (g % 2) + c) * HALF:(2 * (g % 2) + c + 1) * HALF] for c in range(2)]
                    if g >= 2:
                        dve.wait_ge(xt_low, 2 * (n - 2))
                    for c in range(2):
                        dve.wait_ge(xt_high, 2 * (n - 1) + c + 1)
                        nc.vector.tensor_scalar(t[c], PS[:, 2 * (g % 2) + c, :], gcols[:, stage, g // 2, c, 0:1],
                                                gcols[:, stage, g // 2, c, 1:2], ALU.mult, ALU.add).then_inc(xt_t, 1)
                    dve.wait_ge(xt_t, 2 * n)
                    nc.vector.tensor_tensor(XAl[:, cols], t[0], XAh[:, cols].bitcast(F32), ALU.subtract).then_inc(xt_low, 1)
                    nc.vector.tensor_tensor(XC[64:P, cols], t[1][64:P], XC[64:P, cols].bitcast(F32), ALU.subtract)\
                        .then_inc(xt_low, 1)
                dve.wait_ge(xt_low, 2 * nx[0])
            transposed(0)
            for i in range(2):
                note(nc.vector.memset(q2_of(i)[D1:P].bitcast(F32), 0.0))
                note(nc.vector.memset(k2_of(i)[D1:P].bitcast(F32), 0.0))
            dve.wait_ge(dve_step, cnt[0])
            for i in range(2):
                nc.vector.memset(k2_of(i)[MROW:MROW + 2].bitcast(F32), 1.0).then_inc(consts, 1)
            barrier(dve, "dve")

            def split_w(p):
                dve.wait_ge(raw1, 32 * p + 32)
                nc.vector.tensor_scalar(qkbs[:, :], qkb[:, :], qks[:, 0:1], None, ALU.mult).then_inc(wh_done, 1)
                nc.vector.tensor_copy(WH[:, :, :, :], WRAW[:, :, :, :]).then_inc(wh_done, 1)
                dve.wait_ge(wh_done, 2 * p + 2)
                nc.vector.tensor_tensor(WL[:, :, :, :], WRAW[:, :, :, :], WH[:, :, :, :].bitcast(F32), ALU.subtract)\
                    .then_inc(wl_done, 1)

            def high(u, n):
                dve.wait_ge(rot_done, n + 1)
                nc.vector.tensor_copy(HH[:, :], TQ[:, :]).then_inc(hh_done, 1)

            def row_max(k, i, n, wait_mz=None):
                dve.wait_ge(b_ready, n + 1)
                if i == 0 and wait_mz is not None:
                    dve.wait_ge(mz_ready, wait_mz)
                nc.vector.tensor_reduce(MC[:, k % 2, i:i + 1], scoreB[i % 2], AX.XY, ALU.max, negate=True)\
                    .then_inc(rowmax, 1)

            def split_max(k, u, n):
                dve.wait_ge(rowmax, n)
                nc.vector.tensor_copy(MZ[:, k % 2, :, MROW], MC[:, k % 2, :]).then_inc(mz_hi, 1)
                dve.wait_ge(mz_hi, u + 1)
                nc.vector.tensor_tensor(MZ[:, k % 2, :, MROW + 1], MC[:, k % 2, :], MZ[:, k % 2, :, MROW], ALU.subtract)\
                    .then_inc(mz_ready, 1)

            dve.sem_inc(rec_done, 8)
            split_w(0)
            high(0, 1)
            dve.wait_ge(moved[0], 96)
            high(1, 3)
            for i in range(KB):
                row_max(0, i, i)
            split_max(0, 0, KB)

            def recip(u, q, n):
                if q == 0:
                    dve.wait_ge(rot_done, n + 1)
                    dve.wait_ge(ot_done, 2 * u)
                nc.vector.reciprocal(REC[:, P * q:P * q + P], DEN[:, P * q:P * q + P]).then_inc(rec_done, 1)

            def outputs(u, jj, pp):
                dve.wait_ge(o_copied, u + 1)
                dve.wait_ge(rec_done, 8 + 4 * (u + 1))
                for lo in range(2):
                    half = lo if jj % 2 == 0 else 1 - lo
                    s = slice(D1 * lo, D1 * lo + D1)
                    dst = OT[s, jj // 2, pp, half, :] if isinstance(pp, int) else \
                        OT[s, jj // 2, bass.ds(pp, 1), half, :].rearrange("p a n -> p (a n)")
                    nc.vector.tensor_tensor(dst, ORAW[s, :], REC[s, :], ALU.mult).then_inc(ot_done, 1)

            def body1(p, last):
                for j in range(4):
                    u = 4 * p + j
                    d = p * BODY + tile_no[last][(j - 1, "D", 0, 0)] if j > 0 else None
                    bmax = not (last and j == 3)

                    def mx(i):
                        if bmax:
                            row_max(j + 1, i, KB * (u + 1) + i, u)
                    mx(0)
                    mx(1)
                    mx(2)
                    if j > 0:
                        recip(u - 1, 0, d)
                    mx(3)
                    mx(4)
                    if j > 0:
                        recip(u - 1, 1, d)
                    mx(5)
                    mx(6)
                    if j > 0:
                        recip(u - 1, 2, d)
                    mx(7)
                    if bmax:
                        split_max(j + 1, u + 1, KB * (u + 2))
                    if j == 1 and not last:
                        dve.wait_ge(rot_done, p * BODY + tile_no[last][(1, "A", 1, 0)] + 1)
                        split_w(p + 1)
                    if not (last and j >= 2):
                        dve.wait_ge(moved[(j + 1) % 2], 96 * (2 * p + (j + 1) // 2 + 1))
                        high(u + 2, p * BODY + tile_no[last][(j, "A", 1, 0)])
                    if j > 0:
                        recip(u - 1, 3, d)
                        outputs(u - 1, j - 1, p)
                d = p * BODY + tile_no[last][(3, "D", 0, 0)]
                for q in range(4):
                    recip(4 * p + 3, q, d)
                outputs(4 * p + 3, 3, p)
            with dve.Fori(0, PAIRS - 1) as p:
                body1(p, False)
            body1(PAIRS - 1, True)
            barrier(dve, "dve")
            dve.wait_ge(proj_ready, 1)
            link(nc.vector.tensor_tensor(bias1[:, :], PS[:, 7, 0:C], rows[:, 2, :], ALU.add))
            for t in range(TB):
                link(nc.vector.tensor_tensor(HT[:, t, :], HT[:, t, :], bias1[:, :], ALU.add))
                dve.wait_ge(proj_ready, t + 2)
                nc.vector.tensor_tensor(HT[:, t, :], PS[:, t % 7, 0:C], HT[:, t, :], ALU.add).then_inc(proj_used, 1)
            dve.wait_ge(proj_used, TB)
            stats(HT, 1e-5)
            normalise(Y, HT)
            stats(Y, 1e-5)
            normalise(NT, Y)
            twice()
            barrier(dve, "dve")
            transposed(1)
            barrier(dve, "dve")
            dve.wait_ge(w_loaded, 16)
            raw = PA[:, 0:6 * C]
            W2h, W2l = QK[:, 0:6 * C], QK[:, 2048:2048 + 6 * C]
            link(nc.vector.tensor_copy(W2h, raw))
            nc.vector.tensor_tensor(W2l, raw, W2h.bitcast(F32), ALU.subtract).then_inc(wl_done, 1)
            for n in range(16):
                dve.wait_ge(q2_high, n + 1)
                hh = n % 2
                if hh == 0 and n:
                    dve.wait_ge(q2_stored, 16 * 24 * (n // 2))
                s = slice(HALF * hh, HALF * hh + HALF)
                nc.vector.scalar_tensor_tensor(out=LL[0:MROW, s], in0=PS[0:MROW, n % 4, :], scalar=0.25 if n < 8 else 1.0,
                                               in1=HH[0:MROW, s].bitcast(F32), op0=ALU.mult, op1=ALU.subtract)\
                    .then_inc(q2_low, 1)
            barrier(dve, "dve")
            for i in range(3):
                note(nc.vector.memset(q3_of(i)[D1:P].bitcast(F32), 0.0))
                note(nc.vector.memset(k3_of(i)[D1:P].bitcast(F32), 0.0))
            dve.wait_ge(dve_step, cnt[0])
            for i in range(3):
                nc.vector.memset(k3_of(i)[MROW:MROW + 2].bitcast(F32), 1.0).then_inc(consts, 1)
            UB = 2 * H
            for n in range(AHEAD):
                row_max(n // KB, n % KB, KB * UB + n, UB + n // KB - 1)
                if n == KB - 1:
                    split_max(0, UB, KB * (UB + 1))

            def body2(it, last):
                for j in range(6):
                    u = 6 * it + j
                    for i in range(KB):
                        w = KB * j + i + AHEAD
                        if not (last and w >= 6 * KB):
                            row_max(w // KB, w % KB, it * 6 * KB + KB * UB + w, 6 * it + UB + w // KB - 1)
                            if w % KB == KB - 1:
                                split_max(w // KB, 6 * it + UB + w // KB, it * 6 * KB + KB * UB + w + 1)
                        if i == 0 and j > 0:
                            copy_o2(6 * it, j - 1)

                copy_o2(6 * it, 5)

            def copy_o2(u0, j):
                dve.wait_ge(pv_done, PV1 + KB * (u0 + j + 1))
                dve.wait_ge(o2_stored[j % 2], u0 * 32 + 64 * (j // 2))
                nc.vector.tensor_copy(O2S[j % 2], psO[:, 0:256]).then_inc(o2_copied, 1)
            with dve.Fori(0, H // 3 - 1) as it:
                body2(it, False)
            body2(H // 3 - 1, True)
            dve.wait_ge(sums_in, 64)
            nc.vector.reciprocal(R2T, D2T).then_inc(rec_done, 1)
            barrier(dve, "dve")
            for b in range(B):
                for g in range(2):
                    nc.vector.tensor_tensor(O2[:, b, g, :], O2[:, b, g, :], R2[:, b, g, :], ALU.mult).then_inc(ot_done, 1)
            for t in range(TB):
                b = t // KB
                link(nc.vector.tensor_tensor(Y[:, t, :], Y[:, t, :], bias2[:, b, :], ALU.add))
                dve.wait_ge(proj_ready, TB + 1 + t + 1)
                nc.vector.tensor_tensor(Y[:, t, :], PS[:, t % 8, 0:C], Y[:, t, :], ALU.add).then_inc(proj_used, 1)
            dve.wait_ge(proj_used, 2 * TB)
            stats(Y, 1e-5)
            normalise(NT, Y)
            twice()
            link(nc.vector.tensor_tensor(HT[:, :, :], HT[:, :, :], Y[:, :, :], ALU.add))
            for b in range(B):
                note(nc.vector.tensor_tensor(HT[:, KB * b:KB * b + KB, :], HT[:, KB * b:KB * b + KB, :],
                                             biasM[:, b, :].unsqueeze(1).broadcast_to([P, KB, C]), ALU.add))
            dve.wait_ge(dve_step, cnt[0])
            barrier(dve, "dve")
            transposed(2)
            barrier(dve, "dve")
            dve.wait_ge(w_loaded, 48)
            raw = PA[:, 4 * FB * C:4 * FB * C + 2 * F]
            Mh, Ml = QK[:, 0:2 * F], QK[:, 2 * F:4 * F]
            Zh, Zl = QK[0:MROW, 4 * F:5 * F], QK[0:MROW, 5 * F:6 * F]
            link(nc.vector.tensor_copy(Mh, raw))
            link(nc.vector.tensor_tensor(Ml, raw, Mh.bitcast(F32), ALU.subtract))
            note(nc.vector.memset(Zh[64:MROW].bitcast(F32), 0.0))
            note(nc.vector.memset(Zl[64:MROW].bitcast(F32), 0.0))
            note(nc.vector.tensor_copy(Zh[0:64], Mh[0:64, 0:F].bitcast(F32)))
            link(nc.vector.tensor_copy(Zl[0:64], Ml[0:64, 0:F].bitcast(F32)))
            nc.vector.memset(STAT[:, 0, 0:1], 0.0).then_inc(wl_done, 1)
            for t in range(TB):
                dve.wait_ge(fc2_ready, t + 1)
                nc.vector.tensor_tensor(HT[:, t, :], PS[:, 4 + t % 4, 0:C], HT[:, t, :], ALU.add).then_inc(fc2_used, 1)
            barrier(dve, "dve")

        @block.tensor
        def _(pe):
            pe.wait_ge(conv_in, 1)
            pe.wait_ge(dve_step, 2)
            WS = WH[:, :, :, :].rearrange("p a b c -> p (a b c)")[0:CONV_ROWS, 0:C]
            for t in range(TB):
                pe.matmul(PS[:, t // 2, 256 * (t % 2):256 * (t % 2) + C], QK[0:CONV_ROWS, P * t:P * t + P], WS,
                          start=True, stop=True).then_inc(conv_out, 1)
            barrier(pe, "pe")

            nx = [0]

            def transposed():
                n0 = nx[0]
                for g in range(4):
                    if g >= 2:
                        pe.wait_ge(xt_t, 2 * (n0 + g - 1))
                    for tb in range(4):
                        pe.transpose(PS[:, 2 * (g % 2), P * tb:P * tb + P], NT[:, 4 * g + tb, 0:P], identF[:, :])
                        c2 = NT[:, 4 * g + tb, P:2 * P]
                        mm = pe.transpose(PS[:, 2 * (g % 2) + 1, P * tb:P * tb + P], c2, identF[:, :])
                    mm.then_inc(tr_done, 1)
                nx[0] += 4
            transposed()
            barrier(pe, "pe")

            def free(n):
                pe.wait_ge(rot_done, n - NROT + 1)

            CHUNKS = [(XAh, WH, 0), (XAl, WH, 0), (XAh, WL, 0), (XC, WH, 1), (XC, WL, 1)]

            def a_tile(k, b, hd, hh):
                for c, (x, w, r) in enumerate(CHUNKS):
                    mm = pe.matmul(rotT[k % NROT], w[:, r, hd, :], x[:, S * b + HALF * hh:S * b + HALF * hh + HALF],
                                   start=(c == 0), stop=(c == len(CHUNKS) - 1))
                mm.then_inc(rot_ready, 1)

            def v_tile(k, b, part):
                for x_, t in enumerate(VBLK[part]):
                    for c, (x, w, r) in enumerate(CHUNKS):
                        mm = pe.matmul(rotT[k % NROT][:, P * x_:P * x_ + P], x[:, S * b + P * t:S * b + P * t + P],
                                       w[:, r, 2, :], start=(c == 0), stop=(c == len(CHUNKS) - 1))
                mm.then_inc(rot_ready, 1)

            def m_tile(k, j, hh):
                for i in range(4):
                    mm = pe.matmul(rotT[k % NROT][:, P * i:P * i + P], MZ[:, j % 2, 4 * hh + i, :], identB[:, :],
                                   start=True, stop=True)
                mm.then_inc(rot_ready, 1)

            def b_tile(q, k_, i, n):
                pe.wait_ge(rowmax, n - 1)
                for hh in range(2):
                    mm = pe.matmul(scoreB[i % 2][:, hh, :], q[:, P * i:P * i + P], k_[:, HALF * hh:HALF * hh + HALF],
                                   start=True, stop=True)
                mm.then_inc(b_ready, 1)

            pe.wait_ge(wl_done, 1)
            for n in range(4):
                if n == 3:
                    free(n)
                a_tile(n, 0, n // 2, n % 2)
            for part in range(3):
                free(4 + part)
                v_tile(4 + part, 0, part)
            pe.wait_ge(moved[0], 96)
            for i in range(KB):
                if i < 2:
                    for hh in range(2):
                        mm = pe.matmul(scoreB[i % 2][:, hh, :], q_of(0)[:, P * i:P * i + P],
                                       k_of(0)[:, HALF * hh:HALF * hh + HALF], start=True, stop=True)
                    mm.then_inc(b_ready, 1)
                else:
                    b_tile(q_of(0), k_of(0), i, i)
            pe.wait_ge(mz_ready, 1)
            for hh in range(2):
                free(7 + hh)
                m_tile(7 + hh, 0, hh)
            pe.wait_ge(rot_done, PRO)
            pe.sem_inc(pv_done, NP)

            def pv(j, i, u):
                b, odd = j // 2, j % 2
                if i == 0:
                    pe.wait_ge(o_copied, u)
                for lo in range(2):
                    half = lo if odd == 0 else 1 - lo
                    mm = pe.matmul(psO[D1 * lo:D1 * lo + D1, :], V1[:, b, i, D1 * odd:D1 * odd + D1],
                                   prob(i)[:, HALF * half:HALF * half + HALF], start=(i == 0), stop=(i == KB - 1))
                mm.then_inc(pv_done, 1)

            def den(k, j, u):
                pe.wait_ge(psum_step, NP + 7 * (u + 1))
                for lo in range(2):
                    half = lo if j % 2 == 0 else 1 - lo
                    mm = pe.matmul(rotT[k % NROT][D1 * lo:D1 * lo + D1, :], ones[:, :],
                                   psum_of(j)[:, HALF * half:HALF * half + HALF], start=True, stop=True)
                mm.then_inc(rot_ready, 1)

            def body1(p, last):
                for j in range(4):
                    u = 4 * p + j
                    q, k_, q2, k2 = q_of(j), k_of(j), q2_of(j), k2_of(j)
                    nb = 0
                    for i in range(KB + 1):
                        if i < KB and not (last and j == 3):
                            for _x in range(BSLOT[i]):
                                if nb == 0:
                                    jn = (j + 1) % 4
                                    pe.wait_ge(moved[jn % 2], 96 * (2 * p + (2 if j == 3 else 0) + jn // 2 + 1))
                                b_tile(q_of(j + 1), k_of(j + 1), nb, KB * (u + 1) + nb)
                                nb += 1
                        if i == KB and j == 3:
                            pv_wait(j, KB - 1, p, last)
                            pv(j, KB - 1, u)
                        for tile in (t for t in unit_tiles(j, last) if t[0] == i):
                            _, kind, x, owner = tile
                            k = tile_no[last][key_of(tile)]
                            free(p * BODY + k)
                            if kind == "C":
                                cols = slice(HALF * x, HALF * x + HALF)
                                pe.matmul(rotT[k % NROT], k_[:, P * i:P * i + P], q[:, cols], start=True, stop=False)
                                pe.matmul(rotT[k % NROT], k2[0:KC, P * i:P * i + P], q2[0:KC, cols], start=False, stop=True)\
                                    .then_inc(rot_ready, 1)
                            elif kind == "M":
                                if x == 0:
                                    pe.wait_ge(mz_ready, u + 2)
                                m_tile(k, j + 1, x)
                            elif kind == "D":
                                den(k, owner, 4 * p + owner)
                            elif kind == "V":
                                if x == 0 and j == 2:
                                    pe.wait_ge(wl_done, p + 2)
                                v_tile(k, 1 if j == 0 else 0, x)
                            elif kind == "A":
                                a_tile(k, 1 if j < 2 else 0, j % 2, x)
                        if 0 < i < KB:
                            pv_wait(j, i - 1, p, last)
                            pv(j, i - 1, u)
                        elif i == 0 and j > 0:
                            pv_wait(j - 1, KB - 1, p, last)
                            pv(j - 1, KB - 1, u - 1)

            def pv_wait(j, i, p, last):
                pe.wait_ge(rot_done, p * BODY + tile_no[last][(j, "C", 1, i)] + 1)
            with pe.Fori(0, PAIRS - 1) as p:
                body1(p, False)
            body1(PAIRS - 1, True)
            barrier(pe, "pe")

            for p in range(PAIRS):
                mm = pe.matmul(PS[:, 7, 0:C], bvc[:, p:p + 1].broadcast_to([P, P]), WP1[:, 0, p, :],
                               start=(p == 0), stop=(p == PAIRS - 1))
            mm.then_inc(proj_ready, 1)
            for t in range(TB):
                b, half, blk = t // KB, t % KB // 4, t % 4
                if t >= 7:
                    pe.wait_ge(proj_used, t - 6)
                for p in range(PAIRS):
                    mm = pe.matmul(PS[:, t % 7, 0:C], OT[:, b, p, half, P * blk:P * blk + P], WP1[:, half, p, :],
                                   start=(p == 0), stop=(p == PAIRS - 1))
                mm.then_inc(proj_ready, 1)
            barrier(pe, "pe")
            transposed()
            barrier(pe, "pe")
            W2h, W2l = QK[:, 0:6 * C], QK[:, 2048:2048 + 6 * C]
            CH2 = [(XAh, W2h, 0), (XAl, W2h, 0), (XAh, W2l, 0), (XC, W2h, 3 * C), (XC, W2l, 3 * C)]
            pe.wait_ge(wl_done, PAIRS + 1)
            for m in range(4):
                for g in range(4):
                    n = 4 * m + g
                    if n >= 4:
                        pe.wait_ge(q2_low, n - 3)
                    for c, (x, w, o) in enumerate(CH2):
                        mm = pe.matmul(PS[0:MROW, n % 4, :], w[:, o + MROW * m:o + MROW * m + MROW],
                                       x[:, HALF * g:HALF * g + HALF], start=(c == 0), stop=(c == 4))
                    mm.then_inc(q2_ready, 1)
            for t in range(TB):
                if t >= 4:
                    pe.wait_ge(q2_high, 16 + t - 3)
                for c, (x, w, o) in enumerate(CH2):
                    mm = pe.matmul(PS[:, 4 + t % 4, 0:C], x[:, P * t:P * t + P], w[:, o + 2 * C:o + 3 * C],
                                   start=(c == 0), stop=(c == 4))
                mm.then_inc(q2_ready, 1)
            barrier(pe, "pe")

            UB = 2 * H
            pe.wait_ge(consts, 7 + 1)
            for n in range(AHEAD):
                if n % KB == 0:
                    pe.wait_ge(loaded3[n // KB], 32)
                b_tile(q3_of(n // KB), k3_of(n // KB), n % KB, KB * UB + n)
            pe.wait_ge(mz_ready, UB + 1)
            for hh in range(2):
                m_tile(hh, 0, hh)
            pe.wait_ge(rot_done, R1 + PRO2)

            def pv2(j, i, u):
                if i == 0:
                    pe.wait_ge(o2_copied, u)
                    pe.wait_ge(v2s_ready, u + 1)
                for g in range(4):
                    mm = pe.matmul(psO[32 * g:32 * g + V2W, 0:256], V2S[:, j % 3, i, :], prob(i)[:, 256 * g:256 * g + 256],
                                   start=(i == 0), stop=(i == KB - 1))
                mm.then_inc(pv_done, 1)

            def body2(it, last):
                base = R1 + it * 6 * ROT2
                for j in range(6):
                    u = 6 * it + j
                    k = ROT2 * j + PRO2
                    for i in range(KB):
                        w = KB * j + i + AHEAD
                        if not (last and w >= 6 * KB):
                            un = w // KB
                            if w % KB == 0:
                                pe.wait_ge(loaded3[un % 3], it * 64 + 32 * (un // 3 + 1))
                            b_tile(q3_of(un), k3_of(un), w % KB, it * 6 * KB + KB * UB + w)
                        if i == 7 and not (last and j == 5):
                            pe.wait_ge(mz_ready, UB + u + 2)
                            for hh in range(2):
                                pe.wait_ge(rot_done, base + k - NROT + 1)
                                m_tile(k, j + 1, hh)
                                k += 1
                        for hh in range(2):
                            pe.wait_ge(rot_done, base + k - NROT + 1)
                            mm = pe.matmul(rotT[k % NROT], k3_of(j)[0:KC, P * i:P * i + P],
                                           q3_of(j)[0:KC, HALF * hh:HALF * hh + HALF], start=True, stop=True)
                            mm.then_inc(rot_ready, 1)
                            if hh == 1:
                                kk[i % 2] = k
                            k += 1
                        if i > 0:
                            pe.wait_ge(rot_done, base + kk[(i - 1) % 2] + 1)
                            pv2(j, i - 1, u)
                        elif j > 0:
                            pe.wait_ge(rot_done, base + kk[1] + 1)
                            pv2(j - 1, KB - 1, u - 1)
                pe.wait_ge(rot_done, base + kk[1] + 1)
                pv2(5, KB - 1, 6 * it + 5)
            kk = [0, 0]
            with pe.Fori(0, H // 3 - 1) as it:
                body2(it, False)
            body2(H // 3 - 1, True)
            barrier(pe, "pe")
            pe.wait_ge(ot_done, 2 * 2 * H + 4)
            for t in range(TB):
                b, blk = t // KB, t % KB
                if t >= 8:
                    pe.wait_ge(proj_used, TB + t - 7)
                for g in range(2):
                    mm = pe.matmul(PS[:, t % 8, 0:C], O2[:, b, g, P * blk:P * blk + P], WP2[:, b, g, :],
                                   start=(g == 0), stop=(g == 1))
                mm.then_inc(proj_ready, 1)
            barrier(pe, "pe")
            transposed()
            barrier(pe, "pe")
            Mh, Ml = QK[:, 0:2 * F], QK[:, 2 * F:4 * F]
            Zh, Zl = QK[0:MROW, 4 * F:5 * F], QK[0:MROW, 5 * F:6 * F]
            FULL = [(XAh, Mh, 0), (XAl, Mh, 0), (XAh, Ml, 0), (XC, Mh, F), (XC, Ml, F)]
            HALFW = [(XAh[0:MROW], Mh[0:MROW], 0), (XAl[0:MROW], Mh[0:MROW], 0), (XAh[0:MROW], Ml[0:MROW], 0)]
            THIRD = [(XAh[0:MROW], Zh, 0), (XAl[0:MROW], Zh, 0), (XAh[0:MROW], Zl, 0)]
            pe.wait_ge(wl_done, PAIRS + 2)
            pe.wait_ge(pool_step, 5 + 3)
            nh = 0
            for g in range(4):
                evals = [0] if g < 2 else [0, 1, 2]
                for e in evals:
                    chunks = (FULL, HALFW, THIRD)[e]
                    for m in range(FB):
                        if nh >= 4:
                            pe.wait_ge(fc1_used, nh - 3)
                        for c, (x, w, o) in enumerate(chunks):
                            mm = pe.matmul(PS[:, nh % 4, :], w[:, o + P * m:o + P * m + P], x[:, HALF * g:HALF * g + HALF],
                                           start=(c == 0), stop=(c == len(chunks) - 1))
                        mm.then_inc(fc1_ready, 1)
                        nh += 1
                pe.wait_ge(fc1_used, nh)
                for tb in range(4):
                    t = 4 * g + tb
                    if t >= 4:
                        pe.wait_ge(fc2_used, t - 3)
                    for e in evals:
                        ch = KEEP[e]
                        w0 = 0 if g < 2 else (e + 1) * FB * C
                        for m in range(FB):
                            mm = pe.matmul(PS[:, 4 + tb, 0:ch], HB[:, e, m, P * tb:P * tb + P],
                                           PA[:, w0 + C * m:w0 + C * m + ch], start=(e == 0 and m == 0),
                                           stop=(e == evals[-1] and m == FB - 1), skip_group_check=True)
                    mm.then_inc(fc2_ready, 1)
            barrier(pe, "pe")




def kernel(**inputs):
    import numpy as np
    import concourse.bacc as bacc
    from concourse.bass_utils import run_bass_kernel_spmd

    x = {k: np.ascontiguousarray(v) for k, v in inputs.items()}
    f32 = np.float32
    arrays = {}
    ids = np.full((B, S + 6), -1, np.int32)
    ids[:, 3:3 + S] = x["x"]
    win = np.full((CONV_ROWS, B, S), -1, np.int32)
    convw = np.zeros((CONV_ROWS, C), f32)
    vocab = np.full((P, 1), -2, f32)
    for at in (0, 64):
        for tap in range(7):
            for v in range(5):
                r = at + 5 * tap + v
                win[r] = ids[:, tap:tap + S]
                vocab[r] = v
                for c, (name, k) in enumerate((("L0_tok_W3", 3), ("L0_tok_W5", 5), ("L0_tok_W7", 7))):
                    t = tap - 3 + k // 2
                    if 0 <= t < k:
                        convw[r, 64 * c:64 * c + 64] = x[name][:, v, t]
    arrays["windows"] = win.reshape(CONV_ROWS, N)
    arrays["convw"] = convw
    arrays["vocab"] = vocab
    arrays["mask"] = x["mask_BS_f1_0"].reshape(TB, P).T
    arrays["ident"] = np.eye(P, dtype=f32)

    def by_chunk(v):
        return np.stack([v[0:P], np.concatenate([v[P:C], v[P:C]])], 1)

    g = np.zeros((P, 3, B, 2, 2), f32)
    g[:, 0, :, :, 0] = 1.0
    for s_, n_ in ((1, "n1"), (2, "n2")):
        for b, z in enumerate("ls"):
            for k, gb in enumerate("gb"):
                g[:, s_, b, :, k] = by_chunk(x[f"L0_ffn_{n_}{z}_{gb}"])
    arrays["gcols"] = g.reshape(P, -1)
    w, wb = x["L0_attn_qkv_w"], x["L0_attn_qkv_b"]
    HD = H * D1
    w1 = np.zeros((PAIRS, P, 2, 3, P), f32)
    qkb = np.zeros((PAIRS, P, 2), f32)
    for h in range(H):
        r = slice(D1 * h, D1 * h + D1)
        both = np.concatenate([w[0:HD][r], w[HD:2 * HD][r]]).T
        w1[h // 2, :, :, h % 2, :] = np.stack([both[0:P], np.concatenate([both[P:C], both[P:C]])], 1)
        qkb[h // 2, :, h % 2] = np.concatenate([wb[0:HD][r], wb[HD:2 * HD][r]])
    for p in range(PAIRS):
        v = w[2 * HD + P * p:2 * HD + P * p + P].T
        w1[p, :, :, 2, :] = np.stack([v[0:P], np.concatenate([v[P:C], v[P:C]])], 1)
    arrays["w1"] = w1.reshape(PAIRS, P, -1)
    arrays["qkb"] = qkb
    arrays["qks"] = np.repeat(np.array([D1 ** -0.5, 1.0], f32), D1).reshape(P, 1)
    arrays["bvc"] = wb[2 * HD:].reshape(PAIRS, P).T
    wp = x["L0_attn_proj_w"].T.reshape(PAIRS, 2, D1, C)
    arrays["wp1"] = np.stack([wp.reshape(PAIRS, P, C), wp[:, ::-1].reshape(PAIRS, P, C)]).transpose(2, 0, 1, 3).reshape(P, -1)
    arrays["wp2"] = x["L0_ffn_w_proj"].reshape(2, MROW, C).transpose(1, 0, 2).reshape(MROW, -1)
    arrays["gw"] = x["L0_ffn_gumbel_weights"]
    arrays["rows"] = np.stack([x[n] for n in ("L0_tok_ln_gamma", "L0_tok_ln_beta", "L0_attn_proj_b", "L0_ffn_b_proj", "L0_ffn_b_fc2")])
    arrays["w2qkv"] = by_chunk(x["L0_ffn_w_qkv"]).reshape(P, -1)
    arrays["wfc1"] = by_chunk(x["L0_ffn_w_fc1"]).reshape(P, -1)
    arrays["b1c"] = x["L0_ffn_b_fc1"].reshape(FB, P).T
    arrays["wfc2"] = x["L0_ffn_w_fc2"].reshape(FB, P, C).transpose(1, 0, 2).reshape(P, -1)

    nc = bacc.Bacc("TRN2", target_bir_lowering=False, num_devices=1)
    arrays = {f"in_{k}": np.ascontiguousarray(v) for k, v in arrays.items()}
    aps = {k[3:]: nc.dram_tensor(k, v.shape, mybir.dt.from_np(v.dtype), kind="ExternalInput").ap() for k, v in arrays.items()}
    out = nc.dram_tensor("out", (N, C), F32, kind="ExternalOutput").ap()
    tower(nc, aps, out)
    r = run_bass_kernel_spmd(nc, [arrays], core_ids=[0])
    return r.results[0]["out"].reshape(B, S, C)
```

```python
from contextlib import ExitStack

import concourse.bass as bass
from concourse import mybir

F32 = mybir.dt.float32
F32R = mybir.dt.float32r
BF16 = mybir.dt.bfloat16
I32 = mybir.dt.int32
ALU = mybir.AluOpType
ACT = mybir.ActivationFunctionType
AX = mybir.AxisListType

P = 128
B = 2
S = 1024
N = B * S
C = 192
CH = C - P
TB = N // P
KB = S // P
HALF = S // 2
H = 12
D1 = 64
D2 = 16
PAIRS = H // 2
MROW = 96
KC = MROW + 2
CONV_ROWS = 99
KEEP = [C, C // 2, C // 3]
HKEEP = [H, H // 2, H // 3]
F = 4 * C
FB = F // P
NROT = 3
NP = 4


def tower(nc, a, out):
    with ExitStack() as ctx:
        def sb(name, shape, dt=F32):
            return ctx.enter_context(nc.sbuf_tensor(name, shape, dt))

        def sem(name):
            return ctx.enter_context(nc.semaphore(name))

        PS = ctx.enter_context(nc.psum_tensor("PS", [P, 8, HALF], F32))
        scoreB = [PS[:, 2 * i:2 * i + 2, :] for i in range(2)]
        rotT = [PS[:, 4 + i, :] for i in range(NROT)]
        psO = PS[:, 7, :]

        HT = sb("HT", [P, TB, C])
        XAh = sb("XAh", [P, N], F32R)
        XAl = sb("XAl", [P, N], F32R)
        XC = sb("XC", [P, N], F32R)
        BIG = sb("BIG", [P, 12288])
        QK = sb("QK", [P, 8 * S], F32R)
        PA = sb("PA", [P, 6 * S])
        TQ = sb("TQ", [P, S])
        HH = sb("HH", [P, S], F32R)
        LL = sb("LL", [P, S], F32R)
        V1 = sb("V1", [P, B, KB, P])
        WRAW = sb("WRAW", [P, 2, 3, P])
        WH = sb("WH", [P, 2, 3, P], F32R)
        WL = sb("WL", [P, 2, 3, P], F32R)
        WP1 = sb("WP1", [P, 2, PAIRS, C])
        WP2 = sb("WP2", [MROW, B, 2, C])
        MZ = sb("MZ", [P, 2, KB, P], BF16)
        MC = sb("MC", [P, 2, KB])
        DEN = sb("DEN", [P, HALF])
        REC = sb("REC", [P, HALF])
        ORAW = sb("ORAW", [P, HALF])
        identF = sb("identF", [P, P])
        identB = sb("identB", [P, P], BF16)
        ones = sb("ones", [P, D1])
        STAT = sb("STAT", [P, 5, TB, 6])
        MV = sb("MV", [P, 5, TB, 2])
        SD = sb("SD", [P, 5, TB])
        RS = sb("RS", [P, 5, TB])
        NB = sb("NB", [P, 5, TB])
        gcols = sb("gcols", [P, 3, B, 2, 2])
        qkb = sb("qkb", [P, 2])
        qkbs = sb("qkbs", [P, 2])
        qks = sb("qks", [P, 1])
        bvc = sb("bvc", [P, PAIRS])
        maskc = sb("maskc", [P, TB])
        vocab = sb("vocab", [P, 1])
        gw = sb("gw", [P, 3])
        b1c = sb("b1c", [P, FB])
        rows = sb("rows", [P, 5, C])
        bias1 = sb("bias1", [P, C])
        bias2 = sb("bias2", [P, B, C])
        biasM = sb("biasM", [P, B, C])

        def q_of(u):
            return QK[:, (u % 2) * S:(u % 2 + 1) * S]

        def k_of(u):
            return QK[:, (2 + u % 2) * S:(3 + u % 2) * S]

        def q2_of(u):
            return QK[:, (4 + u % 2) * S:(5 + u % 2) * S]

        def k2_of(u):
            return QK[:, (6 + u % 2) * S:(7 + u % 2) * S]

        def q3_of(u):
            return QK[:, (u % 3) * S:(u % 3 + 1) * S]

        def k3_of(u):
            return QK[:, (3 + u % 3) * S:(4 + u % 3) * S]

        def prob(i):
            return PA[:, (i % NP) * S:(i % NP + 1) * S]

        def psum_of(u):
            return PA[:, (NP + u % 2) * S:(NP + 1 + u % 2) * S]

        OT = BIG[:, :].rearrange("p (b h x n) -> p b h x n", b=B, h=PAIRS, x=2)
        Y = BIG[:, 0:TB * C].rearrange("p (t c) -> p t c", t=TB)
        NT = [BIG[:, o:o + TB * 2 * P].rearrange("p (t c) -> p t c", t=TB) for o in (TB * C, TB * C, 7168)]
        V2W = D2 + 1
        V2 = BIG[:, 6144:6144 + B * KB * H * V2W].rearrange("p (b t h d) -> p b t h d", b=B, t=KB, h=H)
        O2S = [BIG[:, 9600 + 256 * i:9856 + 256 * i] for i in range(2)]
        HB = BIG[:, 3072:3072 + 3 * FB * HALF].rearrange("p (e m n) -> p e m n", e=3, m=FB)
        V2S = V1[:, 0, :, :].rearrange("p a b -> p (a b)")[:, 0:3 * KB * V2W].rearrange("p (u t d) -> p u t d", u=3, t=KB)
        O2U = [x[0:MROW, :].bitcast(F32).rearrange("p (g n) -> p g n", g=2) for x in (XAh, XAl)]
        R2 = [x.rearrange("p (b n) -> p b n", b=B) for x in (XC[0:MROW, :].bitcast(F32), BIG[0:MROW, 7168:9216])]
        O2 = BIG[0:MROW, 3072:3072 + 4 * S].rearrange("p (g b n) -> p g b n", g=2, b=B)
        QB = 2 * H * 2
        D2T = [BIG[0:QB, 10240 + 256 * g:10496 + 256 * g] for g in range(2)]
        R2T = [BIG[0:QB, 10752 + 256 * g:11008 + 256 * g] for g in range(2)]
        W2R = BIG[:, 9408:9408 + 6 * C]
        W2h = QK[:, 6 * S:6 * S + 6 * C]
        W2l = [QK[:, 6 * S + 6 * C:6 * S + 9 * C], WL[:, :, :, :].rearrange("p a b c -> p (a b c)")[:, 0:3 * C]]
        HS = [HH[:, :], PA[:, 4 * S:5 * S].bitcast(F32R)]
        LS = [LL[:, :], PA[:, 5 * S:6 * S].bitcast(F32R)]
        M2 = [(m, b) for m in (0, 2, 1, 3) for b in range(B)]
        WF1 = PA[:, 4 * S:4 * S + 2 * F]
        WF2 = PA[:, 0:4 * FB * C].rearrange("p (e c) -> p e c", e=4)

        def xs(stage, g, c):
            at = PA[:, 4 * S:6 * S] if stage == 0 else V1[:, :, :, :].rearrange("p b t d -> p (b t d)")
            return at[:, (2 * (g % 2) + c) * HALF:(2 * (g % 2) + c + 1) * HALF]

        def xbank(stage, g, c):
            return PS[:, (4 if stage else 0) + 2 * (g % 2) + c, :]

        QD = nc.dram_tensor("QD", [B, H, 2 * D2, S], F32, kind="Internal").ap()
        KD = nc.dram_tensor("KD", [B, H, 2 * D2, S], F32, kind="Internal").ap()
        OD = nc.dram_tensor("OD", [B, H, V2W, S], F32, kind="Internal").ap()
        RD = nc.dram_tensor("RD", [2, B, H // 2, S], F32, kind="Internal").ap()

        phase_done = sem("phase_done")
        conv_loads = sem("conv_loads")
        loads = sem("loads")
        dve_step = sem("dve_step")
        act_step = sem("act_step")
        pool_step = sem("pool_step")
        consts = sem("consts")
        conv_in = sem("conv_in")
        conv_out = sem("conv_out")
        h0_ready = sem("h0_ready")
        bias_ready = sem("bias_ready")
        rs_ready = sem("rs_ready")
        norm_act = sem("norm_act")
        norm_dve = sem("norm_dve")
        xc_low = sem("xc_low")
        twice_done = sem("twice_done")
        ht_ready = sem("ht_ready")
        var_ready = sem("var_ready")
        std_ready = sem("std_ready")
        tr_done = sem("tr_done")
        xt_high = sem("xt_high")
        xt_t = sem("xt_t")
        xt_t2 = sem("xt_t2")
        xt_low = sem("xt_low")
        raw1 = sem("raw1")
        wh_done = sem("wh_done")
        wl_done = sem("wl_done")
        w_used = sem("w_used")
        b_ready = sem("b_ready")
        rowmax = sem("rowmax")
        mz_hi = sem("mz_hi")
        mz_ready = sem("mz_ready")
        rot_ready = sem("rot_ready")
        rot_done = sem("rot_done")
        pv_done = sem("pv_done")
        psum_step = sem("psum_step")
        o_copied = sem("o_copied")
        rec_done = sem("rec_done")
        ot_done = sem("ot_done")
        hh_done = sem("hh_done")
        ll_done = sem("ll_done")
        moved_b = [sem(f"moved_b{i}") for i in range(2)]
        moved_c = [sem(f"moved_c{i}") for i in range(2)]
        proj_ready = sem("proj_ready")
        proj_used = sem("proj_used")
        w_loaded = sem("w_loaded")
        wfc2_loaded = sem("wfc2_loaded")
        q2_ready = sem("q2_ready")
        q2_high = sem("q2_high")
        q2_low = sem("q2_low")
        q2_stored = [sem(f"q2_stored{i}") for i in range(2)]
        loaded3 = [sem(f"loaded{i}") for i in range(3)]
        v2s_ready = sem("v2s_ready")
        sums_in = sem("sums_in")
        sums_out = sem("sums_out")
        o2_copied = sem("o2_copied")
        o2_stored = [sem(f"o2_stored{i}") for i in range(2)]
        o2_in = sem("o2_in")
        r2_in = sem("r2_in")
        fc1_ready = sem("fc1_ready")
        fc1_used = sem("fc1_used")
        fc2_ready = sem("fc2_ready")
        fc2_used = sem("fc2_used")
        stored = sem("stored")

        nphase = {}

        def barrier(eng, name):
            nphase[name] = nphase.get(name, 0) + 1
            eng.drain().then_inc(phase_done, 1)
            eng.wait_ge(phase_done, 5 * nphase[name])

        block = ctx.enter_context(nc.Block())

        LN = [(HT, HT, 1e-12), (HT, NT[0], 1e-5), (HT, Y, 1e-5), (Y, NT[1], 1e-5), (Y, NT[2], 1e-5)]
        DOUBLE = [(0, 0), (0, 1), (1, 0), (0, 2), (1, 1), (0, 3), (1, 2), (1, 3)]
        ITEMS = [[(j, g) for j, g in DOUBLE], [(2 + j, g) for j, g in DOUBLE], [(4, g) for g in range(4)]]
        ITEM0 = [0, 8, 16]
        ITEM0X = [0, 4, 8]
        TAKE = [{4: [0], 6: [1], 7: [2, 3]}, {4: [0], 6: [1], 7: [2, 3]}, {1: [0], 2: [1], 3: [2, 3]}]

        def wait_normed(eng, stage, j, g):
            done = [i for st in ITEMS[:stage] for i in st] + ITEMS[stage][:ITEMS[stage].index((j, g)) + 1]
            of_token = sum(i[0] == 0 for i in done)
            eng.wait_ge(norm_dve, 4 * of_token + 2 * (len(done) - of_token))
            if j > 0:
                eng.wait_ge(norm_act, 2 * (len(done) - of_token))

        BSLOT = [0, 0, 1, 2, 2, 2, 1, 0]
        PRO = 9
        FIRST, MID, LAST = range(3)

        def unit_tiles(j, var):
            t = []
            for i in range(KB):
                if i in (0, 1) and not (var == LAST and j >= 2):
                    t += [(i, "A", i, j)]
                if i == 1 and not (var == FIRST and j == 0):
                    t += [(i, "D", 0, j - 1)]
                t += [(i, "C", x, j) for x in range(2)]
                if j % 2 == 0 and i in (2, 3, 7) and not (var == LAST and j == 2):
                    t += [(i, "V", {2: 0, 3: 1, 7: 2}[i], j)]
                if i == 7 and not (var == LAST and j == 3):
                    t += [(i, "M", x, j) for x in range(2)]
            if var == LAST and j == 3:
                t += [(KB, "D", 0, j)]
            return t

        def key_of(tile):
            slot, kind, x, owner = tile
            return owner, kind, x, slot if kind == "C" else 0

        BODY = sum(len(unit_tiles(j, MID)) for j in range(4))
        BODY0 = sum(len(unit_tiles(j, FIRST)) for j in range(4))
        START = [PRO, PRO + BODY0 - BODY, PRO + BODY0 + (PAIRS - 2) * BODY]
        tile_no = [{key_of(t): START[var] + n for n, t in enumerate(t for j in range(4) for t in unit_tiles(j, var))}
                   for var in (FIRST, MID, LAST)]
        R1 = START[LAST] + len(tile_no[LAST])

        def number(var, p, key):
            if key[0] == -1 and key[1] == "C":
                n = START[var] - 3
            else:
                n = tile_no[var][key]
            return n + p * BODY if var == MID else n

        PV1 = NP + KB * 2 * H
        assert BODY % NROT == 0
        VBLK = [range(0, 3), range(3, 6), range(6, 8)]

        PRO2, ROT2 = 2, 2 * KB + 2
        LOADS3 = 16 * 3
        AHEAD = 10

        @block.sync
        def _(sp):
            for dst, src in [(PA[0:CONV_ROWS, 0:N].bitcast(I32), a["windows"]), (PA[0:CONV_ROWS, N:N + C], a["convw"]),
                             (vocab[:, :], a["vocab"])]:
                sp.dma_start(dst, src).then_inc(conv_loads, 16)
            for dst, src in [(maskc[:, :], a["mask"]), (identF[:, :], a["ident"]),
                             (gcols[:, :, :, :, :].rearrange("p a b c d -> p (a b c d)"), a["gcols"]),
                             (qks[:, :], a["qks"]), (bvc[:, :], a["bvc"]), (b1c[:, :], a["b1c"]),
                             (WP1[:, :, :, :].rearrange("p a b c -> p (a b c)"), a["wp1"]),
                             (WP2[:, 0, :, :].rearrange("p b c -> p (b c)"), a["wp2"]),
                             (gw[:, :], a["gw"].partition_broadcast(P)),
                             (rows[:, :, :], a["rows"].partition_broadcast(P))]:
                sp.dma_start(dst, src).then_inc(loads, 16)
            sp.dma_start(WRAW[:, :, :, :].rearrange("p a b c -> p (a b c)"), a["w1"][0]).then_inc(raw1, 16)
            sp.dma_start(qkb[:, :], a["qkb"][0]).then_inc(raw1, 16)

            def move(k, nth):
                sp.wait_ge(ll_done, nth)
                mb, mc = moved_b[k % 2], moved_c[k % 2]
                for dst, src, sem_ in [(q_of(k)[0:D1], HH[0:D1], mb), (q_of(k)[D1:P], LL[0:D1], mb),
                                       (k_of(k)[0:D1], HH[D1:P], mb), (k_of(k)[D1:P], HH[D1:P], mb),
                                       (q2_of(k)[0:D1], HH[0:D1], mc), (k2_of(k)[0:D1], LL[D1:P], mc)]:
                    sp.dma_start(dst.bitcast(F32), src.bitcast(F32)).then_inc(sem_, 16)

            move(0, 1)
            move(1, 2)

            def body1(p, var):
                if var != LAST:
                    nth = sp.snap(p + 1) if var == MID else p + 1
                    sp.wait_ge(wl_done, nth)
                    sp.dma_start(WRAW[:, :, :, :].rearrange("p a b c -> p (a b c)"), a["w1"][nth]).then_inc(raw1, 16)
                    sp.dma_start(qkb[:, :], a["qkb"][nth]).then_inc(raw1, 16)
                for j in range(4):
                    if var == LAST and j >= 2:
                        break
                    keys_used, nth = number(var, p, (j, "C", 1, 7)) + 1, 4 * p + j + 3
                    if var == MID:
                        keys_used, nth = sp.to_reg(keys_used), sp.to_reg(nth)
                    sp.wait_ge(rot_ready, keys_used)
                    move(j, nth)
            body1(0, FIRST)
            with sp.Fori(1, PAIRS - 1) as p:
                body1(p, MID)
            body1(PAIRS - 1, LAST)
            wait_normed(sp, 1, 3, 3)
            sp.dma_start(W2R, a["w2qkv"]).then_inc(w_loaded, 16)

            def load3(b, h, k):
                sp.dma_start(q3_of(k)[0:4 * D2].bitcast(F32), QD[b, h].unsqueeze(0).broadcast_to([2, 2 * D2, S]))\
                    .then_inc(loaded3[k % 3], 16)
                for part in range(2):
                    sp.dma_start(k3_of(k)[2 * D2 * part:2 * D2 * part + 2 * D2].bitcast(F32),
                                 KD[b, h, D2 * part:D2 * part + D2].unsqueeze(0).broadcast_to([2, D2, S]))\
                        .then_inc(loaded3[k % 3], 16)

            for n, (m, b) in enumerate(M2):
                sp.wait_ge(q2_high, 2 * n + 2)
                sp.wait_ge(q2_low, 2 * n + 2)
                dst = (QD if m < 2 else KD)[b, 6 * (m % 2):6 * (m % 2) + 6]
                sp.dma_start(dst[:, 0:D2, :], HS[n % 2][0:MROW].bitcast(F32)).then_inc(q2_stored[n % 2], 16)
                sp.dma_start(dst[:, D2:2 * D2, :], LS[n % 2][0:MROW].bitcast(F32)).then_inc(q2_stored[n % 2], 16)
                if n == 3:
                    for i in range(2):
                        sp.wait_ge(q2_stored[i], 64)
                    for u in range(3):
                        load3(u % 2, u // 2, u)
            for i in range(2):
                sp.wait_ge(q2_stored[i], 128)

            def store2(nth, j, b, h):
                sp.wait_ge(o2_copied, nth)
                for g in range(4):
                    sp.dma_start(OD[b, h, :, 256 * g:256 * g + 256], O2S[j % 2][32 * g:32 * g + V2W, :])\
                        .then_inc(o2_stored[j % 2], 16)

            def gather(g, h0, h1):
                for b in range(B):
                    sp.dma_start(O2U[b][D2 * h0:D2 * h1, g, :], OD[b, 6 * g + h0:6 * g + h1, 0:D2, :]).then_inc(o2_in, 16)

            def sums(g):
                for q in range(4):
                    sp.dma_start(D2T[g][H * q:H * q + H, :],
                                 OD[:, 6 * g:6 * g + 6, D2, 256 * q:256 * q + 256]).then_inc(sums_in, 16)

            def reciprocals_out(g):
                sp.wait_ge(rec_done, 8 + 4 * 2 * H + g + 1)
                for q in range(4):
                    sp.dma_start(RD[g, :, :, 256 * q:256 * q + 256], R2T[g][H * q:H * q + H, :]).then_inc(sums_out, 16)

            def reciprocals_in(g):
                sp.wait_ge(sums_out, 64 * g + 64)
                for b in range(B):
                    sp.dma_start(R2[g][:, b, :], RD[g, b].unsqueeze(1).broadcast_to([H // 2, D2, S])).then_inc(r2_in, 16)

            def body2(it, last):
                def reg(value):
                    return value if last else sp.snap(value)

                if last:
                    sp.dma_start(WF1, a["wfc1"]).then_inc(w_loaded, 16)
                    for i in range(2):
                        sp.wait_ge(o2_stored[i], 64 + 64 * 9)
                    gather(0, 0, 6)
                    gather(1, 0, 3)
                    sums(0)
                for j in range(7):
                    if last and j == 3:
                        reciprocals_out(0)
                    if last and j == 5:
                        reciprocals_in(0)
                    if j > 0:
                        store2(reg(6 * it + j + 1), j - 1, (j - 1) % 2, reg(3 * it + (j - 1) // 2))
                    if j < 6 and not (last and j >= 3):
                        keys_used = reg(R1 + it * 6 * ROT2 + PRO2 + ROT2 * (j + 1))
                        h = reg(3 * it + (j + 3) // 2)
                        sp.wait_ge(rot_ready, keys_used)
                        load3((j + 3) % 2, h, j)
            with sp.Fori(0, H // 3 - 1) as it:
                body2(it, False)
            body2(H // 3 - 1, True)
            for i in range(2):
                sp.wait_ge(o2_stored[i], 64 * (H + 1))
            gather(1, 3, 6)
            sums(1)
            reciprocals_out(1)
            reciprocals_in(1)
            sp.dma_start(WF2[:, 0], a["wfc2"]).then_inc(wfc2_loaded, 16)
            for t in range(TB):
                sp.wait_ge(fc2_used, t + 1)
                sp.dma_start(out[P * t:P * t + P, :], HT[:, t, :]).then_inc(stored, 16)
            sp.wait_ge(stored, 16 * TB)
            barrier(sp, "sp")

        @block.gpsimd
        def _(pool):
            nc.gpsimd.memset(ones[:, :], 1.0).then_inc(consts, 1)
            nc.gpsimd.memset(MZ[:, :, :, :], 0.0).then_inc(consts, 1)
            pool.wait_ge(loads, 16 * 10)
            nc.gpsimd.tensor_scalar(WP2[:, 1, :, :], WP2[:, 0, :, :], gw[0:MROW, 0:1], None, ALU.mult).then_inc(pool_step, 1)
            nc.gpsimd.tensor_scalar(bias2[:, 1, :], rows[:, 3, :], gw[:, 0:1], None, ALU.mult).then_inc(pool_step, 1)
            nc.gpsimd.tensor_scalar(biasM[:, 1, :], rows[:, 4, :], gw[:, 0:1], None, ALU.mult).then_inc(pool_step, 1)
            nc.gpsimd.tensor_copy(bias2[:, 0, :], rows[:, 3, :]).then_inc(pool_step, 1)
            nc.gpsimd.tensor_copy(biasM[:, 0, :], rows[:, 4, :]).then_inc(pool_step, 1)
            pool.wait_ge(pool_step, 5)
            for i in range(2):
                nc.gpsimd.memset(q2_of(i)[D1:P].bitcast(F32), 0.0).then_inc(consts, 1)
                nc.gpsimd.memset(k2_of(i)[D1:P].bitcast(F32), 0.0).then_inc(consts, 1)
            pool.wait_ge(consts, 6)
            for i in range(2):
                nc.gpsimd.memset(k2_of(i)[MROW:MROW + 2].bitcast(F32), 1.0).then_inc(consts, 1)

            pool.wait_ge(consts, 8)
            def twice(stage, j, g):
                wait_normed(pool, stage, j, g)
                blocks = NT[stage][:, 4 * g:4 * g + 4, :]
                nc.gpsimd.tensor_copy(blocks[:, :, C:2 * P], blocks[:, :, P:C]).then_inc(twice_done, 1)

            def chunk_low(stage, g):
                n = ITEM0X[stage] + g + 1
                cols = slice(HALF * g, HALF * g + HALF)
                pool.wait_ge(xt_high, 2 * n)
                nc.gpsimd.tensor_tensor(XC[64:P, cols], xs(stage, g, 1)[64:P], XC[64:P, cols].bitcast(F32), ALU.subtract)\
                    .then_inc(xc_low, 1)
                pool.wait_ge(xc_low, n)

            def x_work(stage, j):
                for g in range(4):
                    twice(stage, j, g)
                    pool.wait_ge(twice_done, 4 * stage + g + 1)
                    if g:
                        chunk_low(stage, g - 1)
                chunk_low(stage, 3)
            x_work(0, 1)
            pool.wait_ge(bias_ready, 1)
            nc.gpsimd.tensor_tensor(HT[:, :, :], HT[:, :, :], bias1[:, :].unsqueeze(1).broadcast_to([P, TB, C]), ALU.add)\
                .then_inc(ht_ready, 1)
            pool.sem_inc(psum_step, NP)

            def body1(p, var):
                for j in range(4):
                    u = 4 * p + j
                    for i in range(1, KB):
                        pool.wait_ge(rot_done, number(var, p, (j, "C", 1, i)) + 1)
                        if i == 1:
                            pool.wait_ge(rec_done, 4 * u + 4)
                            nc.gpsimd.tensor_tensor(psum_of(j), prob(0), prob(1), ALU.add).then_inc(psum_step, 1)
                        else:
                            pool.wait_ge(psum_step, NP + 7 * u + i - 1)
                            nc.gpsimd.tensor_tensor(psum_of(j), prob(i), psum_of(j), ALU.add).then_inc(psum_step, 1)
            body1(0, FIRST)
            with pool.Fori(1, PAIRS - 1) as p:
                body1(p, MID)
            body1(PAIRS - 1, LAST)
            wait_normed(pool, 1, 2, 0)
            pool.wait_ge(psum_step, NP + 7 * 2 * H)
            for i in range(3):
                nc.gpsimd.memset(q3_of(i)[D1:P].bitcast(F32), 0.0).then_inc(consts, 1)
                nc.gpsimd.memset(k3_of(i)[D1:P].bitcast(F32), 0.0).then_inc(consts, 1)
            pool.wait_ge(consts, 8 + 6)
            for i in range(3):
                nc.gpsimd.memset(k3_of(i)[MROW:MROW + 2].bitcast(F32), 1.0).then_inc(consts, 1)
            pool.wait_ge(consts, 8 + 9)
            x_work(1, 3)
            pool.wait_ge(tr_done, 8)
            nc.gpsimd.memset(V2[:, :, :, :, D2:V2W], 1.0).then_inc(consts, 1)
            pool.wait_ge(q2_high, 16 + TB)
            pool.wait_ge(consts, 8 + 9 + 1)
            for b in range(B):
                nc.gpsimd.tensor_tensor(HT[:, KB * b:KB * b + KB, :], HT[:, KB * b:KB * b + KB, :],
                                        biasM[:, b, :].unsqueeze(1).broadcast_to([P, KB, C]), ALU.add).then_inc(ht_ready, 1)

            def stage_v(b, h, k):
                nc.gpsimd.tensor_copy(V2S[:, k % 3, :, :], V2[:, b, :, h, :]).then_inc(v2s_ready, 1)

            for u in range(3):
                stage_v(u % 2, u // 2, u)

            def body2(it, last):
                for j in range(6):
                    if not (last and j >= 3):
                        pool.wait_ge(pv_done, PV1 + KB * (6 * it + j + 1))
                        stage_v((j + 3) % 2, 3 * it + (j + 3) // 2, j)
            with pool.Fori(0, H // 3 - 1) as it:
                body2(it, False)
            body2(H // 3 - 1, True)
            x_work(2, 4)
            pool.wait_ge(wfc2_loaded, 16)
            pool.wait_ge(wl_done, PAIRS + 2 + 2)
            for i in range(3):
                nc.gpsimd.tensor_scalar(WF2[:, i + 1], WF2[:, 0], gw[:, i:i + 1], None, ALU.mult).then_inc(pool_step, 1)
            pool.wait_ge(ht_ready, 3)
            nc.gpsimd.tensor_tensor(HT[:, :, :], HT[:, :, :], Y[:, :, :], ALU.add).then_inc(ht_ready, 1)
            barrier(pool, "pool")

        @block.scalar
        def _(act):
            act.wait_ge(loads, 16 * 10)
            for t in range(TB):
                act.wait_ge(conv_out, t // 2 * 2 + 2)
                nc.scalar.activation(HT[:, t, :], PS[:, t // 2, 256 * (t % 2):256 * (t % 2) + C], ACT.Identity,
                                     scale=maskc[:, t:t + 1]).then_inc(h0_ready, 1)
            nx = [0]

            def x_parts(stage, g):
                nx[0] += 1
                act.wait_ge(tr_done, nx[0])
                if g >= 2:
                    act.wait_ge(xt_low, nx[0] - 2)
                cols = slice(HALF * g, HALF * g + HALF)
                for c, to, s_ in ((0, xs(stage, g, 0), xt_t), (0, XAh[:, cols], xt_high), (1, XC[:, cols], xt_high)):
                    if c == 1:
                        act.wait_ge(xt_t2, nx[0])
                    nc.scalar.activation(to, xbank(stage, g, c), ACT.Identity, scale=gcols[:, stage, g // 2, c, 0:1],
                                         bias=gcols[:, stage, g // 2, c, 1:2]).then_inc(s_, 1)

            def layer_norms(stage):
                def deviation(k):
                    j, g = ITEMS[stage][k]
                    act.wait_ge(var_ready, ITEM0[stage] + k + 1)
                    sd = SD[:, j, 4 * g:4 * g + 4]
                    nc.scalar.activation(sd, sd, ACT.Sqrt).then_inc(std_ready, 1)
                deviation(0)
                for k, (j, g) in enumerate(ITEMS[stage]):
                    if k + 1 < len(ITEMS[stage]):
                        deviation(k + 1)
                    act.wait_ge(rs_ready, ITEM0[stage] + k + 1)
                    src, dst, _ = LN[j]
                    for t in range(4 * g, 4 * g + (0 if j == 0 else 2)):
                        nc.scalar.activation(dst[:, t, 0:C], src[:, t, :], ACT.Identity, scale=RS[:, j, t:t + 1],
                                             bias=NB[:, j, t:t + 1]).then_inc(norm_act, 1)
                    for g_ in TAKE[stage].get(k, []):
                        x_parts(stage, g_)
            layer_norms(0)

            act.sem_inc(o_copied, 1)

            def take(n):
                act.wait_ge(rot_ready, n + 1)

            def t_half(k, hh, hcol, n):
                take(n)
                nc.scalar.activation(TQ[:, HALF * hh:HALF * hh + HALF], rotT[k % NROT], ACT.Identity,
                                     scale=qks[:, 0:1], bias=qkbs[:, hcol:hcol + 1]).then_inc(rot_done, 1)

            def v_tile(k, b, part, n):
                take(n)
                blk = VBLK[part]
                nc.scalar.activation(V1[:, b, blk[0]:blk[-1] + 1, :].rearrange("p t d -> p (t d)"),
                                     rotT[k % NROT][:, 0:P * len(blk)], ACT.Copy).then_inc(rot_done, 1)

            def m_tile(k, dst, hh, n):
                take(n)
                nc.scalar.activation(dst[MROW:MROW + 2, HALF * hh:HALF * hh + HALF], rotT[k % NROT][MROW:MROW + 2, :],
                                     ACT.Copy).then_inc(rot_done, 1)

            for k in range(2):
                if k == 1:
                    act.wait_ge(ll_done, 1)
                for hh in range(2):
                    t_half(2 * k + hh, hh, k, 2 * k + hh)
            for part in range(3):
                v_tile(4 + part, 0, part, 4 + part)
            for hh in range(2):
                m_tile(7 + hh, q2_of(0), hh, 7 + hh)

            def body1(p, var):
                for j in range(4):
                    u = 4 * p + j
                    for tile in unit_tiles(j, var):
                        i, kind, x, owner = tile
                        k = tile_no[var][key_of(tile)]
                        n = number(var, p, key_of(tile))
                        if kind == "C":
                            take(n)
                            if x == 0:
                                act.wait_ge(pv_done, KB * u + i + 1)
                                act.wait_ge(psum_step, 7 * u + i + 1 if i < 4 else 7 * u + max(i - 4, 1) + 4)
                            nc.scalar.activation(prob(i)[:, HALF * x:HALF * x + HALF], rotT[k % NROT], ACT.Exp)\
                                .then_inc(rot_done, 1)
                            if i == 0 and x == 1 and not (var == FIRST and j == 0):
                                copy_o(u - 1)
                        elif kind == "D":
                            take(n)
                            act.wait_ge(rec_done, 4 * (4 * p + owner) + 8)
                            nc.scalar.activation(DEN[:, :], rotT[k % NROT], ACT.Copy).then_inc(rot_done, 1)
                        elif kind == "A":
                            if x == 0:
                                act.wait_ge(ll_done, u + 2)
                            t_half(k, x, j % 2, n)
                        elif kind == "V":
                            v_tile(k, 1 if j == 0 else 0, x, n)
                        elif kind == "M":
                            m_tile(k, q2_of(j + 1), x, n)

            def copy_o(u):
                act.wait_ge(pv_done, NP + KB * (u + 1))
                act.wait_ge(ot_done, 2 * u + 2)
                nc.scalar.activation(ORAW[:, :], psO, ACT.Copy).then_inc(o_copied, 1)
            body1(0, FIRST)
            with act.Fori(1, PAIRS - 1) as p:
                body1(p, MID)
            body1(PAIRS - 1, LAST)
            copy_o(4 * PAIRS - 1)
            layer_norms(1)

            for n, (m, b) in enumerate(M2):
                for hh in range(2):
                    act.wait_ge(q2_ready, 2 * n + hh + 1)
                    if hh == 0 and n >= 2:
                        act.wait_ge(q2_stored[n % 2], 32 * (n // 2))
                    nc.scalar.activation(HS[n % 2][0:MROW, HALF * hh:HALF * hh + HALF], PS[0:MROW, (2 * n + hh) % 4, :],
                                         ACT.Identity, scale=0.25 if m < 2 else 1.0).then_inc(q2_high, 1)
            for t in range(TB):
                act.wait_ge(q2_ready, 16 + t + 1)
                nc.scalar.activation(V2[:, t // KB, t % KB, :, 0:D2],
                                     PS[:, 4 + t % 4, 0:C].rearrange("p (h d) -> p h d", h=H), ACT.Copy)\
                    .then_inc(q2_high, 1)
            base = R1
            for hh in range(2):
                act.wait_ge(rot_ready, base + hh + 1)
                nc.scalar.activation(q3_of(0)[MROW:MROW + 2, HALF * hh:HALF * hh + HALF], rotT[hh][MROW:MROW + 2, :],
                                     ACT.Copy).then_inc(rot_done, 1)

            def body2(it, last):
                for j in range(6):
                    u = 6 * it + j
                    k = ROT2 * j + PRO2
                    for i in range(KB):
                        if i == 7:
                            if not (last and j == 5):
                                for hh in range(2):
                                    act.wait_ge(rot_ready, base + it * 6 * ROT2 + k + 1)
                                    nc.scalar.activation(q3_of(j + 1)[MROW:MROW + 2, HALF * hh:HALF * hh + HALF],
                                                         rotT[k % NROT][MROW:MROW + 2, :], ACT.Copy).then_inc(rot_done, 1)
                                    k += 1
                        for hh in range(2):
                            act.wait_ge(rot_ready, base + it * 6 * ROT2 + k + 1)
                            if hh == 0:
                                act.wait_ge(pv_done, PV1 - NP + KB * u + i + 1)
                            nc.scalar.activation(prob(i)[:, HALF * hh:HALF * hh + HALF], rotT[k % NROT], ACT.Exp)\
                                .then_inc(rot_done, 1)
                            k += 1
            with act.Fori(0, H // 3 - 1) as it:
                body2(it, False)
            body2(H // 3 - 1, True)
            layer_norms(2)
            nh = 0
            for g in range(4):
                for e in range(1 if g < 2 else 3):
                    for m in range(FB):
                        act.wait_ge(fc1_ready, nh + 1)
                        if m == 0 and g > 0:
                            act.wait_ge(fc2_ready, 4 * g)
                        nc.scalar.activation(HB[:, e, m, :], PS[:, nh % 4, :], ACT.Gelu, bias=b1c[:, m:m + 1])\
                            .then_inc(fc1_used, 1)
                        nh += 1
            barrier(act, "act")

        @block.vector
        def _(dve):
            cnt = [0]

            def link(ins):
                cnt[0] += 1
                ins.then_inc(dve_step, 1)
                dve.wait_ge(dve_step, cnt[0])

            def note(ins):
                cnt[0] += 1
                ins.then_inc(dve_step, 1)

            nx = [0]

            def x_low(stage, g):
                nx[0] += 1
                n = nx[0]
                cols = slice(HALF * g, HALF * g + HALF)
                dve.wait_ge(tr_done, n)
                if g >= 2:
                    dve.wait_ge(xc_low, n - 2)
                nc.vector.tensor_scalar(xs(stage, g, 1), xbank(stage, g, 1), gcols[:, stage, g // 2, 1, 0:1],
                                        gcols[:, stage, g // 2, 1, 1:2], ALU.mult, ALU.add).then_inc(xt_t2, 1)
                dve.wait_ge(xt_high, 2 * n - 1)
                nc.vector.tensor_tensor(XAl[:, cols], xs(stage, g, 0), XAh[:, cols].bitcast(F32), ALU.subtract)\
                    .then_inc(xt_low, 1)

            def layer_norms(stage, before):
                def normalise(j, g):
                    src, dst, _ = LN[j]
                    if j == 0:
                        for step in range(2):
                            for t in range(4 * g, 4 * g + 4):
                                ins = nc.vector.scalar_tensor_tensor(
                                    out=HT[:, t, :], in0=HT[:, t, :], scalar=(MV[:, j, t, 0:1], RS[:, j, t:t + 1])[step],
                                    in1=rows[:, step, :], op0=(ALU.subtract, ALU.mult)[step], op1=(ALU.mult, ALU.add)[step])
                                if step == 0:
                                    note(ins)
                                else:
                                    ins.then_inc(norm_dve, 1)
                            dve.wait_ge(dve_step, cnt[0])
                    else:
                        for t in range(4 * g + 2, 4 * g + 4):
                            nc.vector.tensor_scalar(dst[:, t, 0:C], src[:, t, :], MV[:, j, t, 0:1], RS[:, j, t:t + 1],
                                                    ALU.subtract, ALU.mult).then_inc(norm_dve, 1)

                def stats(k):
                    j, g = ITEMS[stage][k]
                    before(j, g)
                    src, _, eps = LN[j]
                    blocks = range(4 * g, 4 * g + 4)
                    for t in blocks:
                        note(nc.vector.bn_stats(STAT[:, j, t, :], src[:, t, :]))
                    dve.wait_ge(dve_step, cnt[0])
                    for t in blocks:
                        note(nc.vector.bn_aggr(MV[:, j, t, :], STAT[:, j, t, :]))
                    dve.wait_ge(dve_step, cnt[0])
                    nc.vector.tensor_scalar(SD[:, j, 4 * g:4 * g + 4], MV[:, j, 4 * g:4 * g + 4, 1], eps, None, ALU.add)\
                        .then_inc(var_ready, 1)
                stats(0)
                for k, (j, g) in enumerate(ITEMS[stage]):
                    if k + 1 < len(ITEMS[stage]):
                        stats(k + 1)
                    cols = slice(4 * g, 4 * g + 4)
                    dve.wait_ge(std_ready, ITEM0[stage] + k + 1)
                    link(nc.vector.reciprocal(RS[:, j, cols], SD[:, j, cols]))
                    nc.vector.scalar_tensor_tensor(out=NB[:, j, cols], in0=MV[:, j, cols, 0], scalar=-1.0, in1=RS[:, j, cols],
                                                   op0=ALU.mult, op1=ALU.mult).then_inc(rs_ready, 1)
                    normalise(j, g)
                    for g_ in TAKE[stage].get(k, []):
                        x_low(stage, g_)

            dve.wait_ge(conv_loads, 16 * 3)
            E = QK[0:CONV_ROWS, 0:N]
            WS = HH[0:CONV_ROWS, 0:C]
            link(nc.vector.tensor_copy(WS, PA[0:CONV_ROWS, N:N + C]))
            link(nc.vector.tensor_tensor(WS[64:CONV_ROWS], PA[64:CONV_ROWS, N:N + C], WS[64:CONV_ROWS].bitcast(F32),
                                         ALU.subtract))
            nc.vector.tensor_scalar(E, PA[0:CONV_ROWS, 0:N].bitcast(I32), vocab[0:CONV_ROWS, 0:1], None, ALU.is_equal)\
                .then_inc(conv_in, 1)
            dve.wait_ge(loads, 16 * 10)
            link(nc.vector.tensor_copy(identB[:, :], identF[:, :]))
            dve.wait_ge(pool_step, 5)
            for i, heads, ch in ((1, HKEEP[1] * D2, KEEP[1]), (2, HKEEP[2] * D2, KEEP[2])):
                w = WP2[0:heads, 1, 0, 0:ch]
                note(nc.vector.scalar_tensor_tensor(out=w, in0=WP2[0:heads, 0, 0, 0:ch], scalar=gw[0:heads, i:i + 1], in1=w,
                                                    op0=ALU.mult, op1=ALU.add))
                for bias, r in ((bias2, 3), (biasM, 4)):
                    note(nc.vector.scalar_tensor_tensor(out=bias[:, 1, 0:ch], in0=rows[:, r, 0:ch], scalar=gw[:, i:i + 1],
                                                        in1=bias[:, 1, 0:ch], op0=ALU.mult, op1=ALU.add))
                dve.wait_ge(dve_step, cnt[0])
            def before0(j, g):
                if j == 0:
                    dve.wait_ge(h0_ready, 4 * g + 4)
                else:
                    wait_normed(dve, 0, 0, g)
            layer_norms(0, before0)
            dve.wait_ge(proj_ready, 1)
            nc.vector.tensor_tensor(bias1[:, :], PS[:, 7, 0:C], rows[:, 2, :], ALU.add).then_inc(bias_ready, 1)

            def split_w(p):
                dve.wait_ge(raw1, 32 * p + 32)
                nc.vector.tensor_scalar(qkbs[:, :], qkb[:, :], qks[:, 0:1], None, ALU.mult).then_inc(wh_done, 1)
                nc.vector.tensor_copy(WH[:, :, :, :], WRAW[:, :, :, :]).then_inc(wh_done, 1)
                dve.wait_ge(wh_done, 2 * p + 2)
                nc.vector.tensor_tensor(WL[:, :, :, :], WRAW[:, :, :, :], WH[:, :, :, :].bitcast(F32), ALU.subtract)\
                    .then_inc(wl_done, 1)

            def parts(u, n):
                dve.wait_ge(rot_done, n + 1)
                nc.vector.tensor_copy(HH[:, :], TQ[:, :]).then_inc(hh_done, 1)
                dve.wait_ge(hh_done, u + 1)
                nc.vector.tensor_tensor(LL[:, :], TQ[:, :], HH[:, :].bitcast(F32), ALU.subtract).then_inc(ll_done, 1)

            def placed(j, turn):
                dve.wait_ge(moved_b[j % 2], 64 * turn)
                dve.wait_ge(moved_c[j % 2], 32 * turn)

            def row_max(k, i, n, wait_mz=None):
                dve.wait_ge(b_ready, n + 1)
                if i == 0 and wait_mz is not None:
                    dve.wait_ge(mz_ready, wait_mz + 1)
                nc.vector.tensor_reduce(MC[:, k % 2, i:i + 1], scoreB[i % 2], AX.XY, ALU.max, negate=True)\
                    .then_inc(rowmax, 1)

            def split_max(k, u, n):
                dve.wait_ge(rowmax, n)
                nc.vector.tensor_copy(MZ[:, k % 2, :, MROW], MC[:, k % 2, :]).then_inc(mz_hi, 1)
                dve.wait_ge(mz_hi, u + 1)
                nc.vector.tensor_tensor(MZ[:, k % 2, :, MROW + 1], MC[:, k % 2, :], MZ[:, k % 2, :, MROW], ALU.subtract)\
                    .then_inc(mz_ready, 1)

            dve.sem_inc(rec_done, 8)
            dve.sem_inc(ot_done, 2)
            dve.sem_inc(mz_ready, 1)
            split_w(0)
            parts(0, 1)
            placed(0, 1)
            parts(1, 3)
            for i in range(KB):
                row_max(0, i, i)
            split_max(0, 0, KB)

            def recip(u, q, n):
                if q == 0:
                    dve.wait_ge(rot_done, n + 1)
                    dve.wait_ge(ot_done, 2 * u + 2)
                nc.vector.reciprocal(REC[:, P * q:P * q + P], DEN[:, P * q:P * q + P]).then_inc(rec_done, 1)

            def outputs(u, jj, pp):
                dve.wait_ge(o_copied, u + 2)
                dve.wait_ge(rec_done, 8 + 4 * (u + 1))
                for lo in range(2):
                    half = lo if jj % 2 == 0 else 1 - lo
                    s = slice(D1 * lo, D1 * lo + D1)
                    dst = OT[s, jj // 2, pp, half, :] if isinstance(pp, int) else \
                        OT[s, jj // 2, bass.ds(pp, 1), half, :].rearrange("p a n -> p (a n)")
                    nc.vector.tensor_tensor(dst, ORAW[s, :], REC[s, :], ALU.mult).then_inc(ot_done, 1)

            def body1(p, var):
                for j in range(4):
                    u = 4 * p + j
                    before = not (var == FIRST and j == 0)
                    d = number(var, p, (j - 1, "D", 0, 0)) if before else None

                    def mx(i):
                        if not (var == LAST and j == 3):
                            row_max(j + 1, i, KB * (u + 1) + i, u)
                    if before:
                        for q in range(3):
                            recip(u - 1, q, d)
                    mx(0)
                    if not (var == LAST and j >= 2):
                        placed(j + 1, 2 * p + (j + 1) // 2 + 1)
                        parts(u + 2, number(var, p, (j, "A", 1, 0)))
                    mx(1)
                    mx(2)
                    mx(3)
                    if j == 1 and var != LAST:
                        dve.wait_ge(rot_done, number(var, p, (1, "A", 1, 0)) + 1)
                        split_w(p + 1)
                    for i in range(4, KB):
                        mx(i)
                    if not (var == LAST and j == 3):
                        split_max(j + 1, u + 1, KB * (u + 2))
                    if before:
                        recip(u - 1, 3, d)
                        outputs(u - 1, (j - 1) % 4, p if j else p - 1)
            body1(0, FIRST)
            with dve.Fori(1, PAIRS - 1) as p:
                body1(p, MID)
            body1(PAIRS - 1, LAST)
            for q in range(4):
                recip(4 * PAIRS - 1, q, number(LAST, PAIRS - 1, (3, "D", 0, 0)))
            outputs(4 * PAIRS - 1, 3, PAIRS - 1)
            def before1(j, g):
                if j == 2:
                    for t in range(4 * g, 4 * g + 4):
                        dve.wait_ge(proj_ready, t + 2)
                        note_used(nc.vector.tensor_tensor(HT[:, t, :], PS[:, t % 4, 0:C], HT[:, t, :], ALU.add))
                    dve.wait_ge(proj_used, used[0])
                else:
                    wait_normed(dve, 1, 2, g)

            used = [0]

            def note_used(ins):
                used[0] += 1
                ins.then_inc(proj_used, 1)
            dve.wait_ge(ht_ready, 1)
            layer_norms(1, before1)
            dve.wait_ge(w_loaded, 16)
            link(nc.vector.tensor_copy(W2h, W2R))
            for i in range(2):
                s = slice(3 * C * i, 3 * C * i + 3 * C)
                nc.vector.tensor_tensor(W2l[i], W2R[:, s], W2h[:, s].bitcast(F32), ALU.subtract).then_inc(wl_done, 1)
            for n, (m, b) in enumerate(M2):
                for hh in range(2):
                    dve.wait_ge(q2_high, 2 * n + hh + 1)
                    if hh == 0 and n >= 2:
                        dve.wait_ge(q2_stored[n % 2], 32 * (n // 2))
                    s = slice(HALF * hh, HALF * hh + HALF)
                    nc.vector.scalar_tensor_tensor(out=LS[n % 2][0:MROW, s], in0=PS[0:MROW, (2 * n + hh) % 4, :],
                                                   scalar=0.25 if m < 2 else 1.0, in1=HS[n % 2][0:MROW, s].bitcast(F32),
                                                   op0=ALU.mult, op1=ALU.subtract).then_inc(q2_low, 1)
            UB = 2 * H
            dve.sem_inc(o2_copied, 1)
            for i in range(2):
                dve.sem_inc(o2_stored[i], 64)
            for n in range(AHEAD):
                row_max(n // KB, n % KB, KB * UB + n, UB + n // KB - 1)
                if n == KB - 1:
                    split_max(0, UB, KB * (UB + 1))

            def body2(it, last):
                for j in range(6):
                    u = 6 * it + j
                    for i in range(KB):
                        w = KB * j + i + AHEAD
                        if not (last and w >= 6 * KB):
                            row_max(w // KB, w % KB, it * 6 * KB + KB * UB + w, 6 * it + UB + w // KB - 1)
                            if w % KB == KB - 1:
                                split_max(w // KB, 6 * it + UB + w // KB, it * 6 * KB + KB * UB + w + 1)
                        if i == 0 and j > 0:
                            copy_o2(6 * it, j - 1)
                    if last and j == 1:
                        sums_to_reciprocals(0)
                    if last and j == 4:
                        scale_outputs(0)
                copy_o2(6 * it, 5)

            def sums_to_reciprocals(g):
                dve.wait_ge(sums_in, 64 * (g + 1))
                nc.vector.reciprocal(R2T[g], D2T[g]).then_inc(rec_done, 1)

            def scale_outputs(g):
                dve.wait_ge(o2_in, (64, 96)[g])
                dve.wait_ge(r2_in, 32 * (g + 1))
                for b in range(B):
                    nc.vector.tensor_tensor(O2[:, g, b, :], O2U[b][:, g, :], R2[g][:, b, :], ALU.mult).then_inc(ot_done, 1)

            def copy_o2(u0, j):
                dve.wait_ge(pv_done, PV1 + KB * (u0 + j + 1))
                dve.wait_ge(o2_stored[j % 2], u0 * 32 + 64 * (j // 2) + 64)
                nc.vector.tensor_copy(O2S[j % 2], psO[:, 0:256]).then_inc(o2_copied, 1)
            with dve.Fori(0, H // 3 - 1) as it:
                body2(it, False)
            body2(H // 3 - 1, True)
            for b in range(B):
                note(nc.vector.tensor_tensor(Y[:, KB * b:KB * b + KB, :], Y[:, KB * b:KB * b + KB, :],
                                             bias2[:, b, :].unsqueeze(1).broadcast_to([P, KB, C]), ALU.add))
            sums_to_reciprocals(1)
            dve.wait_ge(w_loaded, 32)
            raw = WF1
            Mh, Ml = QK[:, 0:2 * F], QK[:, 2 * F:4 * F]
            Zh, Zl = QK[0:MROW, 4 * F:5 * F], QK[0:MROW, 5 * F:6 * F]
            link(nc.vector.tensor_copy(Mh, raw))
            link(nc.vector.tensor_tensor(Ml, raw, Mh.bitcast(F32), ALU.subtract))
            dve.sem_inc(wl_done, 2)
            scale_outputs(1)
            dve.wait_ge(dve_step, cnt[0])
            note(nc.vector.memset(Zh[64:MROW].bitcast(F32), 0.0))
            note(nc.vector.memset(Zl[64:MROW].bitcast(F32), 0.0))
            note(nc.vector.tensor_copy(Zh[0:64], Mh[0:64, 0:F].bitcast(F32)))
            note(nc.vector.tensor_copy(Zl[0:64], Ml[0:64, 0:F].bitcast(F32)))

            def before2(j, g):
                for t in range(4 * g, 4 * g + 4):
                    dve.wait_ge(proj_ready, TB + 1 + t + 1)
                    note_used(nc.vector.tensor_tensor(Y[:, t, :], PS[:, t % 4, 0:C], Y[:, t, :], ALU.add))
                dve.wait_ge(proj_used, used[0])
            layer_norms(2, before2)
            dve.wait_ge(ht_ready, 4)
            for t in range(TB):
                dve.wait_ge(fc2_ready, t + 1)
                nc.vector.tensor_tensor(HT[:, t, :], PS[:, 4 + t % 4, 0:C], HT[:, t, :], ALU.add).then_inc(fc2_used, 1)
            barrier(dve, "dve")

        @block.tensor
        def _(pe):
            pe.wait_ge(conv_in, 1)
            pe.wait_ge(dve_step, 2)
            WS = HH[0:CONV_ROWS, 0:C]
            for t in range(TB):
                pe.matmul(PS[:, t // 2, 256 * (t % 2):256 * (t % 2) + C], QK[0:CONV_ROWS, P * t:P * t + P], WS,
                          start=True, stop=True).then_inc(conv_out, 1)
            pe.wait_ge(h0_ready, TB)
            for p in range(PAIRS):
                mm = pe.matmul(PS[:, 7, 0:C], bvc[:, p:p + 1].broadcast_to([P, P]), WP1[:, 0, p, :],
                               start=(p == 0), stop=(p == PAIRS - 1))
            mm.then_inc(proj_ready, 1)

            nx = [0]

            def transpose(stage, g):
                nx[0] += 1
                pe.wait_ge(twice_done, nx[0])
                if g >= 2:
                    pe.wait_ge(xt_high, 2 * (nx[0] - 2))
                for tb in range(4):
                    cols = slice(P * tb, P * tb + P)
                    pe.transpose(xbank(stage, g, 0)[:, cols], NT[stage][:, 4 * g + tb, 0:P], identF[:, :])
                    mm = pe.transpose(xbank(stage, g, 1)[:, cols], NT[stage][:, 4 * g + tb, P:2 * P], identF[:, :])
                mm.then_inc(tr_done, 1)
            for g in range(4):
                transpose(0, g)
            pe.wait_ge(xt_low, 4)
            pe.wait_ge(xc_low, 4)

            def free(n):
                pe.wait_ge(rot_done, n - NROT + 1)

            CHUNKS = [(XAh, WH, 0), (XAl, WH, 0), (XAh, WL, 0), (XC, WH, 1), (XC, WL, 1)]

            def a_tile(k, b, hd, hh):
                for c, (x, w, r) in enumerate(CHUNKS):
                    mm = pe.matmul(rotT[k % NROT], w[:, r, hd, :], x[:, S * b + HALF * hh:S * b + HALF * hh + HALF],
                                   start=(c == 0), stop=(c == len(CHUNKS) - 1))
                mm.then_inc(rot_ready, 1)

            def v_tile(k, b, part):
                for x_, t in enumerate(VBLK[part]):
                    for c, (x, w, r) in enumerate(CHUNKS):
                        mm = pe.matmul(rotT[k % NROT][:, P * x_:P * x_ + P], x[:, S * b + P * t:S * b + P * t + P],
                                       w[:, r, 2, :], start=(c == 0), stop=(c == len(CHUNKS) - 1))
                mm.then_inc(rot_ready, 1)

            def m_tile(k, j, hh):
                for i in range(4):
                    mm = pe.matmul(rotT[k % NROT][:, P * i:P * i + P], MZ[:, j % 2, 4 * hh + i, :], identB[:, :],
                                   start=True, stop=True)
                mm.then_inc(rot_ready, 1)

            def b_tile(q, k_, i, n):
                pe.wait_ge(rowmax, n - 1)
                for hh in range(2):
                    mm = pe.matmul(scoreB[i % 2][:, hh, :], q[:, P * i:P * i + P], k_[:, HALF * hh:HALF * hh + HALF],
                                   start=True, stop=True)
                mm.then_inc(b_ready, 1)

            pe.wait_ge(wl_done, 1)
            pe.wait_ge(bias_ready, 1)
            for n in range(4):
                if n == 3:
                    free(n)
                a_tile(n, 0, n // 2, n % 2)
            for part in range(3):
                free(4 + part)
                v_tile(4 + part, 0, part)
            pe.wait_ge(moved_b[0], 64)
            for i in range(KB):
                if i < 2:
                    for hh in range(2):
                        mm = pe.matmul(scoreB[i % 2][:, hh, :], q_of(0)[:, P * i:P * i + P],
                                       k_of(0)[:, HALF * hh:HALF * hh + HALF], start=True, stop=True)
                    mm.then_inc(b_ready, 1)
                else:
                    b_tile(q_of(0), k_of(0), i, i)
            pe.wait_ge(mz_ready, 2)
            for hh in range(2):
                free(7 + hh)
                m_tile(7 + hh, 0, hh)
            pe.wait_ge(rot_done, PRO)
            pe.sem_inc(pv_done, NP)

            def pv(j, i, u):
                b, odd = j // 2, j % 2
                if i == 0:
                    pe.wait_ge(o_copied, u + 1)
                for lo in range(2):
                    half = lo if odd == 0 else 1 - lo
                    mm = pe.matmul(psO[D1 * lo:D1 * lo + D1, :], V1[:, b, i, D1 * odd:D1 * odd + D1],
                                   prob(i)[:, HALF * half:HALF * half + HALF], start=(i == 0), stop=(i == KB - 1))
                mm.then_inc(pv_done, 1)

            def den(k, j, u):
                pe.wait_ge(psum_step, NP + 7 * (u + 1))
                for lo in range(2):
                    half = lo if j % 2 == 0 else 1 - lo
                    mm = pe.matmul(rotT[k % NROT][D1 * lo:D1 * lo + D1, :], ones[:, :],
                                   psum_of(j)[:, HALF * half:HALF * half + HALF], start=True, stop=True)
                mm.then_inc(rot_ready, 1)

            def body1(p, var):
                for j in range(4):
                    u = 4 * p + j
                    q, k_, q2, k2 = q_of(j), k_of(j), q2_of(j), k2_of(j)
                    nb = 0
                    for i in range(KB):
                        if not (var == LAST and j == 3):
                            for _x in range(BSLOT[i]):
                                if nb == 0:
                                    pe.wait_ge(moved_b[(j + 1) % 2], 64 * (2 * p + (j + 1) // 2 + 1))
                                b_tile(q_of(j + 1), k_of(j + 1), nb, KB * (u + 1) + nb)
                                nb += 1
                        for tile in (t for t in unit_tiles(j, var) if t[0] == i):
                            _, kind, x, owner = tile
                            k = tile_no[var][key_of(tile)]
                            if kind == "M" and x == 0:
                                pv_wait(j, i - 1, p, var)
                                pv(j, i - 1, u)
                                pe.wait_ge(mz_ready, u + 3)
                            free(number(var, p, key_of(tile)))
                            if kind == "C":
                                if i == 0 and x == 0:
                                    pe.wait_ge(moved_c[j % 2], 32 * (2 * p + j // 2 + 1))
                                    pe.wait_ge(rot_done, number(var, p, (0, "A", 0, 0)) if j == 0 else
                                               number(var, p, (j - 1, "M", 1, 0)) + 1)
                                cols = slice(HALF * x, HALF * x + HALF)
                                pe.matmul(rotT[k % NROT], k_[:, P * i:P * i + P], q[:, cols], start=True, stop=False)
                                pe.matmul(rotT[k % NROT], k2[0:KC, P * i:P * i + P], q2[0:KC, cols], start=False, stop=True)\
                                    .then_inc(rot_ready, 1)
                            elif kind == "M":
                                m_tile(k, j + 1, x)
                            elif kind == "D":
                                den(k, owner % 4, 4 * p + owner)
                            elif kind == "V":
                                v_tile(k, 1 if j == 0 else 0, x)
                            elif kind == "A":
                                if x == 0 and j == 2:
                                    pe.wait_ge(wl_done, p + 2)
                                a_tile(k, 1 if j < 2 else 0, j % 2, x)
                        if 0 < i < KB - 1 or i == KB - 1 and var == LAST and j == 3:
                            pv_wait(j, i - 1, p, var)
                            pv(j, i - 1, u)
                        elif i == 0 and not (var == FIRST and j == 0):
                            pv_wait(j - 1, KB - 1, p, var)
                            pv((j - 1) % 4, KB - 1, u - 1)

            def pv_wait(j, i, p, var):
                pe.wait_ge(rot_done, number(var, p, (j, "C", 1, i)) + 1)
            body1(0, FIRST)
            with pe.Fori(1, PAIRS - 1) as p:
                body1(p, MID)
            body1(PAIRS - 1, LAST)
            pv_wait(3, KB - 1, PAIRS - 1, LAST)
            pv(3, KB - 1, 4 * PAIRS - 1)
            k = tile_no[LAST][(3, "D", 0, 0)]
            free(k)
            den(k, 3, 4 * PAIRS - 1)
            pe.wait_ge(rowmax, KB * 2 * H)
            for t in range(TB):
                b, half, blk = t // KB, t % KB // 4, t % 4
                if t % KB == 0:
                    pe.wait_ge(ot_done, 2 + 2 * (2 * H - 2 + 2 * b))
                if t >= 4:
                    pe.wait_ge(proj_used, t - 3)
                for p in range(PAIRS):
                    mm = pe.matmul(PS[:, t % 4, 0:C], OT[:, b, p, half, P * blk:P * blk + P], WP1[:, half, p, :],
                                   start=(p == 0), stop=(p == PAIRS - 1))
                mm.then_inc(proj_ready, 1)
            pe.wait_ge(rot_done, R1)
            pe.wait_ge(o_copied, 1 + 2 * H)
            for g in range(4):
                transpose(1, g)
            pe.wait_ge(xt_low, 8)
            pe.wait_ge(xc_low, 8)
            CH2 = [(XAh, W2h, 0), (XAl, W2h, 0), (XAh, W2l[0], 0), (XC, W2h, 3 * C), (XC, W2l[1], 0)]
            pe.wait_ge(wl_done, PAIRS + 2)
            for n in range(16):
                m, b = M2[n // 2]
                if n >= 4:
                    pe.wait_ge(q2_low, n - 3)
                for c, (x, w, o) in enumerate(CH2):
                    mm = pe.matmul(PS[0:MROW, n % 4, :], w[:, o + MROW * m:o + MROW * m + MROW],
                                   x[:, S * b + HALF * (n % 2):S * b + HALF * (n % 2) + HALF], start=(c == 0), stop=(c == 4))
                mm.then_inc(q2_ready, 1)
            for t in range(TB):
                if t >= 4:
                    pe.wait_ge(q2_high, 16 + t - 3)
                for c, (x, w, o) in enumerate(CH2):
                    mm = pe.matmul(PS[:, 4 + t % 4, 0:C], x[:, P * t:P * t + P], w[:, o + 2 * C:o + 3 * C],
                                   start=(c == 0), stop=(c == 4))
                mm.then_inc(q2_ready, 1)
            UB = 2 * H
            pe.wait_ge(consts, 8 + 9 + 1)
            pe.wait_ge(q2_low, 16)
            for n in range(AHEAD):
                if n % KB == 0:
                    pe.wait_ge(loaded3[n // KB], LOADS3)
                b_tile(q3_of(n // KB), k3_of(n // KB), n % KB, KB * UB + n)
            pe.wait_ge(mz_ready, UB + 2)
            pe.wait_ge(q2_high, 16 + TB)
            for hh in range(2):
                m_tile(hh, 0, hh)
            pe.wait_ge(rot_done, R1 + PRO2)

            def pv2(j, i, u):
                if i == 0:
                    pe.wait_ge(o2_copied, u + 1)
                    pe.wait_ge(v2s_ready, u + 1)
                for g in range(4):
                    mm = pe.matmul(psO[32 * g:32 * g + V2W, 0:256], V2S[:, j % 3, i, :], prob(i)[:, 256 * g:256 * g + 256],
                                   start=(i == 0), stop=(i == KB - 1))
                mm.then_inc(pv_done, 1)

            def body2(it, last):
                base = R1 + it * 6 * ROT2
                for j in range(6):
                    u = 6 * it + j
                    k = ROT2 * j + PRO2
                    for i in range(KB):
                        w = KB * j + i + AHEAD
                        if not (last and w >= 6 * KB):
                            un = w // KB
                            if w % KB == 0:
                                pe.wait_ge(loaded3[un % 3], it * 2 * LOADS3 + LOADS3 * (un // 3 + 1))
                            b_tile(q3_of(un), k3_of(un), w % KB, it * 6 * KB + KB * UB + w)
                        if i == 7 and not (last and j == 5):
                            pe.wait_ge(mz_ready, UB + u + 3)
                            for hh in range(2):
                                pe.wait_ge(rot_done, base + k - NROT + 1)
                                m_tile(k, j + 1, hh)
                                k += 1
                        for hh in range(2):
                            pe.wait_ge(rot_done, base + k - NROT + 1)
                            mm = pe.matmul(rotT[k % NROT], k3_of(j)[0:KC, P * i:P * i + P],
                                           q3_of(j)[0:KC, HALF * hh:HALF * hh + HALF], start=True, stop=True)
                            mm.then_inc(rot_ready, 1)
                            if hh == 1:
                                kk[i % 2] = k
                            k += 1
                        if i > 0:
                            pe.wait_ge(rot_done, base + kk[(i - 1) % 2] + 1)
                            pv2(j, i - 1, u)
                        elif j > 0:
                            pe.wait_ge(rot_done, base + kk[1] + 1)
                            pv2(j - 1, KB - 1, u - 1)
                pe.wait_ge(rot_done, base + kk[1] + 1)
                pv2(5, KB - 1, 6 * it + 5)
            kk = [0, 0]
            with pe.Fori(0, H // 3 - 1) as it:
                body2(it, False)
            body2(H // 3 - 1, True)
            pe.wait_ge(rowmax, KB * 2 * UB)
            pe.wait_ge(o2_copied, 2 * H + 1)
            pe.wait_ge(ot_done, 2 + 2 * UB + 2)

            def proj2(t, g):
                b, blk = t // KB, t % KB
                return pe.matmul(PS[:, t % 4, 0:C], O2[:, g, b, P * blk:P * blk + P], WP2[:, b, g, :],
                                 start=(g == 0), stop=(g == 1))
            for t in range(4):
                proj2(t, 0)
            pe.wait_ge(ot_done, 2 + 2 * UB + 4)
            for t in range(TB):
                if t >= 4:
                    pe.wait_ge(proj_used, TB + t - 3)
                    proj2(t, 0)
                proj2(t, 1).then_inc(proj_ready, 1)
            for g in range(4):
                transpose(2, g)
            pe.wait_ge(xt_low, 12)
            pe.wait_ge(xc_low, 12)
            Mh, Ml = QK[:, 0:2 * F], QK[:, 2 * F:4 * F]
            Zh, Zl = QK[0:MROW, 4 * F:5 * F], QK[0:MROW, 5 * F:6 * F]
            FULL = [(XAh, Mh, 0), (XAl, Mh, 0), (XAh, Ml, 0), (XC, Mh, F), (XC, Ml, F)]
            HALFW = [(XAh[0:MROW], Mh[0:MROW], 0), (XAl[0:MROW], Mh[0:MROW], 0), (XAh[0:MROW], Ml[0:MROW], 0)]
            THIRD = [(XAh[0:MROW], Zh, 0), (XAl[0:MROW], Zh, 0), (XAh[0:MROW], Zl, 0)]
            pe.wait_ge(wfc2_loaded, 16)
            nh = 0
            for g in range(4):
                evals = [0] if g < 2 else [0, 1, 2]
                for e in evals:
                    chunks = (FULL, HALFW, THIRD)[e]
                    for m in range(FB):
                        if nh >= 4:
                            pe.wait_ge(fc1_used, nh - 3)
                        for c, (x, w, o) in enumerate(chunks):
                            mm = pe.matmul(PS[:, nh % 4, :], w[:, o + P * m:o + P * m + P], x[:, HALF * g:HALF * g + HALF],
                                           start=(c == 0), stop=(c == len(chunks) - 1))
                        mm.then_inc(fc1_ready, 1)
                        nh += 1
                pe.wait_ge(fc1_used, nh)
                if g == 2:
                    pe.wait_ge(pool_step, 5 + 3)
                for tb in range(4):
                    t = 4 * g + tb
                    if t >= 4:
                        pe.wait_ge(fc2_used, t - 3)
                    for e in evals:
                        w = WF2[:, 0 if g < 2 else e + 1]
                        for m in range(FB):
                            mm = pe.matmul(PS[:, 4 + tb, 0:KEEP[e]], HB[:, e, m, P * tb:P * tb + P],
                                           w[:, C * m:C * m + KEEP[e]], start=(e == 0 and m == 0),
                                           stop=(e == evals[-1] and m == FB - 1), skip_group_check=True)
                    mm.then_inc(fc2_ready, 1)
            barrier(pe, "pe")




def kernel(**inputs):
    import numpy as np
    import concourse.bacc as bacc
    from concourse.bass_utils import run_bass_kernel_spmd

    x = {k: np.ascontiguousarray(v) for k, v in inputs.items()}
    f32 = np.float32
    arrays = {}
    ids = np.full((B, S + 6), -1, np.int32)
    ids[:, 3:3 + S] = x["x"]
    win = np.full((CONV_ROWS, B, S), -1, np.int32)
    convw = np.zeros((CONV_ROWS, C), f32)
    vocab = np.full((P, 1), -2, f32)
    for at in (0, 64):
        for tap in range(7):
            for v in range(5):
                r = at + 5 * tap + v
                win[r] = ids[:, tap:tap + S]
                vocab[r] = v
                for c, (name, k) in enumerate((("L0_tok_W3", 3), ("L0_tok_W5", 5), ("L0_tok_W7", 7))):
                    t = tap - 3 + k // 2
                    if 0 <= t < k:
                        convw[r, 64 * c:64 * c + 64] = x[name][:, v, t]
    arrays["windows"] = win.reshape(CONV_ROWS, N)
    arrays["convw"] = convw
    arrays["vocab"] = vocab
    arrays["mask"] = x["mask_BS_f1_0"].reshape(TB, P).T
    arrays["ident"] = np.eye(P, dtype=f32)

    def by_chunk(v):
        return np.stack([v[0:P], np.concatenate([v[P:C], v[P:C]])], 1)

    g = np.zeros((P, 3, B, 2, 2), f32)
    g[:, 0, :, :, 0] = 1.0
    for s_, n_ in ((1, "n1"), (2, "n2")):
        for b, z in enumerate("ls"):
            for k, gb in enumerate("gb"):
                g[:, s_, b, :, k] = by_chunk(x[f"L0_ffn_{n_}{z}_{gb}"])
    arrays["gcols"] = g.reshape(P, -1)
    w, wb = x["L0_attn_qkv_w"], x["L0_attn_qkv_b"]
    HD = H * D1
    w1 = np.zeros((PAIRS, P, 2, 3, P), f32)
    qkb = np.zeros((PAIRS, P, 2), f32)
    for h in range(H):
        r = slice(D1 * h, D1 * h + D1)
        both = np.concatenate([w[0:HD][r], w[HD:2 * HD][r]]).T
        w1[h // 2, :, :, h % 2, :] = np.stack([both[0:P], np.concatenate([both[P:C], both[P:C]])], 1)
        qkb[h // 2, :, h % 2] = np.concatenate([wb[0:HD][r], wb[HD:2 * HD][r]])
    for p in range(PAIRS):
        v = w[2 * HD + P * p:2 * HD + P * p + P].T
        w1[p, :, :, 2, :] = np.stack([v[0:P], np.concatenate([v[P:C], v[P:C]])], 1)
    arrays["w1"] = w1.reshape(PAIRS, P, -1)
    arrays["qkb"] = qkb
    arrays["qks"] = np.repeat(np.array([D1 ** -0.5, 1.0], f32), D1).reshape(P, 1)
    arrays["bvc"] = wb[2 * HD:].reshape(PAIRS, P).T
    wp = x["L0_attn_proj_w"].T.reshape(PAIRS, 2, D1, C)
    arrays["wp1"] = np.stack([wp.reshape(PAIRS, P, C), wp[:, ::-1].reshape(PAIRS, P, C)]).transpose(2, 0, 1, 3).reshape(P, -1)
    arrays["wp2"] = x["L0_ffn_w_proj"].reshape(2, MROW, C).transpose(1, 0, 2).reshape(MROW, -1)
    arrays["gw"] = x["L0_ffn_gumbel_weights"]
    arrays["rows"] = np.stack([x[n] for n in ("L0_tok_ln_gamma", "L0_tok_ln_beta", "L0_attn_proj_b", "L0_ffn_b_proj", "L0_ffn_b_fc2")])
    arrays["w2qkv"] = by_chunk(x["L0_ffn_w_qkv"]).reshape(P, -1)
    arrays["wfc1"] = by_chunk(x["L0_ffn_w_fc1"]).reshape(P, -1)
    arrays["b1c"] = x["L0_ffn_b_fc1"].reshape(FB, P).T
    arrays["wfc2"] = x["L0_ffn_w_fc2"].reshape(FB, P, C).transpose(1, 0, 2).reshape(P, -1)

    nc = bacc.Bacc("TRN2", target_bir_lowering=False, num_devices=1)
    arrays = {f"in_{k}": np.ascontiguousarray(v) for k, v in arrays.items()}
    aps = {k[3:]: nc.dram_tensor(k, v.shape, mybir.dt.from_np(v.dtype), kind="ExternalInput").ap() for k, v in arrays.items()}
    out = nc.dram_tensor("out", (N, C), F32, kind="ExternalOutput").ap()
    tower(nc, aps, out)
    r = run_bass_kernel_spmd(nc, [arrays], core_ids=[0])
    return r.results[0]["out"].reshape(B, S, C)
```

```python
from contextlib import ExitStack

import concourse.bass as bass
from concourse import mybir

F32 = mybir.dt.float32
F32R = mybir.dt.float32r
BF16 = mybir.dt.bfloat16
I32 = mybir.dt.int32
ALU = mybir.AluOpType
ACT = mybir.ActivationFunctionType
AX = mybir.AxisListType

P = 128
B = 2
S = 1024
N = B * S
C = 192
TB = N // P
KB = S // P
HALF = S // 2
H = 12
D1 = 64
D2 = 16
PAIRS = H // 2
MROW = 96
KC = MROW + 2
CONV_ROWS = 99
KEEP = [C, C // 2, C // 3]
HKEEP = [H, H // 2, H // 3]
F = 4 * C
FB = F // P
NROT = 3
NP = 4
CONV_LOADS = 4
LOADS = 10


def tower(nc, a, out):
    with ExitStack() as ctx:
        def sb(name, shape, dt=F32):
            return ctx.enter_context(nc.sbuf_tensor(name, shape, dt))

        def sem(name):
            return ctx.enter_context(nc.semaphore(name))

        PS = ctx.enter_context(nc.psum_tensor("PS", [P, 8, HALF], F32))
        scoreB = [PS[:, 2 * i:2 * i + 2, :] for i in range(2)]
        rotT = [PS[:, 4 + i, :] for i in range(NROT)]
        psO = PS[:, 7, :]

        HT = sb("HT", [P, TB, C])
        XAh = sb("XAh", [P, N], F32R)
        XAl = sb("XAl", [P, N], F32R)
        XC = sb("XC", [P, N], F32R)
        BIG = sb("BIG", [P, 12288])
        QK = sb("QK", [P, 8 * S], F32R)
        PA = sb("PA", [P, 6 * S])
        TQ = sb("TQ", [P, S])
        HH = sb("HH", [P, S], F32R)
        LL = sb("LL", [P, S], F32R)
        V1 = sb("V1", [P, B, KB, P])
        WRAW = sb("WRAW", [P, 2, 2, P])
        WH = sb("WH", [P, 2, 2, P], F32R)
        WL = sb("WL", [P, 2, 2, P], F32R)
        W2LC = sb("W2LC", [P, 3 * C], F32R)
        WP1 = sb("WP1", [P, 2, PAIRS, C])
        WP2 = sb("WP2", [MROW, B, 2, C])
        MZ = sb("MZ", [P, 2, KB, P], BF16)
        MC = sb("MC", [P, 2, KB])
        DEN = sb("DEN", [P, HALF])
        REC = sb("REC", [P, HALF])
        ORAW = sb("ORAW", [P, HALF])
        spread = sb("spread", [4 * H, 2 * 4, MROW])
        identF = sb("identF", [P, P])
        identB = sb("identB", [P, P], BF16)
        ones = sb("ones", [P, D1])
        STAT = sb("STAT", [P, 5, TB, 6])
        MV = sb("MV", [P, 5, TB, 2])
        SD = sb("SD", [P, 5, TB])
        RS = sb("RS", [P, 5, TB])
        NB = sb("NB", [P, 5, TB])
        gcols = sb("gcols", [P, 3, B, 2, 2])
        qkb = sb("qkb", [P, 2])
        qkbs = sb("qkbs", [P, 2])
        qks = sb("qks", [P, 1])
        bvc = sb("bvc", [P, PAIRS])
        maskc = sb("maskc", [P, TB])
        vocab = sb("vocab", [P, 1])
        gw = sb("gw", [P, 3])
        b1c = sb("b1c", [P, FB])
        rows = sb("rows", [P, 5, C])
        bias1 = sb("bias1", [P, C])
        bias2 = sb("bias2", [P, B, C])
        biasM = sb("biasM", [P, B, C])

        def q_of(u):
            return QK[:, (u % 2) * S:(u % 2 + 1) * S]

        def k_of(u):
            return QK[:, (2 + u % 2) * S:(3 + u % 2) * S]

        def q2_of(u):
            return QK[:, (4 + u % 2) * S:(5 + u % 2) * S]

        def k2_of(u):
            return QK[:, (6 + u % 2) * S:(7 + u % 2) * S]

        def q3_of(u):
            return QK[:, (u % 3) * S:(u % 3 + 1) * S]

        def k3_of(u):
            return QK[:, (3 + u % 3) * S:(4 + u % 3) * S]

        def prob(i):
            return PA[:, (i % NP) * S:(i % NP + 1) * S]

        def psum_of(u):
            return PA[:, (NP + u % 2) * S:(NP + 1 + u % 2) * S]

        OT = BIG[:, :].rearrange("p (b h x n) -> p b h x n", b=B, h=PAIRS, x=2)
        Y = BIG[:, 0:TB * C].rearrange("p (t c) -> p t c", t=TB)
        NT = [BIG[:, o:o + TB * 2 * P].rearrange("p (t c) -> p t c", t=TB) for o in (TB * C, TB * C, 7168)]
        V2W = D2 + 1
        V2 = BIG[:, 6144:6144 + B * KB * H * V2W].rearrange("p (b t h d) -> p b t h d", b=B, t=KB, h=H)
        O2S = [BIG[:, 9600 + 256 * i:9856 + 256 * i] for i in range(2)]
        HB = BIG[:, 3072:3072 + 3 * FB * HALF].rearrange("p (e m n) -> p e m n", e=3, m=FB)
        V2S = V1[:, 0, :, :].rearrange("p a b -> p (a b)")[:, 0:3 * KB * V2W].rearrange("p (u t d) -> p u t d", u=3, t=KB)
        O2U = [x[0:MROW, :].bitcast(F32).rearrange("p (g n) -> p g n", g=2) for x in (XAh, XAl)]
        R2 = XC[0:MROW, :].bitcast(F32).rearrange("p (b n) -> p b n", b=B)
        O2 = BIG[0:MROW, 3072:3072 + 4 * S].rearrange("p (g b n) -> p g b n", g=2, b=B)
        QB = 2 * H * 2
        D2T = [BIG[0:QB, 10240 + 256 * g:10496 + 256 * g] for g in range(2)]
        R2T = [BIG[0:QB, 10752 + 256 * g:11008 + 256 * g] for g in range(2)]
        W2R = BIG[:, 9408:9408 + 6 * C]
        W2h = QK[:, 6 * S:6 * S + 6 * C]
        W2l = [QK[:, 6 * S + 6 * C:6 * S + 9 * C], W2LC[:, :]]
        HS = [HH[:, :]] + [PA[:, i * S:(i + 1) * S].bitcast(F32R) for i in (0, 2, 4)]
        LS = [LL[:, :]] + [PA[:, i * S:(i + 1) * S].bitcast(F32R) for i in (1, 3, 5)]
        M2 = [(m, b) for m in (0, 2, 1, 3) for b in range(B)]
        VC = H * D1
        WVR = BIG[:, 7168:7168 + 2 * VC]
        WVH = [QK[:, at:at + VC] for at in (S, 5 * S)]
        WVL = [QK[:, at:at + VC] for at in (3 * S, 7 * S)]
        VS = [BIG[:, 8704 + VC * i:8704 + VC * (i + 1)] for i in range(4)]
        WF1 = PA[:, 4 * S:4 * S + 2 * F]
        WF2 = PA[:, 0:4 * FB * C].rearrange("p (e c) -> p e c", e=4)

        def xs(stage, g, c):
            at = PA[:, 4 * S:6 * S] if stage == 0 else V1[:, :, :, :].rearrange("p b t d -> p (b t d)")
            return at[:, (2 * (g % 2) + c) * HALF:(2 * (g % 2) + c + 1) * HALF]

        def xbank(stage, g, c):
            return PS[:, (4 if stage else 0) + 2 * (g % 2) + c, :]

        VD = nc.dram_tensor("VD", [PAIRS, B, P, KB, P], F32, kind="Internal").ap()
        QD = nc.dram_tensor("QD", [B, H, 2 * D2, S], F32, kind="Internal").ap()
        KD = nc.dram_tensor("KD", [B, H, 2 * D2, S], F32, kind="Internal").ap()
        OD = nc.dram_tensor("OD", [B, H, V2W, S], F32, kind="Internal").ap()
        RD = nc.dram_tensor("RD", [2, B, H // 2, S], F32, kind="Internal").ap()

        phase_done = sem("phase_done")
        conv_loads = sem("conv_loads")
        loads = sem("loads")
        dve_step = sem("dve_step")
        pool_step = sem("pool_step")
        consts = sem("consts")
        conv_in = sem("conv_in")
        conv_out = sem("conv_out")
        h0_ready = sem("h0_ready")
        bias_ready = sem("bias_ready")
        rs_ready = sem("rs_ready")
        norm_act = sem("norm_act")
        norm_dve = sem("norm_dve")
        xc_low = sem("xc_low")
        twice_done = sem("twice_done")
        ht_ready = sem("ht_ready")
        var_ready = sem("var_ready")
        std_ready = sem("std_ready")
        tr_done = sem("tr_done")
        xt_high = sem("xt_high")
        xt_t = sem("xt_t")
        xt_t2 = sem("xt_t2")
        xt_low = sem("xt_low")
        wv_in = sem("wv_in")
        wv_ready = sem("wv_ready")
        v_ready = sem("v_ready")
        v_copied = sem("v_copied")
        v_stored = [sem(f"v_stored{i}") for i in range(4)]
        v1_in = [sem(f"v1_in{b}") for b in range(B)]
        raw1 = sem("raw1")
        wh_done = sem("wh_done")
        wl_done = sem("wl_done")
        b_ready = sem("b_ready")
        rowmax = sem("rowmax")
        mz_hi = sem("mz_hi")
        mz_ready = sem("mz_ready")
        rot_ready = sem("rot_ready")
        rot_done = sem("rot_done")
        pv_done = sem("pv_done")
        psum_step = sem("psum_step")
        o_copied = sem("o_copied")
        rec_done = sem("rec_done")
        ot_done = sem("ot_done")
        hh_done = sem("hh_done")
        ll_done = sem("ll_done")
        moved_b = [sem(f"moved_b{i}") for i in range(2)]
        moved_c = [sem(f"moved_c{i}") for i in range(2)]
        proj_ready = sem("proj_ready")
        proj_used = sem("proj_used")
        w_loaded = sem("w_loaded")
        wfc2_loaded = sem("wfc2_loaded")
        q2_ready = sem("q2_ready")
        q2_high = sem("q2_high")
        q2_low = sem("q2_low")
        q2_stored = [sem(f"q2_stored{i}") for i in range(4)]
        loaded3 = [sem(f"loaded{i}") for i in range(3)]
        v2s_ready = sem("v2s_ready")
        sums_in = sem("sums_in")
        sums_out = sem("sums_out")
        o2_copied = sem("o2_copied")
        o2_stored = [sem(f"o2_stored{i}") for i in range(2)]
        o2_in = sem("o2_in")
        r2_in = sem("r2_in")
        r2_spread = sem("r2_spread")
        fc1_ready = sem("fc1_ready")
        fc1_used = sem("fc1_used")
        fc2_ready = sem("fc2_ready")
        fc2_used = sem("fc2_used")
        stored = sem("stored")

        def finish(eng):
            eng.drain().then_inc(phase_done, 1)
            eng.wait_ge(phase_done, 5)

        block = ctx.enter_context(nc.Block())

        LN = [(HT, HT, 1e-12), (HT, NT[0], 1e-5), (HT, Y, 1e-5), (Y, NT[1], 1e-5), (Y, NT[2], 1e-5)]
        DOUBLE = [(0, 0), (0, 1), (1, 0), (0, 2), (1, 1), (0, 3), (1, 2), (1, 3)]
        ITEMS = [[(j, g) for j, g in DOUBLE], [(2 + j, g) for j, g in DOUBLE], [(4, g) for g in range(4)]]
        ITEM0 = [0, 8, 16]
        ITEM0X = [0, 4, 8]
        TAKE = [{4: [0], 6: [1], 7: [2, 3]}, {4: [0], 6: [1], 7: [2, 3]}, {1: [0], 2: [1], 3: [2, 3]}]

        def wait_normed(eng, stage, j, g):
            done = [i for st in ITEMS[:stage] for i in st] + ITEMS[stage][:ITEMS[stage].index((j, g)) + 1]
            of_token = sum(i[0] == 0 for i in done)
            eng.wait_ge(norm_dve, 4 * of_token + 2 * (len(done) - of_token))
            if j > 0:
                eng.wait_ge(norm_act, 2 * (len(done) - of_token))

        BSLOT = [0, 0, 1, 2, 1, 2, 2, 0]
        PRO = 6
        FIRST, MID, LAST = range(3)

        def unit_tiles(j, var):
            t = []
            for i in range(KB):
                if i == 1 and not (var == FIRST and j == 0):
                    t += [(i, "D", 0, j - 1)]
                if i in (0, 1) and not (var == LAST and j >= 2):
                    t += [(i, "A", i, j)]
                t += [(i, "C", x, j) for x in range(2)]
                if i == 7 and not (var == LAST and j == 3):
                    t += [(i, "M", x, j) for x in range(2)]
            if var == LAST and j == 3:
                t += [(KB, "D", 0, j)]
            return t

        def key_of(tile):
            slot, kind, x, owner = tile
            return owner, kind, x, slot if kind == "C" else 0

        BODY = sum(len(unit_tiles(j, MID)) for j in range(4))
        BODY0 = sum(len(unit_tiles(j, FIRST)) for j in range(4))
        START = [PRO, PRO + BODY0 - BODY, PRO + BODY0 + (PAIRS - 2) * BODY]
        tile_no = [{key_of(t): START[var] + n for n, t in enumerate(t for j in range(4) for t in unit_tiles(j, var))}
                   for var in (FIRST, MID, LAST)]
        R1 = START[LAST] + len(tile_no[LAST])

        def number(var, p, key):
            if key[0] == -1 and key[1] == "C":
                n = START[var] - 3
            else:
                n = tile_no[var][key]
            return n + p * BODY if var == MID else n

        PV1 = NP + KB * 2 * H
        assert BODY % NROT == 0

        PRO2, ROT2 = 2, 2 * KB + 2
        LOADS3 = 16 * 3
        AHEAD = 11

        @block.sync
        def _(sp):
            for dst, src in [(PA[0:CONV_ROWS, 0:N].bitcast(I32), a["windows"]), (PA[0:CONV_ROWS, N:N + C], a["convw"]),
                             (vocab[:, :], a["vocab"]), (maskc[:, :], a["mask"])]:
                sp.dma_start(dst, src).then_inc(conv_loads, 16)
            sp.dma_start(WVR, a["wv"]).then_inc(wv_in, 16)
            for dst, src in [(identF[:, :], a["ident"]),
                             (spread[:, :, :].rearrange("p a b -> p (a b)"), a["spread"]),
                             (gcols[:, :, :, :, :].rearrange("p a b c d -> p (a b c d)"), a["gcols"]),
                             (qks[:, :], a["qks"]), (bvc[:, :], a["bvc"]), (b1c[:, :], a["b1c"]),
                             (WP1[:, :, :, :].rearrange("p a b c -> p (a b c)"), a["wp1"]),
                             (WP2[:, 0, :, :].rearrange("p b c -> p (b c)"), a["wp2"]),
                             (gw[:, :], a["gw"].partition_broadcast(P)),
                             (rows[:, :, :], a["rows"].partition_broadcast(P))]:
                sp.dma_start(dst, src).then_inc(loads, 16)
            sp.dma_start(WRAW[:, :, :, :].rearrange("p a b c -> p (a b c)"), a["w1"][0]).then_inc(raw1, 16)
            sp.dma_start(qkb[:, :], a["qkb"][0]).then_inc(raw1, 16)

            def load_v(b, p):
                sp.dma_start(V1[:, b, :, :], VD[p, b]).then_inc(v1_in[b], 16)

            def move(k, nth):
                sp.wait_ge(ll_done, nth)
                mb, mc = moved_b[k % 2], moved_c[k % 2]
                for dst, src, sem_ in [(q_of(k)[0:D1], HH[0:D1], mb), (q_of(k)[D1:P], LL[0:D1], mb),
                                       (k_of(k)[0:D1], HH[D1:P], mb), (k_of(k)[D1:P], HH[D1:P], mb),
                                       (q2_of(k)[0:D1], HH[0:D1], mc), (k2_of(k)[0:D1], LL[D1:P], mc)]:
                    sp.dma_start(dst.bitcast(F32), src.bitcast(F32)).then_inc(sem_, 16)

            move(0, 1)
            for i in range(4):
                sp.wait_ge(v_stored[i], 32)
            load_v(0, 0)
            sp.wait_ge(v_ready, 2 * TB)
            move(1, 2)
            for i in range(4):
                sp.wait_ge(v_stored[i], 64)

            def body1(p, var):
                if var != LAST:
                    nth = next_pair = sp.snap(p + 1) if var == MID else p + 1
                    sp.wait_ge(wl_done, nth)
                    sp.dma_start(WRAW[:, :, :, :].rearrange("p a b c -> p (a b c)"), a["w1"][nth]).then_inc(raw1, 16)
                    sp.dma_start(qkb[:, :], a["qkb"][nth]).then_inc(raw1, 16)
                for j in range(4):
                    if var == LAST and j >= 2:
                        break
                    keys_used, nth = number(var, p, (j, "C", 1, 7)) + 1, 4 * p + j + 3
                    if var == MID:
                        keys_used, nth = sp.to_reg(keys_used), sp.to_reg(nth)
                    sp.wait_ge(rot_ready, keys_used)
                    move(j, nth)
                    if j == 0:
                        load_v(1, p)
                    elif j == 2:
                        load_v(0, next_pair)
            body1(0, FIRST)
            with sp.Fori(1, PAIRS - 1) as p:
                body1(p, MID)
            body1(PAIRS - 1, LAST)
            sp.wait_ge(proj_ready, 1 + TB)
            sp.dma_start(W2R, a["w2qkv"]).then_inc(w_loaded, 16)

            def load3(b, h, k):
                sp.dma_start(q3_of(k)[0:4 * D2].bitcast(F32), QD[b, h].unsqueeze(0).broadcast_to([2, 2 * D2, S]))\
                    .then_inc(loaded3[k % 3], 16)
                for part in range(2):
                    sp.dma_start(k3_of(k)[2 * D2 * part:2 * D2 * part + 2 * D2].bitcast(F32),
                                 KD[b, h, D2 * part:D2 * part + D2].unsqueeze(0).broadcast_to([2, D2, S]))\
                        .then_inc(loaded3[k % 3], 16)

            for n, (m, b) in enumerate(M2):
                sp.wait_ge(q2_high, 2 * n + 2)
                sp.wait_ge(q2_low, 2 * n + 2)
                dst = (QD if m < 2 else KD)[b, 6 * (m % 2):6 * (m % 2) + 6]
                sp.dma_start(dst[:, 0:D2, :], HS[n % 4][0:MROW].bitcast(F32)).then_inc(q2_stored[n % 4], 16)
                sp.dma_start(dst[:, D2:2 * D2, :], LS[n % 4][0:MROW].bitcast(F32)).then_inc(q2_stored[n % 4], 16)
                if n == 3:
                    for i in range(4):
                        sp.wait_ge(q2_stored[i], 32)
                    for u in range(3):
                        load3(u % 2, u // 2, u)
            for i in range(4):
                sp.wait_ge(q2_stored[i], 64)

            def store2(nth, j, b, h):
                sp.wait_ge(o2_copied, nth)
                for g in range(4):
                    sp.dma_start(OD[b, h, :, 256 * g:256 * g + 256], O2S[j % 2][32 * g:32 * g + V2W, :])\
                        .then_inc(o2_stored[j % 2], 16)

            def gather(g, h0, h1):
                for b in range(B):
                    sp.dma_start(O2U[b][D2 * h0:D2 * h1, g, :], OD[b, 6 * g + h0:6 * g + h1, 0:D2, :]).then_inc(o2_in, 16)

            def sums(g):
                for q in range(4):
                    sp.dma_start(D2T[g][H * q:H * q + H, :],
                                 OD[:, 6 * g:6 * g + 6, D2, 256 * q:256 * q + 256]).then_inc(sums_in, 16)

            def reciprocals_out(g):
                sp.wait_ge(rec_done, 8 + 4 * 2 * H + g + 1)
                for q in range(4):
                    sp.dma_start(RD[g, :, :, 256 * q:256 * q + 256], R2T[g][H * q:H * q + H, :]).then_inc(sums_out, 16)

            def reciprocals_in(g):
                sp.wait_ge(sums_out, 64 * g + 64)
                for b in range(B):
                    sp.dma_start(R2[:, b, :], RD[g, b].unsqueeze(1).broadcast_to([H // 2, D2, S])).then_inc(r2_in, 16)

            def body2(it, last):
                def reg(value):
                    return value if last else sp.snap(value)

                if last:
                    sp.dma_start(WF1, a["wfc1"]).then_inc(w_loaded, 16)
                    for i in range(2):
                        sp.wait_ge(o2_stored[i], 64 + 64 * 9)
                    gather(0, 0, 6)
                    gather(1, 0, 3)
                    sums(0)
                for j in range(7):
                    if last and j == 3:
                        reciprocals_out(0)
                    if last and j == 5:
                        reciprocals_in(0)
                    if j > 0:
                        store2(reg(6 * it + j + 1), j - 1, (j - 1) % 2, reg(3 * it + (j - 1) // 2))
                    if j < 6 and not (last and j >= 3):
                        keys_used = reg(R1 + it * 6 * ROT2 + PRO2 + ROT2 * (j + 1))
                        h = reg(3 * it + (j + 3) // 2)
                        sp.wait_ge(rot_ready, keys_used)
                        load3((j + 3) % 2, h, j)
            with sp.Fori(0, H // 3 - 1) as it:
                body2(it, False)
            body2(H // 3 - 1, True)
            for i in range(2):
                sp.wait_ge(o2_stored[i], 64 * (H + 1))
            gather(1, 3, 6)
            sums(1)
            sp.dma_start(WF2[:, 0], a["wfc2"]).then_inc(wfc2_loaded, 16)
            for t in range(TB):
                sp.wait_ge(fc2_used, t + 1)
                sp.dma_start(out[P * t:P * t + P, :], HT[:, t, :]).then_inc(stored, 16)
            sp.wait_ge(stored, 16 * TB)
            finish(sp)

        @block.gpsimd
        def _(pool):
            nc.gpsimd.memset(ones[:, :], 1.0).then_inc(consts, 1)
            nc.gpsimd.memset(MZ[:, :, :, :], 0.0).then_inc(consts, 1)
            pool.wait_ge(loads, 16 * LOADS)
            nc.gpsimd.tensor_scalar(WP2[:, 1, :, :], WP2[:, 0, :, :], gw[0:MROW, 0:1], None, ALU.mult).then_inc(pool_step, 1)
            nc.gpsimd.tensor_scalar(bias2[:, 1, :], rows[:, 3, :], gw[:, 0:1], None, ALU.mult).then_inc(pool_step, 1)
            nc.gpsimd.tensor_scalar(biasM[:, 1, :], rows[:, 4, :], gw[:, 0:1], None, ALU.mult).then_inc(pool_step, 1)
            nc.gpsimd.tensor_copy(bias2[:, 0, :], rows[:, 3, :]).then_inc(pool_step, 1)
            nc.gpsimd.tensor_copy(biasM[:, 0, :], rows[:, 4, :]).then_inc(pool_step, 1)
            pool.wait_ge(pool_step, 5)
            def blank(i):
                nc.gpsimd.memset(q2_of(i)[D1:P].bitcast(F32), 0.0).then_inc(consts, 1)
                nc.gpsimd.memset(k2_of(i)[D1:P].bitcast(F32), 0.0).then_inc(consts, 1)
                pool.wait_ge(consts, 3 * i + 4)
                nc.gpsimd.memset(k2_of(i)[MROW:MROW + 2].bitcast(F32), 1.0).then_inc(consts, 1)
            blank(0)
            pool.wait_ge(consts, 5)

            def twice(stage, j, g):
                wait_normed(pool, stage, j, g)
                blocks = NT[stage][:, 4 * g:4 * g + 4, :]
                nc.gpsimd.tensor_copy(blocks[:, :, C:2 * P], blocks[:, :, P:C]).then_inc(twice_done, 1)

            def chunk_low(stage, g):
                n = ITEM0X[stage] + g + 1
                cols = slice(HALF * g, HALF * g + HALF)
                pool.wait_ge(xt_high, 2 * n)
                nc.gpsimd.tensor_tensor(XC[64:P, cols], xs(stage, g, 1)[64:P], XC[64:P, cols].bitcast(F32), ALU.subtract)\
                    .then_inc(xc_low, 1)
                pool.wait_ge(xc_low, n)

            def x_work(stage, j):
                for g in range(4):
                    twice(stage, j, g)
                    pool.wait_ge(twice_done, 4 * stage + g + 1)
                    if g:
                        chunk_low(stage, g - 1)
                chunk_low(stage, 3)
            x_work(0, 1)
            pool.wait_ge(bias_ready, 1)
            nc.gpsimd.tensor_tensor(HT[:, :, :], HT[:, :, :], bias1[:, :].unsqueeze(1).broadcast_to([P, TB, C]), ALU.add)\
                .then_inc(ht_ready, 1)
            pool.wait_ge(v_ready, 2 * TB)
            pool.wait_ge(ht_ready, 1)
            blank(1)
            pool.wait_ge(consts, 8)
            pool.sem_inc(psum_step, NP)

            def body1(p, var):
                for j in range(4):
                    u = 4 * p + j
                    for i in range(1, KB):
                        pool.wait_ge(rot_done, number(var, p, (j, "C", 1, i)) + 1)
                        if i == 1:
                            pool.wait_ge(rec_done, 4 * u + 4)
                            nc.gpsimd.tensor_tensor(psum_of(j), prob(0), prob(1), ALU.add).then_inc(psum_step, 1)
                        else:
                            pool.wait_ge(psum_step, NP + 7 * u + i - 1)
                            nc.gpsimd.tensor_tensor(psum_of(j), prob(i), psum_of(j), ALU.add).then_inc(psum_step, 1)
            body1(0, FIRST)
            with pool.Fori(1, PAIRS - 1) as p:
                body1(p, MID)
            body1(PAIRS - 1, LAST)
            wait_normed(pool, 1, 2, 0)
            pool.wait_ge(psum_step, NP + 7 * 2 * H)
            for i in range(3):
                nc.gpsimd.memset(q3_of(i)[D1:P].bitcast(F32), 0.0).then_inc(consts, 1)
                nc.gpsimd.memset(k3_of(i)[D1:P].bitcast(F32), 0.0).then_inc(consts, 1)
            pool.wait_ge(consts, 8 + 6)
            for i in range(3):
                nc.gpsimd.memset(k3_of(i)[MROW:MROW + 2].bitcast(F32), 1.0).then_inc(consts, 1)
            pool.wait_ge(consts, 8 + 9)
            x_work(1, 3)
            pool.wait_ge(tr_done, 8)
            nc.gpsimd.memset(V2[:, :, :, :, D2:V2W], 1.0).then_inc(consts, 1)
            pool.wait_ge(q2_high, 16 + TB)
            pool.wait_ge(consts, 8 + 9 + 1)
            for b in range(B):
                nc.gpsimd.tensor_tensor(HT[:, KB * b:KB * b + KB, :], HT[:, KB * b:KB * b + KB, :],
                                        biasM[:, b, :].unsqueeze(1).broadcast_to([P, KB, C]), ALU.add).then_inc(ht_ready, 1)

            def stage_v(b, h, k):
                nc.gpsimd.tensor_copy(V2S[:, k % 3, :, :], V2[:, b, :, h, :]).then_inc(v2s_ready, 1)

            for u in range(3):
                stage_v(u % 2, u // 2, u)

            def body2(it, last):
                for j in range(6):
                    if not (last and j >= 3):
                        pool.wait_ge(pv_done, PV1 + KB * (6 * it + j + 1))
                        stage_v((j + 3) % 2, 3 * it + (j + 3) // 2, j)
            with pool.Fori(0, H // 3 - 1) as it:
                body2(it, False)
            body2(H // 3 - 1, True)
            pool.wait_ge(o2_copied, 2 * H + 1)
            for part in range(2):
                nc.gpsimd.memset(QK[64:MROW, (4 + part) * F:(5 + part) * F].bitcast(F32), 0.0).then_inc(consts, 1)
            pool.wait_ge(consts, 8 + 9 + 1 + 2)
            x_work(2, 4)
            pool.wait_ge(wfc2_loaded, 16)
            pool.wait_ge(wl_done, PAIRS + 2 + 2)
            for i in range(3):
                nc.gpsimd.tensor_scalar(WF2[:, i + 1], WF2[:, 0], gw[:, i:i + 1], None, ALU.mult).then_inc(pool_step, 1)
            pool.wait_ge(ht_ready, 3)
            nc.gpsimd.tensor_tensor(HT[:, :, :], HT[:, :, :], Y[:, :, :], ALU.add).then_inc(ht_ready, 1)
            finish(pool)

        @block.scalar
        def _(act):
            act.wait_ge(conv_loads, 16 * CONV_LOADS)
            for t in range(TB):
                act.wait_ge(conv_out, t // 2 * 2 + 2)
                nc.scalar.activation(HT[:, t, :], PS[:, t // 2, 256 * (t % 2):256 * (t % 2) + C], ACT.Identity,
                                     scale=maskc[:, t:t + 1]).then_inc(h0_ready, 1)
            nx = [0]

            def x_parts(stage, g):
                nx[0] += 1
                if nx[0] == 1:
                    act.wait_ge(loads, 16 * LOADS)
                act.wait_ge(tr_done, nx[0])
                if g >= 2:
                    act.wait_ge(xt_low, nx[0] - 2)
                cols = slice(HALF * g, HALF * g + HALF)
                for c, to, s_ in ((0, xs(stage, g, 0), xt_t), (0, XAh[:, cols], xt_high), (1, XC[:, cols], xt_high)):
                    if c == 1:
                        act.wait_ge(xt_t2, nx[0])
                    nc.scalar.activation(to, xbank(stage, g, c), ACT.Identity, scale=gcols[:, stage, g // 2, c, 0:1],
                                         bias=gcols[:, stage, g // 2, c, 1:2]).then_inc(s_, 1)

            def layer_norms(stage):
                def deviation(k):
                    j, g = ITEMS[stage][k]
                    act.wait_ge(var_ready, ITEM0[stage] + k + 1)
                    sd = SD[:, j, 4 * g:4 * g + 4]
                    nc.scalar.activation(sd, sd, ACT.Sqrt).then_inc(std_ready, 1)
                deviation(0)
                for k, (j, g) in enumerate(ITEMS[stage]):
                    if k + 1 < len(ITEMS[stage]):
                        deviation(k + 1)
                    act.wait_ge(rs_ready, ITEM0[stage] + k + 1)
                    src, dst, _ = LN[j]
                    for t in range(4 * g, 4 * g + (0 if j == 0 else 2)):
                        nc.scalar.activation(dst[:, t, 0:C], src[:, t, :], ACT.Identity, scale=RS[:, j, t:t + 1],
                                             bias=NB[:, j, t:t + 1]).then_inc(norm_act, 1)
                    for g_ in TAKE[stage].get(k, []):
                        x_parts(stage, g_)
                        if stage == 0 and g_ in (1, 2):
                            v_blocks(g_ - 1)

            def v_blocks(g):
                for t in range(4 * g, 4 * g + 4):
                    for half in range(2):
                        n = 2 * t + half
                        act.wait_ge(v_ready, n + 1)
                        if t >= 4 and half == 0:
                            act.wait_ge(v_stored[t % 4], 16 * (t // 4))
                        nc.scalar.activation(VS[t % 4][:, VC // 2 * half:VC // 2 * (half + 1)],
                                             PS[:, 4 + n % 3, 0:VC // 2], ACT.Copy).then_inc(v_copied, 1)
                    act.wait_ge(v_copied, 2 * t + 2)
                    act.dma_start(VD[:, t // KB, :, t % KB, :].rearrange("a p c -> p a c"),
                                  VS[t % 4].rearrange("p (a c) -> p a c", a=PAIRS)).then_inc(v_stored[t % 4], 16)
            layer_norms(0)

            act.sem_inc(o_copied, 1)

            def take(n):
                act.wait_ge(rot_ready, n + 1)

            def t_half(k, hh, hcol, n):
                take(n)
                nc.scalar.activation(TQ[:, HALF * hh:HALF * hh + HALF], rotT[k % NROT], ACT.Identity,
                                     scale=qks[:, 0:1], bias=qkbs[:, hcol:hcol + 1]).then_inc(rot_done, 1)

            def m_tile(k, dst, hh, n):
                take(n)
                nc.scalar.activation(dst[MROW:MROW + 2, HALF * hh:HALF * hh + HALF], rotT[k % NROT][MROW:MROW + 2, :],
                                     ACT.Copy).then_inc(rot_done, 1)

            for k in range(2):
                if k == 1:
                    act.wait_ge(ll_done, 1)
                for hh in range(2):
                    t_half(2 * k + hh, hh, k, 2 * k + hh)
            v_blocks(2)
            v_blocks(3)
            for hh in range(2):
                m_tile(4 + hh, q2_of(0), hh, 4 + hh)

            def body1(p, var):
                for j in range(4):
                    u = 4 * p + j
                    for tile in unit_tiles(j, var):
                        i, kind, x, owner = tile
                        k = tile_no[var][key_of(tile)]
                        n = number(var, p, key_of(tile))
                        if kind == "C":
                            take(n)
                            if x == 0:
                                act.wait_ge(pv_done, KB * u + i + 1)
                                act.wait_ge(psum_step, 7 * u + i + 1 if i < 4 else 7 * u + max(i - 4, 1) + 4)
                            nc.scalar.activation(prob(i)[:, HALF * x:HALF * x + HALF], rotT[k % NROT], ACT.Exp)\
                                .then_inc(rot_done, 1)
                            if i == 0 and x == 1 and not (var == FIRST and j == 0):
                                copy_o(u - 1)
                        elif kind == "D":
                            take(n)
                            act.wait_ge(rec_done, 4 * (4 * p + owner) + 8)
                            nc.scalar.activation(DEN[:, :], rotT[k % NROT], ACT.Copy).then_inc(rot_done, 1)
                        elif kind == "A":
                            if x == 0:
                                act.wait_ge(ll_done, u + 2)
                            t_half(k, x, j % 2, n)
                        elif kind == "M":
                            m_tile(k, q2_of(j + 1), x, n)

            def copy_o(u):
                act.wait_ge(pv_done, NP + KB * (u + 1))
                act.wait_ge(ot_done, 2 * u + 2)
                nc.scalar.activation(ORAW[:, :], psO, ACT.Copy).then_inc(o_copied, 1)
            body1(0, FIRST)
            with act.Fori(1, PAIRS - 1) as p:
                body1(p, MID)
            body1(PAIRS - 1, LAST)
            copy_o(4 * PAIRS - 1)
            layer_norms(1)

            for n, (m, b) in enumerate(M2):
                for hh in range(2):
                    act.wait_ge(q2_ready, 2 * n + hh + 1)
                    if hh == 0 and n >= 4:
                        act.wait_ge(q2_stored[n % 4], 32)
                    nc.scalar.activation(HS[n % 4][0:MROW, HALF * hh:HALF * hh + HALF], PS[0:MROW, (2 * n + hh) % 4, :],
                                         ACT.Identity, scale=0.25 if m < 2 else 1.0).then_inc(q2_high, 1)
            for t in range(TB):
                act.wait_ge(q2_ready, 16 + t + 1)
                nc.scalar.activation(V2[:, t // KB, t % KB, :, 0:D2],
                                     PS[:, 4 + t % 4, 0:C].rearrange("p (h d) -> p h d", h=H), ACT.Copy)\
                    .then_inc(q2_high, 1)
            for i in range(4):
                act.wait_ge(q2_stored[i], 64)
            base = R1
            for hh in range(2):
                act.wait_ge(rot_ready, base + hh + 1)
                nc.scalar.activation(q3_of(0)[MROW:MROW + 2, HALF * hh:HALF * hh + HALF], rotT[hh][MROW:MROW + 2, :],
                                     ACT.Copy).then_inc(rot_done, 1)

            def body2(it, last):
                for j in range(6):
                    u = 6 * it + j
                    k = ROT2 * j + PRO2
                    for i in range(KB):
                        if i >= 6 and not (last and j == 5):
                            act.wait_ge(rot_ready, base + it * 6 * ROT2 + k + 1)
                            nc.scalar.activation(q3_of(j + 1)[MROW:MROW + 2, HALF * (i - 6):HALF * (i - 6) + HALF],
                                                 rotT[k % NROT][MROW:MROW + 2, :], ACT.Copy).then_inc(rot_done, 1)
                            k += 1
                        for hh in range(2):
                            act.wait_ge(rot_ready, base + it * 6 * ROT2 + k + 1)
                            if hh == 0:
                                act.wait_ge(pv_done, PV1 - NP + KB * u + i + 1)
                            nc.scalar.activation(prob(i)[:, HALF * hh:HALF * hh + HALF], rotT[k % NROT], ACT.Exp)\
                                .then_inc(rot_done, 1)
                            k += 1
            with act.Fori(0, H // 3 - 1) as it:
                body2(it, False)
            body2(H // 3 - 1, True)
            layer_norms(2)
            nh = 0
            for g in range(4):
                for e in range(1 if g < 2 else 3):
                    for m in range(FB):
                        act.wait_ge(fc1_ready, nh + 1)
                        if m == 0 and g > 0:
                            act.wait_ge(fc2_ready, 4 * g)
                        nc.scalar.activation(HB[:, e, m, :], PS[:, nh % 4, :], ACT.Gelu, bias=b1c[:, m:m + 1])\
                            .then_inc(fc1_used, 1)
                        nh += 1
            finish(act)

        @block.vector
        def _(dve):
            cnt = [0]

            def link(ins):
                cnt[0] += 1
                ins.then_inc(dve_step, 1)
                dve.wait_ge(dve_step, cnt[0])

            def note(ins):
                cnt[0] += 1
                ins.then_inc(dve_step, 1)

            nx = [0]

            def x_low(stage, g):
                nx[0] += 1
                n = nx[0]
                cols = slice(HALF * g, HALF * g + HALF)
                dve.wait_ge(tr_done, n)
                if g >= 2:
                    dve.wait_ge(xc_low, n - 2)
                nc.vector.tensor_scalar(xs(stage, g, 1), xbank(stage, g, 1), gcols[:, stage, g // 2, 1, 0:1],
                                        gcols[:, stage, g // 2, 1, 1:2], ALU.mult, ALU.add).then_inc(xt_t2, 1)
                dve.wait_ge(xt_high, 2 * n - 1)
                nc.vector.tensor_tensor(XAl[:, cols], xs(stage, g, 0), XAh[:, cols].bitcast(F32), ALU.subtract)\
                    .then_inc(xt_low, 1)

            def layer_norms(stage, before):
                def normalise(j, g):
                    src, dst, _ = LN[j]
                    if j == 0:
                        for step in range(2):
                            for t in range(4 * g, 4 * g + 4):
                                ins = nc.vector.scalar_tensor_tensor(
                                    out=HT[:, t, :], in0=HT[:, t, :], scalar=(MV[:, j, t, 0:1], RS[:, j, t:t + 1])[step],
                                    in1=rows[:, step, :], op0=(ALU.subtract, ALU.mult)[step], op1=(ALU.mult, ALU.add)[step])
                                if step == 0:
                                    note(ins)
                                else:
                                    ins.then_inc(norm_dve, 1)
                            dve.wait_ge(dve_step, cnt[0])
                    else:
                        for t in range(4 * g + 2, 4 * g + 4):
                            nc.vector.tensor_scalar(dst[:, t, 0:C], src[:, t, :], MV[:, j, t, 0:1], RS[:, j, t:t + 1],
                                                    ALU.subtract, ALU.mult).then_inc(norm_dve, 1)

                def stats(k):
                    j, g = ITEMS[stage][k]
                    before(j, g)
                    src, _, eps = LN[j]
                    blocks = range(4 * g, 4 * g + 4)
                    for t in blocks:
                        note(nc.vector.bn_stats(STAT[:, j, t, :], src[:, t, :]))
                    dve.wait_ge(dve_step, cnt[0])
                    for t in blocks:
                        note(nc.vector.bn_aggr(MV[:, j, t, :], STAT[:, j, t, :]))
                    dve.wait_ge(dve_step, cnt[0])
                    nc.vector.tensor_scalar(SD[:, j, 4 * g:4 * g + 4], MV[:, j, 4 * g:4 * g + 4, 1], eps, None, ALU.add)\
                        .then_inc(var_ready, 1)
                stats(0)
                for k, (j, g) in enumerate(ITEMS[stage]):
                    if k + 1 < len(ITEMS[stage]):
                        stats(k + 1)
                    cols = slice(4 * g, 4 * g + 4)
                    dve.wait_ge(std_ready, ITEM0[stage] + k + 1)
                    link(nc.vector.reciprocal(RS[:, j, cols], SD[:, j, cols]))
                    nc.vector.scalar_tensor_tensor(out=NB[:, j, cols], in0=MV[:, j, cols, 0], scalar=-1.0, in1=RS[:, j, cols],
                                                   op0=ALU.mult, op1=ALU.mult).then_inc(rs_ready, 1)
                    normalise(j, g)
                    for g_ in TAKE[stage].get(k, []):
                        x_low(stage, g_)

            dve.wait_ge(conv_loads, 16 * CONV_LOADS)
            E = QK[0:CONV_ROWS, 0:N]
            WS = HH[0:CONV_ROWS, 0:C]
            link(nc.vector.tensor_copy(WS, PA[0:CONV_ROWS, N:N + C]))
            link(nc.vector.tensor_tensor(WS[64:CONV_ROWS], PA[64:CONV_ROWS, N:N + C], WS[64:CONV_ROWS].bitcast(F32),
                                         ALU.subtract))
            nc.vector.tensor_scalar(E, PA[0:CONV_ROWS, 0:N].bitcast(I32), vocab[0:CONV_ROWS, 0:1], None, ALU.is_equal)\
                .then_inc(conv_in, 1)
            dve.wait_ge(loads, 16 * LOADS)
            link(nc.vector.tensor_copy(identB[:, :], identF[:, :]))
            dve.wait_ge(wv_in, 16)
            dve.wait_ge(conv_out, TB)
            for c in range(2):
                link(nc.vector.tensor_copy(WVH[c], WVR[:, VC * c:VC * c + VC]))
                nc.vector.tensor_tensor(WVL[c], WVR[:, VC * c:VC * c + VC], WVH[c].bitcast(F32), ALU.subtract)\
                    .then_inc(wv_ready, 1)

            def before0(j, g):
                if j == 0:
                    dve.wait_ge(h0_ready, 4 * g + 4)
                else:
                    wait_normed(dve, 0, 0, g)
            layer_norms(0, before0)
            dve.wait_ge(proj_ready, 1)
            nc.vector.tensor_tensor(bias1[:, :], PS[:, 7, 0:C], rows[:, 2, :], ALU.add).then_inc(bias_ready, 1)

            dve.wait_ge(pool_step, 5)
            for i, heads, ch in ((1, HKEEP[1] * D2, KEEP[1]), (2, HKEEP[2] * D2, KEEP[2])):
                w = WP2[0:heads, 1, 0, 0:ch]
                note(nc.vector.scalar_tensor_tensor(out=w, in0=WP2[0:heads, 0, 0, 0:ch], scalar=gw[0:heads, i:i + 1], in1=w,
                                                    op0=ALU.mult, op1=ALU.add))
                for bias, r in ((bias2, 3), (biasM, 4)):
                    note(nc.vector.scalar_tensor_tensor(out=bias[:, 1, 0:ch], in0=rows[:, r, 0:ch], scalar=gw[:, i:i + 1],
                                                        in1=bias[:, 1, 0:ch], op0=ALU.mult, op1=ALU.add))
                dve.wait_ge(dve_step, cnt[0])

            def split_w(p):
                dve.wait_ge(raw1, 32 * p + 32)
                nc.vector.tensor_scalar(qkbs[:, :], qkb[:, :], qks[:, 0:1], None, ALU.mult).then_inc(wh_done, 1)
                nc.vector.tensor_copy(WH[:, :, :, :], WRAW[:, :, :, :]).then_inc(wh_done, 1)
                dve.wait_ge(wh_done, 2 * p + 2)
                nc.vector.tensor_tensor(WL[:, :, :, :], WRAW[:, :, :, :], WH[:, :, :, :].bitcast(F32), ALU.subtract)\
                    .then_inc(wl_done, 1)

            def parts(u, n):
                dve.wait_ge(rot_done, n + 1)
                nc.vector.tensor_copy(HH[:, :], TQ[:, :]).then_inc(hh_done, 1)
                dve.wait_ge(hh_done, u + 1)
                nc.vector.tensor_tensor(LL[:, :], TQ[:, :], HH[:, :].bitcast(F32), ALU.subtract).then_inc(ll_done, 1)

            def placed(j, turn):
                dve.wait_ge(moved_b[j % 2], 64 * turn)
                dve.wait_ge(moved_c[j % 2], 32 * turn)

            def row_max(k, i, n, wait_mz=None):
                dve.wait_ge(b_ready, n + 1)
                if i == 0 and wait_mz is not None:
                    dve.wait_ge(mz_ready, wait_mz + 1)
                nc.vector.tensor_reduce(MC[:, k % 2, i:i + 1], scoreB[i % 2], AX.XY, ALU.max, negate=True)\
                    .then_inc(rowmax, 1)

            def split_max(k, u, n):
                dve.wait_ge(rowmax, n)
                nc.vector.tensor_copy(MZ[:, k % 2, :, MROW], MC[:, k % 2, :]).then_inc(mz_hi, 1)
                dve.wait_ge(mz_hi, u + 1)
                nc.vector.tensor_tensor(MZ[:, k % 2, :, MROW + 1], MC[:, k % 2, :], MZ[:, k % 2, :, MROW], ALU.subtract)\
                    .then_inc(mz_ready, 1)

            dve.sem_inc(rec_done, 8)
            dve.sem_inc(ot_done, 2)
            dve.sem_inc(mz_ready, 1)
            split_w(0)
            parts(0, 1)
            placed(0, 1)
            parts(1, 3)
            for i in range(KB):
                row_max(0, i, i)
            split_max(0, 0, KB)

            def recip(u, q, n):
                if q == 0:
                    dve.wait_ge(rot_done, n + 1)
                    dve.wait_ge(ot_done, 2 * u + 2)
                nc.vector.reciprocal(REC[:, P * q:P * q + P], DEN[:, P * q:P * q + P]).then_inc(rec_done, 1)

            def outputs(u, jj, pp):
                dve.wait_ge(o_copied, u + 2)
                dve.wait_ge(rec_done, 8 + 4 * (u + 1))
                for lo in range(2):
                    half = lo if jj % 2 == 0 else 1 - lo
                    s = slice(D1 * lo, D1 * lo + D1)
                    dst = OT[s, jj // 2, pp, half, :] if isinstance(pp, int) else \
                        OT[s, jj // 2, bass.ds(pp, 1), half, :].rearrange("p a n -> p (a n)")
                    nc.vector.tensor_tensor(dst, ORAW[s, :], REC[s, :], ALU.mult).then_inc(ot_done, 1)

            def body1(p, var):
                for j in range(4):
                    u = 4 * p + j
                    before = not (var == FIRST and j == 0)
                    d = number(var, p, (j - 1, "D", 0, 0)) if before else None

                    def mx(i):
                        if not (var == LAST and j == 3):
                            row_max(j + 1, i, KB * (u + 1) + i, u)
                    if before:
                        for q in range(2):
                            recip(u - 1, q, d)
                    mx(0)
                    if not (var == LAST and j >= 2):
                        placed(j + 1, 2 * p + (j + 1) // 2 + 1)
                        parts(u + 2, number(var, p, (j, "A", 1, 0)))
                    mx(1)
                    mx(2)
                    mx(3)
                    for i in range(4, KB):
                        mx(i)
                    if not (var == LAST and j == 3):
                        split_max(j + 1, u + 1, KB * (u + 2))
                    if j == 1 and var != LAST:
                        dve.wait_ge(rot_done, number(var, p, (1, "A", 1, 0)) + 1)
                        split_w(p + 1)
                    if before:
                        recip(u - 1, 2, d)
                        recip(u - 1, 3, d)
                        outputs(u - 1, (j - 1) % 4, p if j else p - 1)
            for i in range(4):
                dve.wait_ge(v_stored[i], 64)
            body1(0, FIRST)
            with dve.Fori(1, PAIRS - 1) as p:
                body1(p, MID)
            body1(PAIRS - 1, LAST)
            def before1(j, g):
                if (j, g) == (2, 1):
                    for q in range(4):
                        recip(4 * PAIRS - 1, q, number(LAST, PAIRS - 1, (3, "D", 0, 0)))
                    outputs(4 * PAIRS - 1, 3, PAIRS - 1)
                if j == 2:
                    for t in range(4 * g, 4 * g + 4):
                        dve.wait_ge(proj_ready, t + 2)
                        note_used(nc.vector.tensor_tensor(HT[:, t, :], PS[:, t % 4, 0:C], HT[:, t, :], ALU.add))
                    dve.wait_ge(proj_used, used[0])
                else:
                    wait_normed(dve, 1, 2, g)

            used = [0]

            def note_used(ins):
                used[0] += 1
                ins.then_inc(proj_used, 1)
            dve.wait_ge(ht_ready, 1)
            layer_norms(1, before1)
            dve.wait_ge(w_loaded, 16)
            link(nc.vector.tensor_copy(W2h, W2R))
            for i in range(2):
                s = slice(3 * C * i, 3 * C * i + 3 * C)
                nc.vector.tensor_tensor(W2l[i], W2R[:, s], W2h[:, s].bitcast(F32), ALU.subtract).then_inc(wl_done, 1)
            for n, (m, b) in enumerate(M2):
                for hh in range(2):
                    dve.wait_ge(q2_high, 2 * n + hh + 1)
                    if hh == 0 and n >= 4:
                        dve.wait_ge(q2_stored[n % 4], 32)
                    s = slice(HALF * hh, HALF * hh + HALF)
                    nc.vector.scalar_tensor_tensor(out=LS[n % 4][0:MROW, s], in0=PS[0:MROW, (2 * n + hh) % 4, :],
                                                   scalar=0.25 if m < 2 else 1.0, in1=HS[n % 4][0:MROW, s].bitcast(F32),
                                                   op0=ALU.mult, op1=ALU.subtract).then_inc(q2_low, 1)
            UB = 2 * H
            dve.sem_inc(o2_copied, 1)
            for i in range(2):
                dve.sem_inc(o2_stored[i], 64)
            for n in range(AHEAD):
                row_max(n // KB, n % KB, KB * UB + n, UB + n // KB - 1)
                if n == KB - 1:
                    split_max(0, UB, KB * (UB + 1))

            def body2(it, last):
                for j in range(6):
                    u = 6 * it + j
                    for i in range(KB):
                        w = KB * j + i + AHEAD
                        if not (last and w >= 6 * KB):
                            row_max(w // KB, w % KB, it * 6 * KB + KB * UB + w, 6 * it + UB + w // KB - 1)
                            if w % KB == KB - 1:
                                split_max(w // KB, 6 * it + UB + w // KB, it * 6 * KB + KB * UB + w + 1)
                        if i == 0 and j > 0:
                            copy_o2(6 * it, j - 1)
                    if last and j == 1:
                        sums_to_reciprocals(0)
                    if last and j in (2, 3):
                        b = j - 2
                        note(nc.vector.tensor_tensor(Y[:, KB * b:KB * b + KB, :], Y[:, KB * b:KB * b + KB, :],
                                                     bias2[:, b, :].unsqueeze(1).broadcast_to([P, KB, C]), ALU.add))
                    if last and j == 4:
                        scale_outputs(0)
                copy_o2(6 * it, 5)

            def sums_to_reciprocals(g):
                dve.wait_ge(sums_in, 64 * (g + 1))
                nc.vector.reciprocal(R2T[g], D2T[g]).then_inc(rec_done, 1)

            def scale_outputs(g):
                dve.wait_ge(o2_in, (64, 96)[g])
                if g == 0:
                    dve.wait_ge(r2_in, 32)
                for b in range(B):
                    r = R2[:, b, :].rearrange("p (x n) -> p x n", x=2)
                    if g == 1:
                        dve.wait_ge(r2_spread, b + 1)
                        r = PS[0:MROW, 4 + 2 * b:6 + 2 * b, :]
                    nc.vector.tensor_tensor(O2[:, g, b, :].rearrange("p (x n) -> p x n", x=2),
                                            O2U[b][:, g, :].rearrange("p (x n) -> p x n", x=2), r, ALU.mult)\
                        .then_inc(ot_done, 1)

            def copy_o2(u0, j):
                dve.wait_ge(pv_done, PV1 + KB * (u0 + j + 1))
                dve.wait_ge(o2_stored[j % 2], u0 * 32 + 64 * (j // 2) + 64)
                nc.vector.tensor_copy(O2S[j % 2], psO[:, 0:256]).then_inc(o2_copied, 1)
            with dve.Fori(0, H // 3 - 1) as it:
                body2(it, False)
            body2(H // 3 - 1, True)
            dve.wait_ge(w_loaded, 32)
            raw = WF1
            Mh, Ml = QK[:, 0:2 * F], QK[:, 2 * F:4 * F]
            Zh, Zl = QK[0:MROW, 4 * F:5 * F], QK[0:MROW, 5 * F:6 * F]
            link(nc.vector.tensor_copy(Mh, raw))
            link(nc.vector.tensor_tensor(Ml, raw, Mh.bitcast(F32), ALU.subtract))
            dve.sem_inc(wl_done, 2)
            note(nc.vector.tensor_copy(Zh[0:64], Mh[0:64, 0:F].bitcast(F32)))
            note(nc.vector.tensor_copy(Zl[0:64], Ml[0:64, 0:F].bitcast(F32)))

            sums_to_reciprocals(1)
            scale_outputs(1)
            dve.wait_ge(dve_step, cnt[0])
            def before2(j, g):
                for t in range(4 * g, 4 * g + 4):
                    dve.wait_ge(proj_ready, TB + 1 + t + 1)
                    note_used(nc.vector.tensor_tensor(Y[:, t, :], PS[:, t % 4, 0:C], Y[:, t, :], ALU.add))
                dve.wait_ge(proj_used, used[0])
            layer_norms(2, before2)
            dve.wait_ge(ht_ready, 4)
            for t in range(TB):
                dve.wait_ge(fc2_ready, t + 1)
                nc.vector.tensor_tensor(HT[:, t, :], PS[:, 4 + t % 4, 0:C], HT[:, t, :], ALU.add).then_inc(fc2_used, 1)
            finish(dve)

        @block.tensor
        def _(pe):
            pe.wait_ge(conv_in, 1)
            pe.wait_ge(dve_step, 2)
            WS = HH[0:CONV_ROWS, 0:C]
            for t in range(TB):
                pe.matmul(PS[:, t // 2, 256 * (t % 2):256 * (t % 2) + C], QK[0:CONV_ROWS, P * t:P * t + P], WS,
                          start=True, stop=True).then_inc(conv_out, 1)
            pe.wait_ge(h0_ready, TB)
            pe.wait_ge(loads, 16 * LOADS)
            for p in range(PAIRS):
                mm = pe.matmul(PS[:, 7, 0:C], bvc[:, p:p + 1].broadcast_to([P, P]), WP1[:, 0, p, :],
                               start=(p == 0), stop=(p == PAIRS - 1))
            mm.then_inc(proj_ready, 1)

            nx = [0]

            def transpose(stage, g):
                nx[0] += 1
                pe.wait_ge(twice_done, nx[0])
                if g >= 2:
                    pe.wait_ge(xt_high, 2 * (nx[0] - 2))
                for tb in range(4):
                    cols = slice(P * tb, P * tb + P)
                    pe.transpose(xbank(stage, g, 0)[:, cols], NT[stage][:, 4 * g + tb, 0:P], identF[:, :])
                    mm = pe.transpose(xbank(stage, g, 1)[:, cols], NT[stage][:, 4 * g + tb, P:2 * P], identF[:, :])
                mm.then_inc(tr_done, 1)
            WV = [(XAh, WVH[0]), (XAl, WVH[0]), (XAh, WVL[0]), (XC, WVH[1]), (XC, WVL[1])]

            def v_tile(n):
                t, half = n // 2, n % 2
                if t % 4 == 0 and half == 0:
                    pe.wait_ge(xt_low, t // 4 + 1)
                    pe.wait_ge(xc_low, t // 4 + 1)
                if n >= 3:
                    pe.wait_ge(v_copied, n - 2)
                for c, (x, w) in enumerate(WV):
                    mm = pe.matmul(PS[:, 4 + n % 3, 0:VC // 2], x[:, P * t:P * t + P],
                                   w[:, VC // 2 * half:VC // 2 * (half + 1)], start=(c == 0), stop=(c == len(WV) - 1))
                mm.then_inc(v_ready, 1)
            transpose(0, 0)
            pe.wait_ge(wv_ready, 2)
            for g in range(1, 3):
                transpose(0, g)
                for n in range(8 * g - 8, 8 * g):
                    v_tile(n)
            transpose(0, 3)
            pe.wait_ge(v_copied, 16)

            def free(n):
                pe.wait_ge(rot_done, n - NROT + 1)

            CHUNKS = [(XAh, WH, 0), (XAl, WH, 0), (XAh, WL, 0), (XC, WH, 1), (XC, WL, 1)]

            def a_tile(k, b, hd, hh):
                for c, (x, w, r) in enumerate(CHUNKS):
                    mm = pe.matmul(rotT[k % NROT], w[:, r, hd, :], x[:, S * b + HALF * hh:S * b + HALF * hh + HALF],
                                   start=(c == 0), stop=(c == len(CHUNKS) - 1))
                mm.then_inc(rot_ready, 1)

            def m_tile(k, j, hh):
                for i in range(4):
                    mm = pe.matmul(rotT[k % NROT][:, P * i:P * i + P], MZ[:, j % 2, 4 * hh + i, :], identB[:, :],
                                   start=True, stop=True)
                mm.then_inc(rot_ready, 1)

            def b_tile(q, k_, i, n):
                pe.wait_ge(rowmax, n - 1)
                for hh in range(2):
                    mm = pe.matmul(scoreB[i % 2][:, hh, :], q[:, P * i:P * i + P], k_[:, HALF * hh:HALF * hh + HALF],
                                   start=True, stop=True)
                mm.then_inc(b_ready, 1)

            pe.wait_ge(wl_done, 1)
            pe.wait_ge(bias_ready, 1)
            for n in range(4):
                if n == 3:
                    free(n)
                a_tile(n, 0, n // 2, n % 2)
            pe.wait_ge(rot_done, 4)
            for n in range(16, 24):
                v_tile(n)
            pe.wait_ge(xt_low, 4)
            pe.wait_ge(xc_low, 4)
            pe.wait_ge(moved_b[0], 64)
            for i in range(KB):
                v_tile(24 + i)
                if i < 2:
                    for hh in range(2):
                        mm = pe.matmul(scoreB[i % 2][:, hh, :], q_of(0)[:, P * i:P * i + P],
                                       k_of(0)[:, HALF * hh:HALF * hh + HALF], start=True, stop=True)
                    mm.then_inc(b_ready, 1)
                else:
                    b_tile(q_of(0), k_of(0), i, i)
            pe.wait_ge(mz_ready, 2)
            pe.wait_ge(v_copied, 2 * TB)
            for hh in range(2):
                free(4 + hh)
                m_tile(4 + hh, 0, hh)
            pe.wait_ge(consts, 8)
            pe.wait_ge(rot_done, PRO)
            pe.sem_inc(pv_done, NP)

            def pv(j, i, u):
                b, odd = j // 2, j % 2
                if i == 0:
                    pe.wait_ge(o_copied, u + 1)
                for lo in range(2):
                    half = lo if odd == 0 else 1 - lo
                    mm = pe.matmul(psO[D1 * lo:D1 * lo + D1, :], V1[:, b, i, D1 * odd:D1 * odd + D1],
                                   prob(i)[:, HALF * half:HALF * half + HALF], start=(i == 0), stop=(i == KB - 1))
                mm.then_inc(pv_done, 1)

            def den(k, j, u):
                pe.wait_ge(psum_step, NP + 7 * (u + 1))
                for lo in range(2):
                    half = lo if j % 2 == 0 else 1 - lo
                    mm = pe.matmul(rotT[k % NROT][D1 * lo:D1 * lo + D1, :], ones[:, :],
                                   psum_of(j)[:, HALF * half:HALF * half + HALF], start=True, stop=True)
                mm.then_inc(rot_ready, 1)

            def body1(p, var):
                for j in range(4):
                    u = 4 * p + j
                    q, k_, q2, k2 = q_of(j), k_of(j), q2_of(j), k2_of(j)
                    nb = 0
                    for i in range(KB):
                        if not (var == LAST and j == 3):
                            for _x in range(BSLOT[i]):
                                if nb == 0:
                                    pe.wait_ge(moved_b[(j + 1) % 2], 64 * (2 * p + (j + 1) // 2 + 1))
                                b_tile(q_of(j + 1), k_of(j + 1), nb, KB * (u + 1) + nb)
                                nb += 1
                        for tile in (t for t in unit_tiles(j, var) if t[0] == i):
                            _, kind, x, owner = tile
                            k = tile_no[var][key_of(tile)]
                            if kind == "M" and x == 0:
                                pv_wait(j, i - 1, p, var)
                                pv(j, i - 1, u)
                                pe.wait_ge(mz_ready, u + 3)
                            free(number(var, p, key_of(tile)))
                            if kind == "C":
                                if i == 0 and x == 0:
                                    pe.wait_ge(moved_c[j % 2], 32 * (2 * p + j // 2 + 1))
                                    pe.wait_ge(rot_done, number(var, p, (0, "A", 0, 0)) if j == 0 else
                                               number(var, p, (j - 1, "M", 1, 0)) + 1)
                                cols = slice(HALF * x, HALF * x + HALF)
                                pe.matmul(rotT[k % NROT], k_[:, P * i:P * i + P], q[:, cols], start=True, stop=False)
                                pe.matmul(rotT[k % NROT], k2[0:KC, P * i:P * i + P], q2[0:KC, cols], start=False, stop=True)\
                                    .then_inc(rot_ready, 1)
                            elif kind == "M":
                                m_tile(k, j + 1, x)
                            elif kind == "D":
                                den(k, owner % 4, 4 * p + owner)
                            elif kind == "A":
                                if x == 0 and j == 2:
                                    pe.wait_ge(wl_done, p + 2)
                                a_tile(k, 1 if j < 2 else 0, j % 2, x)
                        if i == 1 and j % 2 == 0:
                            pe.wait_ge(v1_in[j // 2], 16 * (p + 1))
                        if 0 < i < KB - 1 or i == KB - 1 and var == LAST and j == 3:
                            pv_wait(j, i - 1, p, var)
                            pv(j, i - 1, u)
                        elif i == 0 and not (var == FIRST and j == 0):
                            pv_wait(j - 1, KB - 1, p, var)
                            pv((j - 1) % 4, KB - 1, u - 1)

            def pv_wait(j, i, p, var):
                pe.wait_ge(rot_done, number(var, p, (j, "C", 1, i)) + 1)
            body1(0, FIRST)
            with pe.Fori(1, PAIRS - 1) as p:
                body1(p, MID)
            body1(PAIRS - 1, LAST)
            pv_wait(3, KB - 1, PAIRS - 1, LAST)
            pv(3, KB - 1, 4 * PAIRS - 1)
            pe.wait_ge(rowmax, KB * 2 * H)
            for t in range(TB):
                b, half, blk = t // KB, t % KB // 4, t % 4
                if t % KB == 0:
                    pe.wait_ge(ot_done, 2 + 2 * (2 * H - 2 + 2 * b))
                if t == 4:
                    k = tile_no[LAST][(3, "D", 0, 0)]
                    free(k)
                    den(k, 3, 4 * PAIRS - 1)
                if t >= 4:
                    pe.wait_ge(proj_used, t - 3)
                for p in range(PAIRS):
                    mm = pe.matmul(PS[:, t % 4, 0:C], OT[:, b, p, half, P * blk:P * blk + P], WP1[:, half, p, :],
                                   start=(p == 0), stop=(p == PAIRS - 1))
                mm.then_inc(proj_ready, 1)
            pe.wait_ge(rot_done, R1)
            pe.wait_ge(o_copied, 1 + 2 * H)
            for g in range(4):
                transpose(1, g)
            pe.wait_ge(xt_low, 8)
            pe.wait_ge(xc_low, 8)
            CH2 = [(XAh, W2h, 0), (XAl, W2h, 0), (XAh, W2l[0], 0), (XC, W2h, 3 * C), (XC, W2l[1], 0)]
            pe.wait_ge(wl_done, PAIRS + 2)
            for n in range(16):
                m, b = M2[n // 2]
                if n >= 4:
                    pe.wait_ge(q2_low, n - 3)
                for c, (x, w, o) in enumerate(CH2):
                    mm = pe.matmul(PS[0:MROW, n % 4, :], w[:, o + MROW * m:o + MROW * m + MROW],
                                   x[:, S * b + HALF * (n % 2):S * b + HALF * (n % 2) + HALF], start=(c == 0), stop=(c == 4))
                mm.then_inc(q2_ready, 1)

            def v2_tile(t):
                if t >= 4:
                    pe.wait_ge(q2_high, 16 + t - 3)
                for c, (x, w, o) in enumerate(CH2):
                    mm = pe.matmul(PS[:, 4 + t % 4, 0:C], x[:, P * t:P * t + P], w[:, o + 2 * C:o + 3 * C],
                                   start=(c == 0), stop=(c == 4))
                mm.then_inc(q2_ready, 1)
            UB = 2 * H
            pe.wait_ge(consts, 8 + 9 + 1)
            pe.wait_ge(q2_low, 16)
            for n in range(AHEAD):
                if n % KB == 0:
                    pe.wait_ge(loaded3[n // KB], LOADS3)
                b_tile(q3_of(n // KB), k3_of(n // KB), n % KB, KB * UB + n)
                for t in range(2 * n, min(2 * n + 2, TB)):
                    v2_tile(t)
            pe.wait_ge(mz_ready, UB + 2)
            pe.wait_ge(q2_high, 16 + TB)
            for hh in range(2):
                m_tile(hh, 0, hh)
            pe.wait_ge(rot_done, R1 + PRO2)

            def pv2(j, i, u):
                if i == 0:
                    pe.wait_ge(o2_copied, u + 1)
                    pe.wait_ge(v2s_ready, u + 1)
                for g in range(4):
                    mm = pe.matmul(psO[32 * g:32 * g + V2W, 0:256], V2S[:, j % 3, i, :], prob(i)[:, 256 * g:256 * g + 256],
                                   start=(i == 0), stop=(i == KB - 1))
                mm.then_inc(pv_done, 1)

            def body2(it, last):
                base = R1 + it * 6 * ROT2
                for j in range(6):
                    u = 6 * it + j
                    k = ROT2 * j + PRO2
                    for i in range(KB):
                        w = KB * j + i + AHEAD
                        if not (last and w >= 6 * KB):
                            un = w // KB
                            if w % KB == 0:
                                pe.wait_ge(loaded3[un % 3], it * 2 * LOADS3 + LOADS3 * (un // 3 + 1))
                            b_tile(q3_of(un), k3_of(un), w % KB, it * 6 * KB + KB * UB + w)
                        if i >= 6 and not (last and j == 5):
                            if i == 6:
                                pe.wait_ge(mz_ready, UB + u + 3)
                            pe.wait_ge(rot_done, base + k - NROT + 1)
                            m_tile(k, j + 1, i - 6)
                            k += 1
                        for hh in range(2):
                            pe.wait_ge(rot_done, base + k - NROT + 1)
                            mm = pe.matmul(rotT[k % NROT], k3_of(j)[0:KC, P * i:P * i + P],
                                           q3_of(j)[0:KC, HALF * hh:HALF * hh + HALF], start=True, stop=True)
                            mm.then_inc(rot_ready, 1)
                            if hh == 1:
                                kk[i % 2] = k
                            k += 1
                        if i > 0:
                            pe.wait_ge(rot_done, base + kk[(i - 1) % 2] + 1)
                            pv2(j, i - 1, u)
                        elif j > 0:
                            pe.wait_ge(rot_done, base + kk[1] + 1)
                            pv2(j - 1, KB - 1, u - 1)
                pe.wait_ge(rot_done, base + kk[1] + 1)
                pv2(5, KB - 1, 6 * it + 5)
            kk = [0, 0]
            with pe.Fori(0, H // 3 - 1) as it:
                body2(it, False)
            body2(H // 3 - 1, True)
            pe.wait_ge(rowmax, KB * 2 * UB)
            pe.wait_ge(o2_copied, 2 * H + 1)
            pe.wait_ge(ot_done, 2 + 2 * UB + 2)

            def proj2(t, g):
                b, blk = t // KB, t % KB
                return pe.matmul(PS[:, t % 4, 0:C], O2[:, g, b, P * blk:P * blk + P], WP2[:, b, g, :],
                                 start=(g == 0), stop=(g == 1))
            for t in range(4):
                proj2(t, 0)
            pe.wait_ge(rec_done, 8 + 4 * UB + 2)
            for b in range(B):
                for q in range(4):
                    mm = pe.matmul(PS[0:MROW, 4 + 2 * b + q // 2, 256 * (q % 2):256 * (q % 2) + 256],
                                   spread[:, 4 * b + q, :], R2T[1], start=True, stop=True)
                mm.then_inc(r2_spread, 1)
            for t in range(TB):
                if t % KB == 0:
                    pe.wait_ge(ot_done, 2 + 2 * UB + 3 + t // KB)
                if t >= 4:
                    pe.wait_ge(proj_used, TB + t - 3)
                    proj2(t, 0)
                proj2(t, 1).then_inc(proj_ready, 1)
            Mh, Ml = QK[:, 0:2 * F], QK[:, 2 * F:4 * F]
            Zh, Zl = QK[0:MROW, 4 * F:5 * F], QK[0:MROW, 5 * F:6 * F]
            FULL = [(XAh, Mh, 0), (XAl, Mh, 0), (XAh, Ml, 0), (XC, Mh, F), (XC, Ml, F)]
            HALFW = [(XAh[0:MROW], Mh[0:MROW], 0), (XAl[0:MROW], Mh[0:MROW], 0), (XAh[0:MROW], Ml[0:MROW], 0)]
            THIRD = [(XAh[0:MROW], Zh, 0), (XAl[0:MROW], Zh, 0), (XAh[0:MROW], Zl, 0)]
            EARLY = 4

            def fc1_tile(g, e, m, nh):
                chunks = (FULL, HALFW, THIRD)[e]
                for c, (x, w, o) in enumerate(chunks):
                    mm = pe.matmul(PS[:, nh % 4, :], w[:, o + P * m:o + P * m + P], x[:, HALF * g:HALF * g + HALF],
                                   start=(c == 0), stop=(c == len(chunks) - 1))
                mm.then_inc(fc1_ready, 1)
            transpose(2, 0)
            transpose(2, 1)
            pe.wait_ge(proj_used, 2 * TB)
            pe.wait_ge(xt_low, 9)
            pe.wait_ge(xc_low, 9)
            for m in range(EARLY):
                fc1_tile(0, 0, m, m)
            transpose(2, 2)
            transpose(2, 3)
            pe.wait_ge(xt_low, 12)
            pe.wait_ge(xc_low, 12)
            pe.wait_ge(wfc2_loaded, 16)
            pe.wait_ge(consts, 8 + 9 + 1 + 2)
            nh = 0
            for g in range(4):
                evals = [0] if g < 2 else [0, 1, 2]
                for e in evals:
                    for m in range(FB):
                        if nh >= EARLY:
                            pe.wait_ge(fc1_used, nh - 3)
                            fc1_tile(g, e, m, nh)
                        nh += 1
                pe.wait_ge(fc1_used, nh)
                if g == 2:
                    pe.wait_ge(pool_step, 5 + 3)
                for tb in range(4):
                    t = 4 * g + tb
                    if t >= 4:
                        pe.wait_ge(fc2_used, t - 3)
                    for e in evals:
                        w = WF2[:, 0 if g < 2 else e + 1]
                        for m in range(FB):
                            mm = pe.matmul(PS[:, 4 + tb, 0:KEEP[e]], HB[:, e, m, P * tb:P * tb + P],
                                           w[:, C * m:C * m + KEEP[e]], start=(e == 0 and m == 0),
                                           stop=(e == evals[-1] and m == FB - 1), skip_group_check=True)
                    mm.then_inc(fc2_ready, 1)
            finish(pe)




def kernel(**inputs):
    import numpy as np
    import concourse.bacc as bacc
    from concourse.bass_utils import run_bass_kernel_spmd

    x = {k: np.ascontiguousarray(v) for k, v in inputs.items()}
    f32 = np.float32
    arrays = {}
    ids = np.full((B, S + 6), -1, np.int32)
    ids[:, 3:3 + S] = x["x"]
    win = np.full((CONV_ROWS, B, S), -1, np.int32)
    convw = np.zeros((CONV_ROWS, C), f32)
    vocab = np.full((P, 1), -2, f32)
    for at in (0, 64):
        for tap in range(7):
            for v in range(5):
                r = at + 5 * tap + v
                win[r] = ids[:, tap:tap + S]
                vocab[r] = v
                for c, (name, k) in enumerate((("L0_tok_W3", 3), ("L0_tok_W5", 5), ("L0_tok_W7", 7))):
                    t = tap - 3 + k // 2
                    if 0 <= t < k:
                        convw[r, 64 * c:64 * c + 64] = x[name][:, v, t]
    arrays["windows"] = win.reshape(CONV_ROWS, N)
    arrays["convw"] = convw
    arrays["vocab"] = vocab
    arrays["mask"] = x["mask_BS_f1_0"].reshape(TB, P).T
    arrays["ident"] = np.eye(P, dtype=f32)
    spread = np.zeros((4, B, H // 2, B, 4, MROW), f32)
    for q in range(4):
        for b in range(B):
            for h in range(H // 2):
                spread[q, b, h, b, q, D2 * h:D2 * h + D2] = 1.0
    arrays["spread"] = spread.reshape(4 * H, -1)

    def by_chunk(v):
        return np.stack([v[0:P], np.concatenate([v[P:C], v[P:C]])], 1)

    g = np.zeros((P, 3, B, 2, 2), f32)
    g[:, 0, :, :, 0] = 1.0
    for s_, n_ in ((1, "n1"), (2, "n2")):
        for b, z in enumerate("ls"):
            for k, gb in enumerate("gb"):
                g[:, s_, b, :, k] = by_chunk(x[f"L0_ffn_{n_}{z}_{gb}"])
    arrays["gcols"] = g.reshape(P, -1)
    w, wb = x["L0_attn_qkv_w"], x["L0_attn_qkv_b"]
    HD = H * D1
    w1 = np.zeros((PAIRS, P, 2, 2, P), f32)
    qkb = np.zeros((PAIRS, P, 2), f32)
    for h in range(H):
        r = slice(D1 * h, D1 * h + D1)
        both = np.concatenate([w[0:HD][r], w[HD:2 * HD][r]]).T
        w1[h // 2, :, :, h % 2, :] = np.stack([both[0:P], np.concatenate([both[P:C], both[P:C]])], 1)
        qkb[h // 2, :, h % 2] = np.concatenate([wb[0:HD][r], wb[HD:2 * HD][r]])
    arrays["w1"] = w1.reshape(PAIRS, P, -1)
    arrays["qkb"] = qkb
    arrays["wv"] = by_chunk(w[2 * HD:].T).reshape(P, -1)
    arrays["qks"] = np.repeat(np.array([D1 ** -0.5, 1.0], f32), D1).reshape(P, 1)
    arrays["bvc"] = wb[2 * HD:].reshape(PAIRS, P).T
    wp = x["L0_attn_proj_w"].T.reshape(PAIRS, 2, D1, C)
    arrays["wp1"] = np.stack([wp.reshape(PAIRS, P, C), wp[:, ::-1].reshape(PAIRS, P, C)]).transpose(2, 0, 1, 3).reshape(P, -1)
    arrays["wp2"] = x["L0_ffn_w_proj"].reshape(2, MROW, C).transpose(1, 0, 2).reshape(MROW, -1)
    arrays["gw"] = x["L0_ffn_gumbel_weights"]
    arrays["rows"] = np.stack([x[n] for n in ("L0_tok_ln_gamma", "L0_tok_ln_beta", "L0_attn_proj_b", "L0_ffn_b_proj", "L0_ffn_b_fc2")])
    arrays["w2qkv"] = by_chunk(x["L0_ffn_w_qkv"]).reshape(P, -1)
    arrays["wfc1"] = by_chunk(x["L0_ffn_w_fc1"]).reshape(P, -1)
    arrays["b1c"] = x["L0_ffn_b_fc1"].reshape(FB, P).T
    arrays["wfc2"] = x["L0_ffn_w_fc2"].reshape(FB, P, C).transpose(1, 0, 2).reshape(P, -1)

    nc = bacc.Bacc("TRN2", target_bir_lowering=False, num_devices=1)
    arrays = {f"in_{k}": np.ascontiguousarray(v) for k, v in arrays.items()}
    aps = {k[3:]: nc.dram_tensor(k, v.shape, mybir.dt.from_np(v.dtype), kind="ExternalInput").ap() for k, v in arrays.items()}
    out = nc.dram_tensor("out", (N, C), F32, kind="ExternalOutput").ap()
    tower(nc, aps, out)
    r = run_bass_kernel_spmd(nc, [arrays], core_ids=[0])
    return r.results[0]["out"].reshape(B, S, C)
```
